# Optimizing a Trainium2 kernel written in Bass

```python
import numpy as np
import jax
import jax.numpy as jnp

def _softmax(x, axis=-1):
    return jax.nn.softmax(x, axis=axis)

def _gelu(x):
    return jax.nn.gelu(x, approximate=True)

def _silu(x):
    return jax.nn.silu(x)

def _sigmoid(x):
    return jax.nn.sigmoid(x)

def _layernorm(x, axis=-1, eps=1e-05):
    m = jnp.mean(x, axis=axis, keepdims=True)
    v = jnp.var(x, axis=axis, keepdims=True)
    return (x - m) / jnp.sqrt(v + eps)

def _scatter_add(tgt, idx, src, axis=0):
    return tgt.at[idx].add(src)

def _segment_sum(src, seg, n):
    return jax.ops.segment_sum(src, seg, n)
kernel_name = 'mk_xattn_ffn_d4_seqx_r4_eddbfb'

def setup_inputs(seed: int=0):
    np.random.seed(seed)
    _w = jnp.asarray

    def _rec_inputs():
        import jax
        import jax.numpy as jnp
        _rk = jax.random.key(seed)
        x = -0.0003929 + 0.9999 * jax.random.normal(jax.random.fold_in(_rk, 1), (8, 100, 512), jnp.float32)
        _lenS = 100 - jax.random.randint(jax.random.fold_in(_rk, 7), (8,), 0, max(1, 100 // 4) + 1, jnp.int32)
        _lenS2 = 361 - jax.random.randint(jax.random.fold_in(_rk, 8), (8,), 0, max(1, 361 // 4) + 1, jnp.int32)
        _ctx_2048P = jax.random.normal(jax.random.fold_in(_rk, 11), (8, 16, 512), jnp.float32)
        _ctx_2048c = jax.random.dirichlet(jax.random.fold_in(_rk, 511), 0.3 * jnp.ones((16,), jnp.float32), (8, 361))
        _ctx_2048t = jnp.einsum('bsk,bkd->bsd', _ctx_2048c, _ctx_2048P)
        _ctx_2048t = _ctx_2048t * jax.lax.rsqrt(jnp.mean(jnp.square(_ctx_2048t)) + 1e-12) * 0.953939
        ctx_2048 = -1.39393e-06 + 0.999914 * (_ctx_2048t + 0.3 * jax.random.normal(jax.random.fold_in(_rk, 611), (8, 361, 512), jnp.float32))
        itok_BxS_0_1023 = jax.random.randint(jax.random.fold_in(_rk, 12), (8, 100), 0, 256, jnp.int32)
        _validS = jnp.arange(100)[None, :] < _lenS[:, None]
        _validS2 = jnp.arange(361)[None, :] < _lenS2[:, None]
        _causal = jnp.tril(jnp.ones((100, 100), dtype=bool))
        mask_BxS2_ik0 = jnp.where(jnp.broadcast_to(_validS2[:, :], (8, 361)), 0, 1).astype(jnp.int32)
        mask_BxS2_ff1 = jnp.where(jnp.ones((8, 361), dtype=bool), 1.0, 0.0).astype(jnp.float32)
        return (x, ctx_2048, itok_BxS_0_1023, mask_BxS2_ik0, mask_BxS2_ff1)
    x, ctx_2048, itok_BxS_0_1023, mask_BxS2_ik0, mask_BxS2_ff1 = _rec_inputs()

    def _L0_xattn_setup():
        import jax, jax.numpy as jnp
        import numpy as np
        B, Lq, Lk = (2, 1024, 256)
        Q_DIM, KV_DIM = (512, 512)
        H, HD = (16, 128)
        KVC, QC, R = (128, 192, 64)
        LOOKBACK = 8
        NEG = -1e+30

        def _rope(x, L):
            half = x.shape[-1] // 2
            inv_freq = 1.0 / 10000.0 ** (jnp.arange(half, dtype=jnp.float32) / half)
            ang = jnp.arange(L, dtype=jnp.float32)[:, None] * inv_freq
            cos, sin = (jnp.cos(ang), jnp.sin(ang))
            x1, x2 = (x[..., :half], x[..., half:])
            return jnp.concatenate([x1 * cos - x2 * sin, x1 * sin + x2 * cos], axis=-1)
        key = jax.random.key(seed)
        ks = jax.random.split(key, 11)

        def w(k, shape, fan_in):
            return jax.random.normal(k, shape, jnp.float32) / np.sqrt(fan_in).astype(np.float32)
        return {'q': jax.random.normal(ks[0], (B, Lq, Q_DIM), jnp.float32), 'kv': jax.random.normal(ks[1], (B, Lk, KV_DIM), jnp.float32), 'seg_id': jnp.sort(jax.random.randint(ks[2], (B, Lq), 0, Lk), axis=-1), 'W_kvc': w(ks[3], (KV_DIM, KVC), KV_DIM), 'W_dq': w(ks[4], (Q_DIM, QC), Q_DIM), 'W_uq': w(ks[5], (QC, H * HD), QC), 'W_qr': w(ks[6], (QC, H * R), QC), 'W_uk': w(ks[7], (KVC, H * HD), KVC), 'W_kr': w(ks[8], (KVC, R), KVC), 'W_uv': w(ks[9], (KVC, H * HD), KVC), 'W_o': w(ks[10], (H * HD, Q_DIM), H * HD)}
    _L0_xattn_all = _L0_xattn_setup()
    _L0_xattn_in = {k: v for k, v in _L0_xattn_all.items() if k in ('W_kvc', 'W_dq', 'W_uq', 'W_qr', 'W_uk', 'W_kr', 'W_uv', 'W_o')}
    del _L0_xattn_all

    def _L0_ffn_setup():
        import jax, jax.numpy as jnp
        import numpy as np
        B, S, D, I, E, K = (4, 256, 512, 256, 8, 2)
        key = jax.random.key(seed)
        ks = jax.random.split(key, 7)

        def w(k, shape, fan_in):
            return jax.random.normal(k, shape, dtype=jnp.float32) * fan_in ** (-0.5)
        return {'hidden_states': jax.random.normal(ks[0], (B, S, D), dtype=jnp.float32), 'router_w': w(ks[1], (D, E), D), 'gate_up_w': w(ks[2], (E, D, 2 * I), D), 'down_w': w(ks[3], (E, I, D), I), 'shared_gate_w': w(ks[4], (D, I), D), 'shared_up_w': w(ks[5], (D, I), D), 'shared_down_w': w(ks[6], (I, D), I)}
    _L0_ffn_all = _L0_ffn_setup()
    _L0_ffn_in = {k: v for k, v in _L0_ffn_all.items() if k in ('router_w', 'gate_up_w', 'down_w', 'shared_gate_w', 'shared_up_w', 'shared_down_w')}
    del _L0_ffn_all

    def _L1_xattn_setup():
        import jax, jax.numpy as jnp
        import numpy as np
        import math
        H = 512
        NH = 16
        HD = H // NH
        EPS_LN = 1e-05
        RES_SCALE_MAX = 0.3

        def _nan_clean(x, lim=10000.0):
            return jnp.nan_to_num(x, nan=0.0, posinf=lim, neginf=-lim)
        key = jax.random.key(seed)
        ks = jax.random.split(key, 12)
        B, S, T = (4, 512, 64)
        std = 1.0 / math.sqrt(H)
        return {'hidden_states': jax.random.normal(ks[0], (B, S, H), jnp.float32), 'audio_tokens': jax.random.normal(ks[1], (B, T, H), jnp.float32), 'attention_mask': jax.random.randint(ks[2], (B, T), 0, 2, jnp.int32), 'Wq': jax.random.normal(ks[3], (H, H), jnp.float32) * std, 'bq': jnp.zeros((H,), jnp.float32), 'Wk': jax.random.normal(ks[4], (H, H), jnp.float32) * std, 'bk': jnp.zeros((H,), jnp.float32), 'Wv': jax.random.normal(ks[5], (H, H), jnp.float32) * std, 'bv': jnp.zeros((H,), jnp.float32), 'Wo': jax.random.normal(ks[6], (H, H), jnp.float32) * std, 'bo': jnp.zeros((H,), jnp.float32), 'ln_gamma': jnp.ones((H,), jnp.float32), 'ln_beta': jnp.zeros((H,), jnp.float32), 'residual_scale': jnp.float32(0.05)}
    _L1_xattn_all = _L1_xattn_setup()
    _L1_xattn_in = {k: v for k, v in _L1_xattn_all.items() if k in ('Wq', 'bq', 'Wk', 'bk', 'Wv', 'bv', 'Wo', 'bo', 'ln_gamma', 'ln_beta', 'residual_scale')}
    del _L1_xattn_all

    def _L1_ffn_setup():
        import jax, jax.numpy as jnp
        import numpy as np
        EPS = 1e-05

        def activation_quant(x):
            scale = 127.0 / jnp.clip(jnp.max(jnp.abs(x), axis=-1, keepdims=True), EPS, None)
            xq = jnp.clip(jnp.round(x * scale), -128.0, 127.0) / scale
            return x + jax.lax.stop_gradient(xq - x)

        def weight_quant(w):
            scale = 1.0 / jnp.clip(jnp.mean(jnp.abs(w)), EPS, None)
            wq = jnp.clip(jnp.round(w * scale), -1.0, 1.0) / scale
            return w + jax.lax.stop_gradient(wq - w)

        def bitlinear(x, w):
            return jnp.einsum('bsd,od->bso', activation_quant(x), weight_quant(w))
        key = jax.random.key(seed)
        k1, k2, k3 = jax.random.split(key, 3)
        dim, inner = (512, 2048)
        x = jax.random.normal(k1, (4, 512, dim), dtype=jnp.float32)
        w1 = jax.random.normal(k2, (inner, dim), dtype=jnp.float32) * dim ** (-0.5)
        w2 = jax.random.normal(k3, (dim, inner), dtype=jnp.float32) * inner ** (-0.5)
        return {'x': x, 'w1': w1, 'w2': w2}
    _L1_ffn_all = _L1_ffn_setup()
    _L1_ffn_in = {k: v for k, v in _L1_ffn_all.items() if k in ('w1', 'w2')}
    del _L1_ffn_all

    def _L2_xattn_setup():
        import jax, jax.numpy as jnp
        import numpy as np
        D_MODEL = 512
        NUM_HEADS = 16
        HEAD_DIM = D_MODEL // NUM_HEADS
        key = jax.random.key(seed)
        ks = jax.random.split(key, 10)
        B, S, T = (4, 1024, 256)
        s = 1.0 / np.sqrt(D_MODEL)
        inp = {'query': jax.random.normal(ks[0], (B, S, D_MODEL), jnp.float32), 'key_value': jax.random.normal(ks[1], (B, T, D_MODEL), jnp.float32), 'Wq': jax.random.normal(ks[2], (D_MODEL, D_MODEL), jnp.float32) * s, 'bq': jnp.zeros((D_MODEL,), jnp.float32), 'Wk': jax.random.normal(ks[3], (D_MODEL, D_MODEL), jnp.float32) * s, 'bk': jnp.zeros((D_MODEL,), jnp.float32), 'Wv': jax.random.normal(ks[4], (D_MODEL, D_MODEL), jnp.float32) * s, 'bv': jnp.zeros((D_MODEL,), jnp.float32), 'Wo': jax.random.normal(ks[5], (D_MODEL, D_MODEL), jnp.float32) * s, 'bo': jnp.zeros((D_MODEL,), jnp.float32)}
        return inp
    _L2_xattn_all = _L2_xattn_setup()
    _L2_xattn_in = {k: v for k, v in _L2_xattn_all.items() if k in ('Wq', 'bq', 'Wk', 'bk', 'Wv', 'bv', 'Wo', 'bo')}
    del _L2_xattn_all

    def _L2_ffn_setup():
        import jax, jax.numpy as jnp
        import numpy as np
        HIDDEN = 512
        INTER = 2048
        BATCH, LOCAL_SEQ = (2, 1024)
        key = jax.random.key(seed)
        k1, k2, k3 = jax.random.split(key, 3)
        h_shard = jax.random.normal(k1, (BATCH, LOCAL_SEQ, HIDDEN), dtype=jnp.float32)
        w_gate_up = jax.random.normal(k2, (2 * INTER, HIDDEN), dtype=jnp.float32) * 0.02
        w_down = jax.random.normal(k3, (HIDDEN, INTER), dtype=jnp.float32) * 0.02
        return {'h_shard': h_shard, 'w_gate_up': w_gate_up, 'w_down': w_down}
    _L2_ffn_all = _L2_ffn_setup()
    _L2_ffn_in = {k: v for k, v in _L2_ffn_all.items() if k in ('w_gate_up', 'w_down')}
    del _L2_ffn_all

    def _L3_xattn_setup():
        import jax, jax.numpy as jnp
        import numpy as np
        H = 512
        NH = 16
        HD = H // NH
        FD = 64
        key = jax.random.key(seed)
        ks = jax.random.split(key, 12)
        B, S = (4, 1024)
        s = 1.0 / np.sqrt(H)
        sf = 1.0 / np.sqrt(HD)
        return {'query': jax.random.normal(ks[0], (B, S, H), jnp.float32), 'key': jax.random.normal(ks[1], (B, S, H), jnp.float32), 'value': jax.random.normal(ks[2], (B, S, H), jnp.float32), 'attention_mask': jnp.ones((B, S), jnp.float32), 'Wq': jax.random.normal(ks[3], (H, H), jnp.float32) * s, 'bq': jnp.zeros((H,), jnp.float32), 'Wk': jax.random.normal(ks[4], (H, H), jnp.float32) * s, 'bk': jnp.zeros((H,), jnp.float32), 'Wv': jax.random.normal(ks[5], (H, H), jnp.float32) * s, 'bv': jnp.zeros((H,), jnp.float32), 'Wqf': jax.random.normal(ks[6], (FD, HD), jnp.float32) * sf, 'Wkf': jax.random.normal(ks[7], (FD, HD), jnp.float32) * sf, 'Wo': jax.random.normal(ks[8], (H, H), jnp.float32) * s, 'bo': jnp.zeros((H,), jnp.float32)}
    _L3_xattn_all = _L3_xattn_setup()
    _L3_xattn_in = {k: v for k, v in _L3_xattn_all.items() if k in ('Wq', 'bq', 'Wk', 'bk', 'Wv', 'bv', 'Wqf', 'Wkf', 'Wo', 'bo')}
    del _L3_xattn_all

    def _L3_ffn_setup():
        import jax, jax.numpy as jnp
        import numpy as np
        E, H, I, TOPK = (16, 512, 352, 4)
        B, S = (2, 256)
        key = jax.random.key(seed)
        ks = jax.random.split(key, 6)
        hidden_states = jax.random.normal(ks[0], (B, S, H), dtype=jnp.float32)
        topk_idx = jax.random.randint(ks[1], (B, S, TOPK), 0, E)
        topk_weight = jax.random.uniform(ks[2], (B, S, TOPK), dtype=jnp.float32) / TOPK
        gate_weight = jax.random.normal(ks[3], (E, I, H), dtype=jnp.float32) * (1.0 / np.sqrt(H))
        up_weight = jax.random.normal(ks[4], (E, I, H), dtype=jnp.float32) * (1.0 / np.sqrt(H))
        down_weight = jax.random.normal(ks[5], (E, H, I), dtype=jnp.float32) * (1.0 / np.sqrt(I))
        return {'hidden_states': hidden_states, 'topk_idx': topk_idx, 'topk_weight': topk_weight, 'gate_weight': gate_weight, 'up_weight': up_weight, 'down_weight': down_weight}
    _L3_ffn_all = _L3_ffn_setup()
    _L3_ffn_in = {k: v for k, v in _L3_ffn_all.items() if k in ('topk_idx', 'topk_weight', 'gate_weight', 'up_weight', 'down_weight')}
    del _L3_ffn_all
    return {'x': x, 'ctx_2048': ctx_2048, 'itok_BxS_0_1023': itok_BxS_0_1023, 'mask_BxS2_ik0': mask_BxS2_ik0, 'mask_BxS2_ff1': mask_BxS2_ff1, 'L0_xattn_W_kvc': _L0_xattn_in['W_kvc'], 'L0_xattn_W_dq': _L0_xattn_in['W_dq'], 'L0_xattn_W_uq': _L0_xattn_in['W_uq'], 'L0_xattn_W_qr': _L0_xattn_in['W_qr'], 'L0_xattn_W_uk': _L0_xattn_in['W_uk'], 'L0_xattn_W_kr': _L0_xattn_in['W_kr'], 'L0_xattn_W_uv': _L0_xattn_in['W_uv'], 'L0_xattn_W_o': _L0_xattn_in['W_o'], 'L0_ffn_router_w': _L0_ffn_in['router_w'], 'L0_ffn_gate_up_w': _L0_ffn_in['gate_up_w'], 'L0_ffn_down_w': _L0_ffn_in['down_w'], 'L0_ffn_shared_gate_w': _L0_ffn_in['shared_gate_w'], 'L0_ffn_shared_up_w': _L0_ffn_in['shared_up_w'], 'L0_ffn_shared_down_w': _L0_ffn_in['shared_down_w'], 'L1_xattn_Wq': _L1_xattn_in['Wq'], 'L1_xattn_bq': _L1_xattn_in['bq'], 'L1_xattn_Wk': _L1_xattn_in['Wk'], 'L1_xattn_bk': _L1_xattn_in['bk'], 'L1_xattn_Wv': _L1_xattn_in['Wv'], 'L1_xattn_bv': _L1_xattn_in['bv'], 'L1_xattn_Wo': _L1_xattn_in['Wo'], 'L1_xattn_bo': _L1_xattn_in['bo'], 'L1_xattn_ln_gamma': _L1_xattn_in['ln_gamma'], 'L1_xattn_ln_beta': _L1_xattn_in['ln_beta'], 'L1_xattn_residual_scale': _L1_xattn_in['residual_scale'], 'L1_ffn_w1': _L1_ffn_in['w1'], 'L1_ffn_w2': _L1_ffn_in['w2'], 'L2_xattn_Wq': _L2_xattn_in['Wq'], 'L2_xattn_bq': _L2_xattn_in['bq'], 'L2_xattn_Wk': _L2_xattn_in['Wk'], 'L2_xattn_bk': _L2_xattn_in['bk'], 'L2_xattn_Wv': _L2_xattn_in['Wv'], 'L2_xattn_bv': _L2_xattn_in['bv'], 'L2_xattn_Wo': _L2_xattn_in['Wo'], 'L2_xattn_bo': _L2_xattn_in['bo'], 'L2_ffn_w_gate_up': _L2_ffn_in['w_gate_up'], 'L2_ffn_w_down': _L2_ffn_in['w_down'], 'L3_xattn_Wq': _L3_xattn_in['Wq'], 'L3_xattn_bq': _L3_xattn_in['bq'], 'L3_xattn_Wk': _L3_xattn_in['Wk'], 'L3_xattn_bk': _L3_xattn_in['bk'], 'L3_xattn_Wv': _L3_xattn_in['Wv'], 'L3_xattn_bv': _L3_xattn_in['bv'], 'L3_xattn_Wqf': _L3_xattn_in['Wqf'], 'L3_xattn_Wkf': _L3_xattn_in['Wkf'], 'L3_xattn_Wo': _L3_xattn_in['Wo'], 'L3_xattn_bo': _L3_xattn_in['bo'], 'L3_ffn_topk_idx': _L3_ffn_in['topk_idx'], 'L3_ffn_topk_weight': _L3_ffn_in['topk_weight'], 'L3_ffn_gate_weight': _L3_ffn_in['gate_weight'], 'L3_ffn_up_weight': _L3_ffn_in['up_weight'], 'L3_ffn_down_weight': _L3_ffn_in['down_weight']}

def reference(x, ctx_2048, itok_BxS_0_1023, mask_BxS2_ik0, mask_BxS2_ff1, L0_xattn_W_kvc, L0_xattn_W_dq, L0_xattn_W_uq, L0_xattn_W_qr, L0_xattn_W_uk, L0_xattn_W_kr, L0_xattn_W_uv, L0_xattn_W_o, L0_ffn_router_w, L0_ffn_gate_up_w, L0_ffn_down_w, L0_ffn_shared_gate_w, L0_ffn_shared_up_w, L0_ffn_shared_down_w, L1_xattn_Wq, L1_xattn_bq, L1_xattn_Wk, L1_xattn_bk, L1_xattn_Wv, L1_xattn_bv, L1_xattn_Wo, L1_xattn_bo, L1_xattn_ln_gamma, L1_xattn_ln_beta, L1_xattn_residual_scale, L1_ffn_w1, L1_ffn_w2, L2_xattn_Wq, L2_xattn_bq, L2_xattn_Wk, L2_xattn_bk, L2_xattn_Wv, L2_xattn_bv, L2_xattn_Wo, L2_xattn_bo, L2_ffn_w_gate_up, L2_ffn_w_down, L3_xattn_Wq, L3_xattn_bq, L3_xattn_Wk, L3_xattn_bk, L3_xattn_Wv, L3_xattn_bv, L3_xattn_Wqf, L3_xattn_Wkf, L3_xattn_Wo, L3_xattn_bo, L3_ffn_topk_idx, L3_ffn_topk_weight, L3_ffn_gate_weight, L3_ffn_up_weight, L3_ffn_down_weight):
    import jax
    import jax.numpy as jnp

    def _L0_xattn_ref(q, kv, seg_id, W_kvc, W_dq, W_uq, W_qr, W_uk, W_kr, W_uv, W_o):
        import jax, jax.numpy as jnp
        import numpy as np
        B, Lq, Lk = (2, 1024, 256)
        Q_DIM, KV_DIM = (512, 512)
        H, HD = (16, 128)
        KVC, QC, R = (128, 192, 64)
        LOOKBACK = 8
        NEG = -1e+30

        def _rope(x, L):
            half = x.shape[-1] // 2
            inv_freq = 1.0 / 10000.0 ** (jnp.arange(half, dtype=jnp.float32) / half)
            ang = jnp.arange(L, dtype=jnp.float32)[:, None] * inv_freq
            cos, sin = (jnp.cos(ang), jnp.sin(ang))
            x1, x2 = (x[..., :half], x[..., half:])
            return jnp.concatenate([x1 * cos - x2 * sin, x1 * sin + x2 * cos], axis=-1)
        b, lq, _ = q.shape
        lk = kv.shape[1]
        kv_c = kv @ W_kvc
        q_c = q @ W_dq
        q_nope = (q_c @ W_uq).reshape(b, lq, H, HD).transpose(0, 2, 1, 3)
        q_rope = (q_c @ W_qr).reshape(b, lq, H, R).transpose(0, 2, 1, 3)
        k_nope = (kv_c @ W_uk).reshape(b, lk, H, HD)
        v = (kv_c @ W_uv).reshape(b, lk, H, HD)
        k_rope = kv_c @ W_kr
        q_rope = _rope(q_rope, lq)
        k_rope = _rope(k_rope, lk)
        scale = 1.0 / np.sqrt(HD + R).astype(np.float32)
        scores = (jnp.einsum('bhqd,bkhd->bhqk', q_nope, k_nope) + jnp.einsum('bhqr,bkr->bhqk', q_rope, k_rope)) * scale
        k_ids = jnp.arange(lk)[None, None, :]
        qs = seg_id[:, :, None]
        good = (k_ids <= qs) & (k_ids >= qs - LOOKBACK)
        scores = jnp.where(good[:, None, :, :], scores, NEG)
        attn = jax.nn.softmax(scores, axis=-1)
        out = jnp.einsum('bhqk,bkhd->bqhd', attn, v).reshape(b, lq, H * HD)
        return out @ W_o

    def _L0_ffn_ref(hidden_states, router_w, gate_up_w, down_w, shared_gate_w, shared_up_w, shared_down_w):
        import jax, jax.numpy as jnp
        import numpy as np
        B, S, D, I, E, K = (4, 256, 512, 256, 8, 2)
        Bb, Ss, Dd = hidden_states.shape
        x = hidden_states.reshape(-1, Dd)
        T = x.shape[0]
        shared = jax.nn.silu(x @ shared_gate_w) * (x @ shared_up_w) @ shared_down_w
        logits = x @ router_w
        top_val, top_idx = jax.lax.top_k(logits, K)
        probs = jnp.zeros_like(logits).at[jnp.arange(T)[:, None], top_idx].set(jax.nn.sigmoid(top_val))
        xin = probs.T[:, :, None] * x[None]
        gu = jnp.einsum('etd,edf->etf', xin, gate_up_w)
        gate, up = jnp.split(gu, 2, axis=-1)
        h = jax.nn.silu(gate) * up
        expert_out = jnp.einsum('eti,eid->etd', h, down_w)
        combined = shared + expert_out.sum(axis=0)
        return combined.reshape(Bb, Ss, Dd)

    def _L1_xattn_ref(hidden_states, audio_tokens, attention_mask, Wq, bq, Wk, bk, Wv, bv, Wo, bo, ln_gamma, ln_beta, residual_scale):
        import jax, jax.numpy as jnp
        import numpy as np
        import math
        H = 512
        NH = 16
        HD = H // NH
        EPS_LN = 1e-05
        RES_SCALE_MAX = 0.3

        def _nan_clean(x, lim=10000.0):
            return jnp.nan_to_num(x, nan=0.0, posinf=lim, neginf=-lim)
        B, S, _ = hidden_states.shape
        T = audio_tokens.shape[1]
        hs = _nan_clean(hidden_states).astype(jnp.float32)
        at = _nan_clean(audio_tokens).astype(jnp.float32)

        def proj(x, W, b, L):
            y = x @ W.T + b
            return y.reshape(B, L, NH, HD).transpose(0, 2, 1, 3)
        q = _nan_clean(proj(hs, Wq, bq, S))
        k = _nan_clean(proj(at, Wk, bk, T))
        v = _nan_clean(proj(at, Wv, bv, T))
        scale = max(math.sqrt(HD), 1e-08)
        scores = jnp.einsum('bhsd,bhtd->bhst', q, k) / scale
        scores = jnp.clip(scores, -50.0, 50.0)
        scores = jnp.nan_to_num(scores, nan=0.0, posinf=50.0, neginf=-50.0)
        attend = (attention_mask.astype(jnp.float32) > 0.5)[:, None, None, :]
        scores = jnp.where(attend, scores, -10000.0)
        scores = jnp.clip(scores, -50.0, 50.0)
        probs = jax.nn.softmax(scores, axis=-1)
        probs = jnp.nan_to_num(probs, nan=0.0, posinf=1.0, neginf=0.0)
        probs = probs / (probs.sum(axis=-1, keepdims=True) + 1e-08)
        ctx = jnp.einsum('bhst,bhtd->bhsd', probs, v)
        ctx = ctx.transpose(0, 2, 1, 3).reshape(B, S, H)
        delta = _nan_clean(ctx @ Wo.T + bo)
        rs = jnp.clip(residual_scale, 0.0, RES_SCALE_MAX)
        delta = rs * delta
        mu = delta.mean(axis=-1, keepdims=True)
        var = jnp.mean((delta - mu) ** 2, axis=-1, keepdims=True)
        delta = (delta - mu) / jnp.sqrt(var + EPS_LN) * ln_gamma + ln_beta
        return delta

    def _L1_ffn_ref(x, w1, w2):
        import jax, jax.numpy as jnp
        import numpy as np
        EPS = 1e-05

        def activation_quant(x):
            scale = 127.0 / jnp.clip(jnp.max(jnp.abs(x), axis=-1, keepdims=True), EPS, None)
            xq = jnp.clip(jnp.round(x * scale), -128.0, 127.0) / scale
            return x + jax.lax.stop_gradient(xq - x)

        def weight_quant(w):
            scale = 1.0 / jnp.clip(jnp.mean(jnp.abs(w)), EPS, None)
            wq = jnp.clip(jnp.round(w * scale), -1.0, 1.0) / scale
            return w + jax.lax.stop_gradient(wq - w)

        def bitlinear(x, w):
            return jnp.einsum('bsd,od->bso', activation_quant(x), weight_quant(w))
        h = bitlinear(x, w1)
        h = jax.nn.relu(h)
        return bitlinear(h, w2)

    def _L2_xattn_ref(query, key_value, Wq, bq, Wk, bk, Wv, bv, Wo, bo):
        import jax, jax.numpy as jnp
        import numpy as np
        D_MODEL = 512
        NUM_HEADS = 16
        HEAD_DIM = D_MODEL // NUM_HEADS
        B, S, _ = query.shape
        T = key_value.shape[1]
        Q = query @ Wq.T + bq
        K = key_value @ Wk.T + bk
        V = key_value @ Wv.T + bv
        Q = Q.reshape(B, S, NUM_HEADS, HEAD_DIM).transpose(0, 2, 1, 3)
        K = K.reshape(B, T, NUM_HEADS, HEAD_DIM).transpose(0, 2, 1, 3)
        V = V.reshape(B, T, NUM_HEADS, HEAD_DIM).transpose(0, 2, 1, 3)
        scale = 1.0 / np.sqrt(HEAD_DIM).astype(np.float32)
        scores = jnp.einsum('bhsd,bhtd->bhst', Q, K) * scale
        attn = jax.nn.softmax(scores, axis=-1)
        ctx = jnp.einsum('bhst,bhtd->bhsd', attn, V)
        ctx = ctx.transpose(0, 2, 1, 3).reshape(B, S, D_MODEL)
        return ctx @ Wo.T + bo

    def _L2_ffn_ref(h_shard, w_gate_up, w_down):
        import jax, jax.numpy as jnp
        import numpy as np
        HIDDEN = 512
        INTER = 2048
        BATCH, LOCAL_SEQ = (2, 1024)
        batch, local_seq, hidden = h_shard.shape
        gate_up = jnp.einsum('bsh,oh->bso', h_shard, w_gate_up)
        gate, up = jnp.split(gate_up, 2, axis=-1)
        h = jax.nn.silu(gate) * up
        out = jnp.einsum('bsi,hi->bsh', h, w_down)
        return out

    def _L3_xattn_ref(query, key, value, attention_mask, Wq, bq, Wk, bk, Wv, bv, Wqf, Wkf, Wo, bo):
        import jax, jax.numpy as jnp
        import numpy as np
        H = 512
        NH = 16
        HD = H // NH
        FD = 64
        B, Sq, _ = query.shape
        Sk = key.shape[1]

        def heads(x, W, b, S):
            return (x @ W.T + b).reshape(B, S, NH, HD).transpose(0, 2, 1, 3)
        q = heads(query, Wq, bq, Sq)
        k = heads(key, Wk, bk, Sk)
        v = heads(value, Wv, bv, Sk)
        q_prime = jax.nn.relu(jnp.einsum('bhnd,fd->bhnf', q, Wqf))
        k_prime = jax.nn.relu(jnp.einsum('bhnd,fd->bhnf', k, Wkf))
        k_prime = k_prime * attention_mask[:, None, :, None]
        kv = jnp.einsum('bhnf,bhne->bhfe', k_prime, v)
        qkv = jnp.einsum('bhmf,bhfe->bhme', q_prime, kv)
        k_sum = jnp.sum(k_prime, axis=2)
        qk_sum = jnp.einsum('bhmf,bhf->bhm', q_prime, k_sum)[..., None]
        out = qkv / (qk_sum + 1e-08)
        out = out.transpose(0, 2, 1, 3).reshape(B, Sq, H)
        return out @ Wo.T + bo

    def _L3_ffn_ref(hidden_states, topk_idx, topk_weight, gate_weight, up_weight, down_weight):
        import jax, jax.numpy as jnp
        import numpy as np
        E, H, I, TOPK = (16, 512, 352, 4)
        B, S = (2, 256)
        b, s, h = hidden_states.shape
        n_tokens = b * s
        topk = topk_idx.shape[-1]
        x = hidden_states.reshape(n_tokens, h)
        flat_expert = topk_idx.reshape(-1)
        flat_weight = topk_weight.reshape(-1).astype(hidden_states.dtype)
        perm = jnp.argsort(flat_expert)
        tok = jnp.repeat(jnp.arange(n_tokens), topk)[perm]
        xs = x[tok]
        group_sizes = jnp.bincount(flat_expert, length=E).astype(jnp.int32)
        gate = jax.lax.ragged_dot(xs, jnp.swapaxes(gate_weight, 1, 2), group_sizes)
        up = jax.lax.ragged_dot(xs, jnp.swapaxes(up_weight, 1, 2), group_sizes)
        h_act = jax.nn.silu(gate) * up
        down = jax.lax.ragged_dot(h_act, jnp.swapaxes(down_weight, 1, 2), group_sizes)
        w_sorted = flat_weight[perm]
        out = jnp.zeros((n_tokens, h), hidden_states.dtype).at[tok].add(down * w_sorted[:, None])
        return out.reshape(b, s, h)
    x = x + _L0_xattn_ref(_layernorm(x, axis=-1), ctx_2048, itok_BxS_0_1023, L0_xattn_W_kvc, L0_xattn_W_dq, L0_xattn_W_uq, L0_xattn_W_qr, L0_xattn_W_uk, L0_xattn_W_kr, L0_xattn_W_uv, L0_xattn_W_o)
    x = x + _L0_ffn_ref(_layernorm(x, axis=-1), L0_ffn_router_w, L0_ffn_gate_up_w, L0_ffn_down_w, L0_ffn_shared_gate_w, L0_ffn_shared_up_w, L0_ffn_shared_down_w)
    x = x + _L1_xattn_ref(_layernorm(x, axis=-1), ctx_2048, mask_BxS2_ik0, L1_xattn_Wq, L1_xattn_bq, L1_xattn_Wk, L1_xattn_bk, L1_xattn_Wv, L1_xattn_bv, L1_xattn_Wo, L1_xattn_bo, L1_xattn_ln_gamma, L1_xattn_ln_beta, L1_xattn_residual_scale)
    x = x + _L1_ffn_ref(_layernorm(x, axis=-1), L1_ffn_w1, L1_ffn_w2)
    x = x + _L2_xattn_ref(_layernorm(x, axis=-1), ctx_2048, L2_xattn_Wq, L2_xattn_bq, L2_xattn_Wk, L2_xattn_bk, L2_xattn_Wv, L2_xattn_bv, L2_xattn_Wo, L2_xattn_bo)
    x = x + _L2_ffn_ref(_layernorm(x, axis=-1), L2_ffn_w_gate_up, L2_ffn_w_down)
    x = x + _L3_xattn_ref(_layernorm(x, axis=-1), ctx_2048, ctx_2048, mask_BxS2_ff1, L3_xattn_Wq, L3_xattn_bq, L3_xattn_Wk, L3_xattn_bk, L3_xattn_Wv, L3_xattn_bv, L3_xattn_Wqf, L3_xattn_Wkf, L3_xattn_Wo, L3_xattn_bo)
    x = x + _L3_ffn_ref(_layernorm(x, axis=-1), L3_ffn_topk_idx, L3_ffn_topk_weight, L3_ffn_gate_weight, L3_ffn_up_weight, L3_ffn_down_weight)
    return x

_drawn_inputs = setup_inputs


def setup_inputs(seed=0):
    import zlib

    import numpy as np

    out = dict(_drawn_inputs(seed))
    spreads = {'L1_xattn_bq': (0.0, 0.322),
     'L1_xattn_bk': (0.0, 2.0),
     'L1_xattn_bv': (0.0, 0.1),
     'L1_xattn_bo': (0.0, 0.1),
     'L1_xattn_ln_gamma': (1.0, 0.2),
     'L1_xattn_ln_beta': (0.0, 0.1),
     'L2_xattn_bq': (0.0, 0.705),
     'L2_xattn_bk': (0.0, 2.0),
     'L2_xattn_bv': (0.0, 0.1),
     'L2_xattn_bo': (0.0, 0.1),
     'L3_xattn_bq': (0.0, 2.0),
     'L3_xattn_bk': (0.0, 2.0),
     'L3_xattn_bv': (0.0, 0.1),
     'L3_xattn_bo': (0.0, 0.1)}
    factors = {'L3_xattn_Wq': 16.365, 'L3_xattn_Wqf': 11.013, 'L3_xattn_Wk': 3.182, 'L3_xattn_Wkf': 3.417}
    for name, (base, spread) in spreads.items():
        noise = np.random.default_rng([zlib.crc32(name.encode()), seed]).standard_normal(out[name].shape)
        drawn = base * np.exp(spread * noise) if base else spread * noise
        out[name] = jnp.asarray(drawn.astype(out[name].dtype))
    for name, factor in factors.items():
        out[name] = (out[name] * factor).astype(out[name].dtype)
    return out
```

```python
from contextlib import ExitStack

import concourse.bass as bass
import numpy as np
from concourse import mybir

ALU = mybir.AluOpType
ACT = mybir.ActivationFunctionType
AX = mybir.AxisListType
F32 = mybir.dt.float32
F32R = mybir.dt.float32r
BF16 = mybir.dt.bfloat16
I32 = mybir.dt.int32

P = 128
D = 512
KD = D // P
B, S = 8, 100
T = B * S
HALF = T // 2
C = 361
CP = C + C % 2
EPS_LN = 1e-5


class Core:
    SHARED, SET_SIZES = 24, (72, 48)

    def __init__(self, nc, ctx, stages):
        self.nc, self.ctx, self.sems = nc, ctx, {}
        self.holders = [nc.alloc_semaphore(name=f"held_{n}") for n in range(self.SHARED + sum(self.SET_SIZES))]
        self.stages = {st.name: st.index for st in stages}
        self.used = {name: 0 for name in [*self.stages, "shared"]}

    def first_of(self, parity):
        return self.SHARED + (self.SET_SIZES[0] if parity else 0)

    def sem(self, name):
        if name not in self.sems:
            owner = name.split("_")[0] if name.split("_")[0] in self.stages else "shared"
            n, size = self.used[owner], self.SHARED
            self.used[owner] += 1
            if owner != "shared":
                parity = self.stages[owner] % 2
                size, at = self.SET_SIZES[parity], self.first_of(parity) + n
            else:
                at = n
            assert n < size, f"too many semaphores for {owner}"
            number = self.holders[at].num
            self.nc.release_semaphore(self.holders[at])
            self.sems[name] = self.holders[at] = self.nc.alloc_semaphore(name=name, num=number)
        return self.sems[name]

    def apart(self, engine):
        engine.nop().then_inc(self.sem("waits_passed"), 1)

    def enter(self, engine, st):
        if st.index >= 2:
            engine.wait_ge(self.sem("sets_cleared"), st.index - 1)
            engine.nop().then_inc(self.sem("stages_entered"), 1)

    def leave(self, engine, name):
        engine.nop().then_inc(self.sem(f"{name}_left_stages"), 1)

    def clear_set(self, sp, st):
        if st.index:
            for name in ("pool", "tensor", "scalar", "vector"):
                sp.wait_ge(self.sem(f"{name}_left_stages"), st.index)
            parity = (st.index - 1) % 2
            first = self.holders[self.first_of(parity)].num
            sp.sem_clear(range(first, first + self.SET_SIZES[parity])).then_inc(self.sem("sets_cleared"), 1)

    def sb(self, ctx, name, shape, dt=F32):
        return ctx.enter_context(self.nc.sbuf_tensor(name, shape, dt))


def wait(engine, semaphore, value):
    if isinstance(value, int) and value <= 0:
        return
    engine.wait_ge(semaphore, value)


def product(pe, outs, weight_hi, weight_lo, moving, first, last):
    n = len(outs)
    for i in range(n):
        pe.matmul(outs[i], weight_hi, moving[i][0], start=first, stop=False)
        pe.matmul(outs[i], weight_hi, moving[i][1], start=False, stop=False)
    for i in range(n):
        mm = pe.matmul(outs[i], weight_lo, moving[i][0], start=False, stop=last)
    return mm



def ln_pe(c, pe, st):
    before = 2 * st.index
    pe.wait_ge(c.sem("residual_ready"), st.index + 1)
    for h in range(2):
        for k in range(KD):
            mm = pe.matmul(c.psum[:, h, 0:HALF], c.mean_matrix[:, :],
                           c.residual[:, k, h * HALF:(h + 1) * HALF], start=k == 0, stop=k == KD - 1)
        mm.then_inc(c.sem("ln_mean"), 1)
    for h in range(2):
        pe.wait_ge(c.sem("ln_squares"), before + h + 1)
        for k in range(KD):
            mm = pe.matmul(c.psum[:, 2 + h, 0:HALF], c.mean_matrix[:, :],
                           c.ln_squares[:, k, h * HALF:(h + 1) * HALF], start=k == 0, stop=k == KD - 1)
        mm.then_inc(c.sem("ln_variance"), 1)


def ln_dve(c, dve, st):
    before = 2 * st.index
    centered, high = c.sem("ln_centered"), c.sem("ln_xn_hi")
    for h in range(2):
        t = slice(h * HALF, (h + 1) * HALF)
        dve.wait_ge(c.sem("ln_mean"), before + h + 1)
        mean = c.psum[:, h, 0:HALF].unsqueeze(1).broadcast_to([P, KD, HALF])
        dve.tensor_tensor(c.xn[:, :, t], c.residual[:, :, t], mean, ALU.subtract).then_inc(centered, 1)
    for h in range(2):
        t = slice(h * HALF, (h + 1) * HALF)
        dve.wait_ge(c.sem("ln_std"), before + h + 1)
        dve.reciprocal(c.ln_rstd[:, t], c.ln_std[:, t]).then_inc(c.sem("ln_rstd"), 1)
        dve.wait_ge(c.sem("ln_rstd"), before + h + 1)
        dve.wait_ge(centered, before + h + 1)
        rstd = c.ln_rstd[:, t].unsqueeze(1).broadcast_to([P, KD, HALF])
        dve.tensor_tensor(c.xn[:, :, t], c.xn[:, :, t], rstd, ALU.mult).then_inc(c.sem("ln_xn"), 1)
    for h in range(2):
        t = slice(h * HALF, (h + 1) * HALF)
        dve.wait_ge(high, before + h + 1)
        dve.tensor_tensor(c.xn_lo[:, :, t], c.xn[:, :, t], c.xn_hi[:, :, t],
                          ALU.subtract).then_inc(c.sem("ln_xn_lo"), 1)


def ln_act(c, act, st):
    before = 2 * st.index
    for h in range(2):
        t = slice(h * HALF, (h + 1) * HALF)
        act.wait_ge(c.sem("ln_centered"), before + h + 1)
        act.activation(c.ln_squares[:, :, t], c.xn[:, :, t], ACT.Square).then_inc(
            c.sem("ln_squares"), 1)
    for h in range(2):
        act.wait_ge(c.sem("ln_variance"), before + h + 1)
        act.activation(c.ln_std[:, h * HALF:(h + 1) * HALF], c.psum[:, 2 + h, 0:HALF], ACT.Sqrt,
                       bias=c.eps[:, 0:1]).then_inc(c.sem("ln_std"), 1)
    for h in range(2):
        t = slice(h * HALF, (h + 1) * HALF)
        act.wait_ge(c.sem("ln_xn"), before + h + 1)
        act.activation(c.xn_hi[:, :, t], c.xn[:, :, t], ACT.Copy).then_inc(c.sem("ln_xn_hi"), 1)



class Ffn:
    def __init__(self, name, index, chunks, blocks, tokens, scale, slabs_at, experts=0):
        self.name, self.index, self.chunks, self.blocks = name, index, chunks, blocks
        self.tokens = tokens
        self.scale = scale
        self.slabs_at, self.experts = slabs_at, experts
        self.halves = [(0, HALF), (HALF, T)] if tokens == T else [(0, tokens)]
        self.gu_slabs, self.dn_slabs = 2 * blocks, blocks
        self.per_chunk = 3 * blocks

    def buffers(self, c, own):
        n = self.name
        self.raw_gu = c.sb(own, n + "_raw_gu", [P, self.gu_slabs, 512])
        self.raw_dn = c.sb(own, n + "_raw_dn", [P, self.dn_slabs, 512])
        self.w = [c.sb(own, n + "_" + x, [P, self.gu_slabs if "gu" in x else self.dn_slabs, 512], F32R)
                  for x in ("w_gu_hi", "w_gu_lo", "w_dn_hi", "w_dn_lo")]
        self.h_hi, self.h_lo = (c.sb(own, n + x, [P, 2, self.blocks, self.tokens], F32R) for x in ("_h_hi", "_h_lo"))
        self.h, self.silu, self.up, self.gate = (c.sb(own, n + x, [P, 2, self.tokens]) for x in ("_h", "_silu", "_up", "_gate"))
        self.scales = c.sb(own, n + "_scales", [P, self.tokens])
        if self.experts:
            self.expert_row = c.sb(own, n + "_expert_row", [self.experts, 2, self.tokens])
            self.expert_weights = c.sb(own, n + "_expert_weights", [self.experts, self.tokens])

    def sync(self, c, sp):
        ffn_sync(c, sp, self)

    def pool(self, c, pool):
        ffn_pool(c, pool, self)

    def pe(self, c, pe):
        ln_pe(c, pe, self)
        self.prepare_pe(c, pe)
        ffn_pe(c, pe, self)

    def act(self, c, act):
        act.wait_ge(c.sem("residual_ready"), self.index + 1)
        for j in range(self.gu_slabs):
            ffn_high_gu(c, act, self, 0, j)
        ln_act(c, act, self)
        self.prepare_act(c, act)
        ffn_act(c, act, self)

    def dve(self, c, dve):
        ln_dve(c, dve, self)
        self.prepare_dve(c, dve)
        ffn_dve(c, dve, self)

    def prepare_pe(self, c, pe):
        pass

    def prepare_act(self, c, act):
        pass

    def prepare_dve(self, c, dve):
        pass

    def views(self, c, bank):
        return [c.psum[:, bank + n, 0:b - a] for n, (a, b) in enumerate(self.halves)]

    def span(self, c, bank):
        if len(self.halves) == 1:
            return c.psum[:, bank, 0:self.tokens]
        return c.psum[:, bank:bank + 2, 0:HALF]

    def cut(self, ap):
        return ap if len(self.halves) == 1 else ap.rearrange("p (h t) -> p h t", h=2)


def ffn_schedule(engine, st, gate_up, down):
    n = st.chunks
    gate_up(0, 0)
    gate_up(1, 1)
    down(0, 0)
    turns = (n - 3) // 2
    with engine.Fori(0, turns) as i:
        gate_up(i * 2 + 2, 0)
        down(i * 2 + 1, 1)
        gate_up(i * 2 + 3, 1)
        down(i * 2 + 2, 0)
    for x in range(2 * turns + 1, n):
        if x + 1 < n:
            gate_up(x + 1, (x + 1) % 2)
        down(x, x % 2)


def ffn_sync(c, sp, st):
    def load(raw, landed, split, count, at, n_of_kind, chunk):
        for j in range(count):
            wait(sp, split, (chunk - 1) * count + j + 1 if not isinstance(chunk, int) or chunk else 0)
            sp.dma_start(raw[:, j, :], c.slabs[bass.DynSlice(at + j, 1), :, :].rearrange("a p n -> p (a n)")
                         if not isinstance(at, int) else c.slabs[at + j, :, :]).then_inc(
                             c.sem(f"{landed}{j}"), 16)

    def gate_up(chunk, q):
        load(st.raw_gu, st.name + "_gu_landed", c.sem(st.name + "_gu_split"), st.gu_slabs,
             chunk * st.per_chunk + st.slabs_at, st.gu_slabs, chunk)

    def down(chunk, q):
        load(st.raw_dn, st.name + "_dn_landed", c.sem(st.name + "_dn_split"), st.dn_slabs,
             chunk * st.per_chunk + st.slabs_at + st.gu_slabs, st.dn_slabs, chunk)
    sp.wait_ge(c.sem("residual_ready"), st.index + 1)
    ffn_schedule(sp, st, gate_up, down)


def ffn_pool(c, pool, st):
    def split(raw, hi, lo, kind, count, chunk):
        for j in range(count):
            pool.wait_ge(c.sem(f"{st.name}_{kind}_hi"), chunk * count + j + 1)
            pool.tensor_tensor(lo[:, j, :], raw[:, j, :], hi[:, j, :], ALU.subtract).then_inc(
                c.sem(f"{st.name}_{kind}_split"), 1)

    pool.wait_ge(c.sem("residual_ready"), st.index + 1)
    ffn_schedule(pool, st, lambda chunk, q: split(st.raw_gu, st.w[0], st.w[1], "gu", st.gu_slabs, chunk),
                 lambda chunk, q: split(st.raw_dn, st.w[2], st.w[3], "dn", st.dn_slabs, chunk))


def ffn_high_gu(c, act, st, chunk, j):
    if not isinstance(chunk, int) or chunk:
        units = 2 * st.blocks + (st.scale != "none")
        act.wait_ge(c.sem(st.name + "_gu_units"), (chunk - 1) * units + j + 1 + (units - st.gu_slabs))
    act.wait_ge(c.sem(f"{st.name}_gu_landed{j}"), (chunk + 1) * 16)
    act.activation(st.w[0][:, j, :], st.raw_gu[:, j, :], ACT.Copy).then_inc(c.sem(st.name + "_gu_hi"), 1)


def ffn_high_dn(c, act, st, chunk, j):
    if not isinstance(chunk, int) or chunk:
        act.wait_ge(c.sem(st.name + "_dn_units"), (chunk - 1) * KD + (4 * j + 3) // st.blocks + 1)
    act.wait_ge(c.sem(f"{st.name}_dn_landed{j}"), (chunk + 1) * 16)
    act.activation(st.w[2][:, j, :], st.raw_dn[:, j, :], ACT.Copy).then_inc(c.sem(st.name + "_dn_hi"), 1)


def ffn_pe(c, pe, st):
    nb = st.blocks
    gate_read = "_gate_scaled" if st.scale == "before" else "_g_read"
    up_read = "_h" if st.scale == "none" else "_u_read"

    def gate_up(chunk, q):
        if st.scale != "none":
            pe.wait_ge(c.sem(st.name + "_row"), chunk + 1)
            if not isinstance(chunk, int) or chunk:
                pe.wait_ge(c.sem(st.name + "_u_read"), chunk * nb)
            for (a, b), out in zip(st.halves, st.views(c, 2)):
                mm = pe.matmul(out, c.ones[0:st.experts, :], st.expert_row[0:st.experts, q, a:b],
                               start=True, stop=True)
            mm.then_inc(c.sem(st.name + "_gu_units"), 1)
        for j in range(2 * nb):
            pe.wait_ge(c.sem(st.name + "_gu_split"), chunk * st.gu_slabs + j + 1)
            if j % 2 == 0:
                wait(pe, c.sem(st.name + gate_read), chunk * nb + j // 2)
            else:
                wait(pe, c.sem(st.name + up_read), chunk * nb + j // 2)
                if j == 1 and st.scale != "none":
                    pe.wait_ge(c.sem(st.name + "_scale_copied"), chunk + 1)
            outs = st.views(c, 0 if j % 2 == 0 else 2)
            for k in range(KD):
                w = slice(k * P, (k + 1) * P)
                mm = product(pe, outs, st.w[0][:, j, w], st.w[1][:, j, w],
                             [(c.xn_hi[:, k, a:b], c.xn_lo[:, k, a:b]) for a, b in st.halves],
                             k == 0, k == KD - 1)
            mm.then_inc(c.sem(st.name + "_gu_units"), 1)

    def down(chunk, q):
        pe.wait_ge(c.sem(st.name + "_h_lo"), (chunk + 1) * nb)
        for m in range(KD):
            pe.wait_ge(c.sem(st.name + "_dn_split"), chunk * st.dn_slabs + (m * nb + nb - 1) // 4 + 1)
            if m < 2:
                wait(pe, c.sem(st.name + "_added"), chunk * KD + m - 1 if not isinstance(chunk, int) or chunk else 0)
            else:
                pe.wait_ge(c.sem(st.name + "_added"), chunk * KD + m - 1)
            outs = st.views(c, 4 + 2 * (m % 2))
            for k in range(nb):
                tile = m * nb + k
                j, w = tile // 4, slice(tile % 4 * P, (tile % 4 + 1) * P)
                mm = product(pe, outs, st.w[2][:, j, w], st.w[3][:, j, w],
                             [(st.h_hi[:, q, k, a:b], st.h_lo[:, q, k, a:b]) for a, b in st.halves],
                             k == 0, k == nb - 1)
            mm.then_inc(c.sem(st.name + "_dn_units"), 1)
    for h in range(2):
        pe.wait_ge(c.sem("ln_xn_lo"), 2 * st.index + h + 1)
    ffn_schedule(pe, st, gate_up, down)


def ffn_act(c, act, st):
    nb, n = st.blocks, st.tokens

    def more(chunk):
        return not isinstance(chunk, int) or chunk + 1 < st.chunks

    def gate_up(chunk, q):
        if st.scale != "none":
            units = chunk * (2 * nb + 1)
            act.wait_ge(c.sem(st.name + "_gu_units"), units + 1)
            if not isinstance(chunk, int) or chunk:
                act.wait_ge(c.sem(st.name + "_u_read"), chunk * nb)
            act.activation(st.cut(st.scales[:, 0:n]), st.span(c, 2), ACT.Copy).then_inc(
                c.sem(st.name + "_scale_copied"), 1)

        def split_high(j):
            act.wait_ge(c.sem(st.name + "_h"), chunk * nb + j + 1)
            act.activation(st.h_hi[:, q, j, 0:n], st.h[:, (q * nb + j) % 2, 0:n], ACT.Copy).then_inc(
                c.sem(st.name + "_h_hi"), 1)
        for j in range(nb):
            b = (q * nb + j) % 2
            if not (isinstance(chunk, int) and chunk == 0 and j < 2):
                act.wait_ge(c.sem(st.name + "_h"), chunk * nb + j - 1)
            if st.scale == "before":
                act.wait_ge(c.sem(st.name + "_gate_scaled"), chunk * nb + j + 1)
                act.activation(st.silu[:, b, 0:n], st.gate[:, b, 0:n], ACT.Silu).then_inc(
                    c.sem(st.name + "_silu"), 1)
            else:
                first = 1 if st.scale != "none" else 0
                act.wait_ge(c.sem(st.name + "_gu_units"), chunk * (2 * nb + first) + first + 2 * j + 1)
                act.activation(st.cut(st.silu[:, b, 0:n]), st.span(c, 0), ACT.Silu).then_inc(
                    c.sem(st.name + "_g_read"), 1)
            if more(chunk):
                for slab in range(max(2 * j - 1, 0), 2 * j + 1):
                    ffn_high_gu(c, act, st, chunk + 1, slab)
            if j:
                split_high(j - 1)
        split_high(nb - 1)
        if more(chunk):
            ffn_high_gu(c, act, st, chunk + 1, 2 * nb - 1)

    def down(chunk, q):
        if more(chunk):
            for j in range(st.dn_slabs):
                ffn_high_dn(c, act, st, chunk + 1, j)
    for j in range(st.dn_slabs):
        ffn_high_dn(c, act, st, 0, j)
    ffn_schedule(act, st, gate_up, down)


def ffn_dve(c, dve, st):
    nb, n = st.blocks, st.tokens
    first = 1 if st.scale != "none" else 0
    silu_done = c.sem(st.name + ("_silu" if st.scale == "before" else "_g_read"))

    def make_row(chunk, q):
        if not isinstance(chunk, int) or chunk >= 2:
            dve.wait_ge(c.sem(st.name + "_gu_units"), (chunk - 2) * (2 * nb + 1) + 1)
        e = st.experts
        column = (c.identity[0:e, chunk:chunk + 1] if isinstance(chunk, int)
                  else c.identity[0:e, bass.DynSlice(chunk, 1)])
        dve.tensor_scalar(st.expert_row[0:e, q, 0:n], st.expert_weights[0:e, 0:n], column, None,
                          ALU.mult).then_inc(c.sem(st.name + "_row"), 1)

    def gate_up(chunk, q):
        units = chunk * (2 * nb + first) + first

        def finish(j):
            b = (q * nb + j) % 2
            dve.wait_ge(silu_done, chunk * nb + j + 1)
            if st.scale == "none":
                dve.wait_ge(c.sem(st.name + "_gu_units"), units + 2 * j + 2)
                if not (isinstance(chunk, int) and chunk == 0 and j < 2):
                    dve.wait_ge(c.sem(st.name + "_h_hi"), chunk * nb + j - 1)
                    dve.wait_ge(c.sem(st.name + "_h_lo"), chunk * nb + j - 1)
                dve.tensor_tensor(st.cut(st.h[:, b, 0:n]), st.cut(st.silu[:, b, 0:n]), st.span(c, 2),
                                  ALU.mult).then_inc(c.sem(st.name + "_h"), 1)
            else:
                if not (isinstance(chunk, int) and chunk == 0 and j < 2):
                    dve.wait_ge(c.sem(st.name + "_h_hi"), chunk * nb + j - 1)
                    dve.wait_ge(c.sem(st.name + "_h_lo"), chunk * nb + j - 1)
                dve.wait_ge(c.sem(st.name + "_u_read"), chunk * nb + j + 1)
                dve.tensor_tensor(st.h[:, b, 0:n], st.silu[:, b, 0:n], st.up[:, b, 0:n],
                                  ALU.mult).then_inc(c.sem(st.name + "_h"), 1)

        def split_low(j):
            b = (q * nb + j) % 2
            dve.wait_ge(c.sem(st.name + "_h_hi"), chunk * nb + j + 1)
            dve.tensor_tensor(st.h_lo[:, q, j, 0:n], st.h[:, b, 0:n], st.h_hi[:, q, j, 0:n],
                              ALU.subtract).then_inc(c.sem(st.name + "_h_lo"), 1)
        if first:
            make_row(chunk + 1, 1 - q)
            dve.wait_ge(c.sem(st.name + "_scale_copied"), chunk + 1)
        for j in range(nb):
            b = (q * nb + j) % 2
            if st.scale == "before":
                dve.wait_ge(c.sem(st.name + "_gu_units"), units + 2 * j + 1)
                if not (isinstance(chunk, int) and chunk == 0 and j < 2):
                    dve.wait_ge(c.sem(st.name + "_silu"), chunk * nb + j - 1)
                dve.tensor_tensor(st.cut(st.gate[:, b, 0:n]), st.cut(st.scales[:, 0:n]), st.span(c, 0),
                                  ALU.mult).then_inc(c.sem(st.name + "_gate_scaled"), 1)
            if first:
                dve.wait_ge(c.sem(st.name + "_gu_units"), units + 2 * j + 2)
                dve.tensor_tensor(st.cut(st.up[:, b, 0:n]), st.cut(st.scales[:, 0:n]), st.span(c, 2),
                                  ALU.mult).then_inc(c.sem(st.name + "_u_read"), 1)
            finish(j)
            if j:
                split_low(j - 1)
        split_low(nb - 1)

    def down(chunk, q):
        for m in range(KD):
            dve.wait_ge(c.sem(st.name + "_dn_units"), chunk * KD + m + 1)
            if not (isinstance(chunk, int) and chunk == 0):
                dve.wait_ge(c.sem(st.name + "_added"), (chunk - 1) * KD + m + 1)
            into = st.cut(c.residual[:, m, 0:n])
            dve.tensor_tensor(into, into, st.span(c, 4 + 2 * (m % 2)), ALU.add).then_inc(
                c.sem(st.name + "_added"), 1)
    if first:
        make_row(0, 0)
    ffn_schedule(dve, st, gate_up, down)
    dve.wait_ge(c.sem(st.name + "_added"), st.chunks * KD)
    dve.nop().then_inc(c.sem("residual_ready"), 1)



class RoutedFfn(Ffn):
    ROUTED, TOP = 8, 2

    def buffers(self, c, own):
        super().buffers(c, own)
        n, e = self.name, self.ROUTED
        self.router = c.sb(own, n + "_router", [P, KD, e])
        self.router_hi, self.router_lo = (c.sb(own, n + x, [P, KD, e], F32R) for x in ("_router_hi", "_router_lo"))
        self.logits = c.sb(own, n + "_logits", [S, B, e])
        self.sigmoid = c.sb(own, n + "_sigmoid", [S, B, e])
        self.above = c.sb(own, n + "_above", [S, B, e, e])
        self.equal = c.sb(own, n + "_equal", [S, B, e, e])
        self.earlier = c.sb(own, n + "_earlier", [S, e, e])
        self.rank = c.sb(own, n + "_rank", [S, B, e])
        self.probs = c.sb(own, n + "_probs", [S, B, e + 1])

    def sync(self, c, sp):
        sp.wait_ge(c.sem("residual_ready"), self.index + 1)
        sp.dma_start(self.router[:, :, :], c.a["router"]).then_inc(c.sem(self.name + "_router_landed"), 16)
        sp.dma_start(self.earlier[:, :, :], c.a["earlier"]).then_inc(c.sem(self.name + "_earlier_landed"), 16)
        super().sync(c, sp)

    def prepare_pe(self, c, pe):
        for h in range(2):
            pe.wait_ge(c.sem("ln_xn_lo"), 2 * self.index + h + 1)
        pe.wait_ge(c.sem(self.name + "_router_split"), 2)
        for b in range(B):
            t = slice(b * S, (b + 1) * S)
            for k in range(KD):
                mm = product(pe, [c.psum[0:S, 4, b * self.ROUTED:(b + 1) * self.ROUTED]], c.xn_hi[:, k, t],
                             c.xn_lo[:, k, t], [(self.router_hi[:, k, :], self.router_lo[:, k, :])],
                             k == 0, k == KD - 1)
        mm.then_inc(c.sem(self.name + "_logits"), 1)
        pe.wait_ge(c.sem(self.name + "_probs"), 2)
        for b in range(B):
            mm = pe.transpose(c.psum[0:self.experts, 6 + b // 4, b % 4 * S:(b % 4 + 1) * S],
                              self.probs[:, b, :], c.identity[0:S, 0:S])
        mm.then_inc(c.sem(self.name + "_probs_turned"), 1)

    def prepare_act(self, c, act):
        act.wait_ge(c.sem(self.name + "_logits_copied"), 1)
        act.activation(self.sigmoid[:, :, :], self.logits[:, :, :], ACT.Sigmoid).then_inc(
            c.sem(self.name + "_sigmoid"), 1)

    def prepare_dve(self, c, dve):
        e, split, step = self.ROUTED, c.sem(self.name + "_router_split"), c.sem(self.name + "_ranking")
        dve.wait_ge(c.sem(self.name + "_router_landed"), 16)
        dve.tensor_copy(self.router_hi[:, :, :], self.router[:, :, :]).then_inc(split, 1)
        dve.wait_ge(split, 1)
        dve.tensor_tensor(self.router_lo[:, :, :], self.router[:, :, :], self.router_hi[:, :, :],
                          ALU.subtract).then_inc(split, 1)
        dve.wait_ge(c.sem(self.name + "_logits"), 1)
        dve.tensor_copy(self.logits[:, :, :], c.psum[0:S, 4, 0:B * e].rearrange("s (b e) -> s b e", b=B)).then_inc(
            c.sem(self.name + "_logits_copied"), 1)
        dve.wait_ge(c.sem(self.name + "_logits_copied"), 1)
        other = self.logits[:, :, :].unsqueeze(2).broadcast_to([S, B, e, e])
        mine = self.logits[:, :, :].unsqueeze(3).broadcast_to([S, B, e, e])
        dve.tensor_tensor(self.above[:, :, :, :], other, mine, ALU.is_gt).then_inc(step, 1)
        dve.tensor_tensor(self.equal[:, :, :, :], other, mine, ALU.is_equal).then_inc(step, 1)
        dve.wait_ge(c.sem(self.name + "_earlier_landed"), 16)
        dve.wait_ge(step, 2)
        dve.tensor_tensor(self.equal[:, :, :, :], self.equal[:, :, :, :],
                          self.earlier[:, :, :].unsqueeze(1).broadcast_to([S, B, e, e]), ALU.mult).then_inc(step, 1)
        dve.wait_ge(step, 3)
        dve.tensor_tensor(self.above[:, :, :, :], self.above[:, :, :, :], self.equal[:, :, :, :],
                          ALU.add).then_inc(step, 1)
        dve.wait_ge(step, 4)
        dve.tensor_reduce(self.rank[:, :, :], self.above[:, :, :, :], AX.X, ALU.add).then_inc(step, 1)
        dve.memset(self.probs[:, :, e:e + 1], 1.0).then_inc(c.sem(self.name + "_probs"), 1)
        dve.wait_ge(step, 5)
        dve.wait_ge(c.sem(self.name + "_sigmoid"), 1)
        dve.scalar_tensor_tensor(self.probs[:, :, 0:e], self.rank[:, :, :], float(self.TOP), self.sigmoid[:, :, :],
                                 ALU.is_lt, ALU.mult).then_inc(c.sem(self.name + "_probs"), 1)
        dve.wait_ge(c.sem(self.name + "_probs_turned"), 1)
        dve.tensor_copy(self.cut(self.expert_weights[:, :]), c.psum[0:self.experts, 6:8, 0:HALF]).then_inc(
            c.sem(self.name + "_weights"), 1)
        dve.wait_ge(c.sem(self.name + "_weights"), 1)


class ChosenFfn(Ffn):
    NAMES = 4

    def buffers(self, c, own):
        super().buffers(c, own)
        n, g = self.name, self.tokens // P
        self.groups = g
        self.names = c.sb(own, n + "_names", [P, g, self.NAMES], I32)
        self.names_f = c.sb(own, n + "_names_f", [P, g, self.NAMES])
        self.name_weights = c.sb(own, n + "_name_weights", [P, g, self.NAMES])
        self.expert_ids = c.sb(own, n + "_expert_ids", [P, self.experts])
        self.matches = c.sb(own, n + "_matches", [P, g, self.NAMES, self.experts])
        self.token_weights = c.sb(own, n + "_token_weights", [P, g, self.experts])

    def sync(self, c, sp):
        sp.wait_ge(c.sem("residual_ready"), self.index + 1)
        for name, buffer in (("names", self.names), ("name_weights", self.name_weights)):
            sp.dma_start(buffer[:, :, :], c.a[name]).then_inc(c.sem(f"{self.name}_{name}_landed"), 16)
        sp.dma_start(self.expert_ids[:, :], c.a["expert_ids"]).then_inc(c.sem(self.name + "_ids_landed"), 16)
        super().sync(c, sp)

    def prepare_pe(self, c, pe):
        pe.wait_ge(c.sem(self.name + "_token_weights"), 1)
        for g in range(self.groups):
            mm = pe.transpose(c.psum[0:self.experts, 6, g * P:(g + 1) * P], self.token_weights[:, g, :],
                              c.identity[:, :])
        mm.then_inc(c.sem(self.name + "_turned"), 1)

    def prepare_dve(self, c, dve):
        dve.wait_ge(c.sem(self.name + "_names_landed"), 16)
        dve.wait_ge(c.sem(self.name + "_name_weights_landed"), 16)
        dve.wait_ge(c.sem(self.name + "_ids_landed"), 16)
        dve.tensor_copy(self.names_f[:, :, :], self.names[:, :, :]).then_inc(c.sem(self.name + "_names_f"), 1)
        dve.wait_ge(c.sem(self.name + "_names_f"), 1)
        for g in range(self.groups):
            for k in range(self.NAMES):
                dve.tensor_scalar(self.matches[:, g, k, :], self.expert_ids[:, :], self.names_f[:, g, k:k + 1],
                                  self.name_weights[:, g, k:k + 1], ALU.is_equal, ALU.mult).then_inc(
                                      c.sem(self.name + "_matches"), 1)
        dve.wait_ge(c.sem(self.name + "_matches"), self.groups * self.NAMES)
        dve.tensor_reduce(self.token_weights[:, :, :], self.matches[:, :, :, :].rearrange("p g k e -> p g e k"),
                          AX.X, ALU.add).then_inc(c.sem(self.name + "_token_weights"), 1)
        dve.wait_ge(c.sem(self.name + "_turned"), 1)
        dve.tensor_copy(self.expert_weights[:, :], c.psum[0:self.experts, 6, 0:self.tokens]).then_inc(
            c.sem(self.name + "_weights"), 1)
        dve.wait_ge(c.sem(self.name + "_weights"), 1)



HEADS, HD = 16, 32
GROUP = P // HD
KEY_TILES = [(0, P), (P, 2 * P), (2 * P, C)]


def batches(engine, body):
    turns = (B - 4) // 2
    body(0, 0, True, True)
    with engine.Fori(0, turns) as i:
        body(i * 2 + 1, 1, True, True)
        body(i * 2 + 2, 0, True, True)
    for b in range(2 * turns + 1, B):
        body(b, b % 2, b + 1 < B, b + 2 < B)


def tokens_of(b):
    return slice(b * S, (b + 1) * S) if isinstance(b, int) else bass.DynSlice(b * S, S)


class Attention:
    K_AT, V_AT, Q_AT = 4, 8, 0
    RAW = 2
    VALUES_BANK = 7
    SCALE = 1.0 / float(HD) ** 0.5

    def __init__(self, name, index, slabs_at):
        self.name, self.index, self.slabs_at = name, index, slabs_at
        self.places = ([self.K_AT + j for j in range(4)] + [self.V_AT + j for j in range(4)]
                       + [self.Q_AT + j for j in range(4)] + [self.Q_AT + j for j in range(4)])
        self.biases = ["bq", "bk", "bo"]

    def buffers(self, c, own):
        n = self.name
        self.c = c
        self.w_hi, self.w_lo = (c.sb(own, n + x, [P, 12, 512], F32R) for x in ("_w_hi", "_w_lo"))
        self.w_raw = c.sb(own, n + "_w_raw", [P, self.RAW, 512])
        self.ctx_raw = c.sb(own, n + "_ctx_raw", [P, KD, CP])
        self.ctx_hi, self.ctx_lo = (c.sb(own, n + x, [P, 2, KD, CP], F32R) for x in ("_ctx_hi", "_ctx_lo"))
        self.k_hi, self.k_lo = (c.sb(own, n + x, [P, 2, KD, CP], F32R) for x in ("_k_hi", "_k_lo"))
        self.v = c.sb(own, n + "_v", [P, 2, 3, D])
        self.bv = c.sb(own, n + "_bv", [P, D])
        self.vectors = c.sb(own, n + "_vectors", [P, len(self.biases), KD])
        self.own_buffers(c, own)

    def own_buffers(self, c, own):
        n = self.name
        self.qm_hi, self.qm_lo = (c.sb(own, n + x, [P, HEADS, S], F32R) for x in ("_qm_hi", "_qm_lo"))
        self.probs = c.sb(own, n + "_probs", [S, GROUP, C])
        self.highest = c.sb(own, n + "_highest", [S, GROUP])
        self.shift = c.sb(own, n + "_shift", [S, GROUP])
        self.total = c.sb(own, n + "_total", [S, GROUP])
        self.inverse = c.sb(own, n + "_inverse", [S, GROUP])

    def turned(self, c):
        return c.ln_squares[:, :, :].rearrange("p k t -> p (k t)")[:, 0:3 * GROUP * S].rearrange(
            "p (t n) -> p t n", t=3)

    def s(self, name):
        return self.c.sem(f"{self.name}_{name}")

    def bias(self, name, m):
        return self.vectors[:, self.biases.index(name), m:m + 1]

    def sync(self, c, sp):
        sp.wait_ge(c.sem("residual_ready"), self.index + 1)
        sp.dma_start(self.ctx_raw[:, :, :], c.a["ctx"][0, :, :, :]).then_inc(self.s("ctx_landed"), 16)
        for i, _ in enumerate(self.places):
            if i == 1:
                sp.dma_start(self.vectors[:, :, :], c.a[self.name + "_vectors"]).then_inc(self.s("vectors_landed"), 16)
                sp.dma_start(self.bv[:, :], c.a[self.name + "_bv"]).then_inc(self.s("bv_landed"), 16)
                self.sync_more(c, sp)
            if i == 6:
                sp.wait_ge(self.s("ctx_split"), 1)
                sp.dma_start(self.ctx_raw[:, :, :], c.a["ctx"][1, :, :, :]).then_inc(self.s("ctx_landed"), 16)
            wait(sp, self.s("w_split"), i - self.RAW + 1)
            sp.dma_start(self.w_raw[:, i % self.RAW, :], c.slabs[self.slabs_at + i, :, :]).then_inc(
                self.s(f"w_landed{i % self.RAW}"), 16)

        def body(b, q, more, two_more):
            if two_more:
                sp.wait_ge(self.s("ctx_split"), b + 2)
                sp.dma_start(self.ctx_raw[:, :, :], c.a["ctx"][bass.DynSlice(b + 2, 1), :, :, :].rearrange(
                    "a p k t -> p (a k) t") if not isinstance(b, int) else c.a["ctx"][b + 2, :, :, :]).then_inc(
                        self.s("ctx_landed"), 16)
        batches(sp, body)

    def sync_more(self, c, sp):
        pass

    def split_weight(self, pool, i):
        if i < 4:
            pool.wait_ge(self.s(f"w_landed{i % self.RAW}"), 16 * (i // self.RAW + 1))
            pool.tensor_copy(self.w_hi[:, self.places[i], :], self.w_raw[:, i % self.RAW, :]).then_inc(self.s("w_hi"), 1)
        pool.wait_ge(self.s("w_hi"), i + 1)
        pool.tensor_tensor(self.w_lo[:, self.places[i], :], self.w_raw[:, i % self.RAW, :],
                           self.w_hi[:, self.places[i], :], ALU.subtract).then_inc(self.s("w_split"), 1)

    def split_weight_high(self, act, i):
        if i == 4:
            act.wait_ge(self.s("w_hi"), 4)
        act.wait_ge(self.s(f"w_landed{i % self.RAW}"), 16 * (i // self.RAW + 1))
        act.activation(self.w_hi[:, self.places[i], :], self.w_raw[:, i % self.RAW, :], ACT.Copy).then_inc(
            self.s("w_hi"), 1)

    def pool(self, c, pool):
        pool.wait_ge(c.sem("residual_ready"), self.index + 1)
        self.pool_start(c, pool)
        pool.wait_ge(self.s("ctx_landed"), 16)
        pool.tensor_copy(self.ctx_hi[:, 0, :, :], self.ctx_raw[:, :, :]).then_inc(self.s("ctx_hi"), 1)
        pool.wait_ge(self.s("ctx_hi"), 1)
        pool.tensor_tensor(self.ctx_lo[:, 0, :, :], self.ctx_raw[:, :, :], self.ctx_hi[:, 0, :, :],
                           ALU.subtract).then_inc(self.s("ctx_split"), 1)
        for i in range(12):
            self.split_weight(pool, i)
        self.split_context(pool, 1, 1)
        for i in range(12, 16):
            self.split_weight(pool, i)

        def body(b, q, more, two_more):
            if two_more:
                self.split_context(pool, b + 2, q)
        batches(pool, body)

    def pool_start(self, c, pool):
        for buffer in (self.qm_hi, self.qm_lo):
            pool.memset(buffer[:, :, :].bitcast(F32), 0.0).then_inc(self.s("qm_zero"), 1)

    def split_context(self, pool, b, q):
        pool.wait_ge(self.s("ctx_hi"), b + 1)
        pool.tensor_tensor(self.ctx_lo[:, q, :, :], self.ctx_raw[:, :, :], self.ctx_hi[:, q, :, :],
                           ALU.subtract).then_inc(self.s("ctx_split"), 1)

    def split_context_high(self, act, b, q):
        act.wait_ge(self.s("ctx_landed"), 16 * (b + 1))
        if isinstance(b, int) and b < 2:
            act.wait_ge(self.s("ctx_hi"), b)
        else:
            act.wait_ge(self.s("k_units"), 4 * (b - 1))
            act.wait_ge(self.s("v_units"), 3 * (b - 1))
        act.activation(self.ctx_hi[:, q, :, :], self.ctx_raw[:, :, :], ACT.Copy).then_inc(self.s("ctx_hi"), 1)

    def pe_keys(self, pe, b, q, m):
        c = self.c
        if m == 0:
            pe.wait_ge(self.s("ctx_split"), b + 1)
        if m == 0 or self.VALUES_BANK != 7:
            wait(pe, self.s("k_lo"), 4 * b + m)
        else:
            pe.wait_ge(self.s("v_added"), 3 * b + m)
        for k in range(KD):
            w = slice(k * P, (k + 1) * P)
            mm = product(pe, [c.psum[:, 7, 0:CP]], self.w_hi[:, self.K_AT + m, w], self.w_lo[:, self.K_AT + m, w],
                         [(self.ctx_hi[:, q, k, :], self.ctx_lo[:, q, k, :])], k == 0, k == KD - 1)
        mm.then_inc(self.s("k_units"), 1)

    def pe_values(self, pe, b, q, m):
        c, (a, z) = self.c, KEY_TILES[m]
        if self.VALUES_BANK == 7:
            pe.wait_ge(self.s("k_lo"), 4 * b + m + 1)
        else:
            wait(pe, self.s("v_added"), 3 * b + m)
        for k in range(KD):
            mm = product(pe, [c.psum[0:z - a, self.VALUES_BANK, :]], self.ctx_hi[:, q, k, a:z], self.ctx_lo[:, q, k, a:z],
                         [(self.w_hi[:, self.V_AT + k, :], self.w_lo[:, self.V_AT + k, :])], k == 0, k == KD - 1)
        mm.then_inc(self.s("v_units"), 1)

    def act_keys(self, act, b, q, m):
        act.wait_ge(self.s("k_units"), 4 * b + m + 1)
        act.activation(self.k_hi[:, q, m, :], self.c.psum[:, 7, 0:CP], ACT.Identity, bias=self.bias("bk", m)).then_inc(
            self.s("k_hi"), 1)

    def dve_keys(self, dve, b, q, m):
        dve.wait_ge(self.s("k_hi"), 4 * b + m + 1)
        dve.scalar_tensor_tensor(self.k_lo[:, q, m, :], self.c.psum[:, 7, 0:CP], self.bias("bk", m),
                                 self.k_hi[:, q, m, :], ALU.add, ALU.subtract).then_inc(self.s("k_lo"), 1)

    def dve_values(self, dve, b, q, m):
        a, z = KEY_TILES[m]
        dve.wait_ge(self.s("v_units"), 3 * b + m + 1)
        dve.tensor_tensor(self.v[0:z - a, q, m, :], self.c.psum[0:z - a, self.VALUES_BANK, :], self.bv[0:z - a, :],
                          ALU.add).then_inc(self.s("v_added"), 1)

    def pe_project(self, pe, units, freed, moving):
        c = self.c
        for m in range(KD):
            bank = 2 * (m % 2)
            wait(pe, self.s(freed), m - 1)
            for k in range(KD):
                w = slice(k * P, (k + 1) * P)
                mm = product(pe, [c.psum[:, bank + h, 0:HALF] for h in range(2)], self.w_hi[:, self.Q_AT + m, w],
                             self.w_lo[:, self.Q_AT + m, w],
                             [tuple(x[:, k, h * HALF:(h + 1) * HALF] for x in moving) for h in range(2)],
                             k == 0, k == KD - 1)
            mm.then_inc(self.s(units), 1)

    def pe(self, c, pe):
        ln_pe(c, pe, self)
        pe.wait_ge(self.s("w_split"), 8)
        for m in range(KD):
            self.pe_keys(pe, 0, 0, m)
            if m < 3:
                self.pe_values(pe, 0, 0, m)
        for h in range(2):
            pe.wait_ge(c.sem("ln_xn_lo"), 2 * self.index + h + 1)
        pe.wait_ge(self.s("w_split"), 12)
        self.pe_project(pe, "q_units", "q_copied", (c.xn_hi, c.xn_lo))
        self.pe_start(c, pe)
        batches(pe, lambda b, q, more, two_more: self.pe_batch(c, pe, b, q, more))
        self.pe_after_batches(c, pe)
        pe.wait_ge(self.s("o_lo"), B * KD)
        pe.wait_ge(self.s("w_split"), 16)
        self.pe_project(pe, "out_units", "out_read", (c.xn_hi, c.xn_lo))
        self.pe_finish(c, pe)

    def pe_start(self, c, pe):
        pe.wait_ge(self.s("q_copied"), KD)
        self.pe_first_scores(c, pe)

    def pe_first_scores(self, c, pe):
        self.pe_scores(c, pe, 0, 0, 0)

    def pe_after_batches(self, c, pe):
        pass

    def pe_finish(self, c, pe):
        pass

    def act(self, c, act):
        ln_act(c, act, self)
        for i in range(4, 8):
            self.split_weight_high(act, i)
        act.wait_ge(self.s("vectors_landed"), 16)
        for m in range(KD):
            self.act_keys(act, 0, 0, m)
            self.split_weight_high(act, 8 + m)
        self.split_context_high(act, 1, 1)
        for m in range(KD):
            bank = 2 * (m % 2)
            act.wait_ge(self.s("q_units"), m + 1)
            act.activation(c.xn[:, m, :].rearrange("p (h t) -> p h t", h=2), c.psum[:, bank:bank + 2, 0:HALF],
                           ACT.Identity, bias=self.bias("bq", m)).then_inc(self.s("q_copied"), 1)
        for i in range(12, 16):
            self.split_weight_high(act, i)
        self.act_start(c, act)
        self.act_before_batches(c, act)
        batches(act, lambda b, q, more, two_more: self.act_batch(c, act, b, q, more, two_more))
        self.act_finish(c, act)

    def act_start(self, c, act):
        act.wait_ge(self.s("qm_zero"), 2)
        act.wait_ge(self.s("q_copied"), KD)
        self.act_queries(c, act, 0)

    def act_finish(self, c, act):
        pass

    def act_queries(self, c, act, b):
        for g in range(GROUP):
            rows = slice(g * HD, (g + 1) * HD)
            act.activation(self.qm_hi[rows, g:HEADS:GROUP, :], c.xn[rows, :, tokens_of(b)], ACT.Copy).then_inc(
                self.s("qm_hi"), 1)

    def dve_queries(self, c, dve, b):
        for g in range(GROUP):
            rows = slice(g * HD, (g + 1) * HD)
            dve.wait_ge(self.s("qm_hi"), b * 4 + g + 1)
            dve.tensor_tensor(self.qm_lo[rows, g:HEADS:GROUP, :], c.xn[rows, :, tokens_of(b)],
                              self.qm_hi[rows, g:HEADS:GROUP, :], ALU.subtract).then_inc(self.s("qm_lo"), 1)

    def dve(self, c, dve):
        ln_dve(c, dve, self)
        dve.wait_ge(self.s("vectors_landed"), 16)
        dve.wait_ge(self.s("bv_landed"), 16)
        for m in range(KD):
            self.dve_keys(dve, 0, 0, m)
            if m < 3:
                self.dve_values(dve, 0, 0, m)
        self.dve_start(c, dve)
        self.dve_before_batches(c, dve)
        batches(dve, lambda b, q, more, two_more: self.dve_batch(c, dve, b, q, more))
        self.dve_finish(c, dve)
        dve.nop().then_inc(c.sem("residual_ready"), 1)

    def dve_start(self, c, dve):
        dve.wait_ge(self.s("qm_zero"), 2)
        self.dve_queries(c, dve, 0)

    def dve_finish(self, c, dve):
        for m in range(KD):
            bank = 2 * (m % 2)
            dve.wait_ge(self.s("out_units"), m + 1)
            into = c.residual[:, m, :].rearrange("p (h t) -> p h t", h=2)
            dve.scalar_tensor_tensor(into, c.psum[:, bank:bank + 2, 0:HALF], self.bias("bo", m), into,
                                     ALU.add, ALU.add).then_inc(self.s("out_read"), 1)
        dve.wait_ge(self.s("out_read"), KD)

    def pe_batch(self, c, pe, b, q, more):
        turned = self.turned(c)
        for m in range(KD):
            i = b * 4 + m
            if more:
                self.pe_keys(pe, b + 1, 1 - q, m)
            if m < 3:
                self.pe_scores(c, pe, b, q, m + 1)
            elif more:
                self.pe_scores(c, pe, b + 1, 1 - q, 0)
            pe.wait_ge(self.s("normalised"), i * GROUP + GROUP)
            wait(pe, self.s("turned_01"), i)
            wait(pe, self.s("turned_2"), i)
            for g in range(GROUP):
                for t, (a, z) in enumerate(KEY_TILES):
                    mm = pe.transpose(c.psum[0:z - a, 4 + t, g * S:(g + 1) * S], self.probs[:, g, a:z],
                                      c.identity[0:S, 0:S])
            mm.then_inc(self.s("t_units"), 1)
            if more and m < 3:
                self.pe_values(pe, b + 1, 1 - q, m)
            pe.wait_ge(self.s("turned_01"), i + 1)
            pe.wait_ge(self.s("turned_2"), i + 1)
            if m == 0:
                pe.wait_ge(self.s("v_added"), b * 3 + 3)
            wait(pe, self.s("o_lo"), i - 1)
            for g in range(GROUP):
                head = slice((m * GROUP + g) * HD, (m * GROUP + g + 1) * HD)
                for t, (a, z) in enumerate(KEY_TILES):
                    mm = pe.matmul(c.psum[g * HD:(g + 1) * HD, 4 + m % 2, 400:400 + S], self.v[0:z - a, q, t, head],
                                   turned[0:z - a, t, g * S:(g + 1) * S], start=t == 0, stop=t == 2)
            mm.then_inc(self.s("pv_units"), 1)

    def pe_scores(self, c, pe, b, q, m):
        i = b * 4 + m
        if m == 0:
            pe.wait_ge(self.s("qm_hi"), b * 4 + 4)
            pe.wait_ge(self.s("qm_lo"), b * 4 + 4)
        pe.wait_ge(self.s("k_lo"), i + 1)
        wait(pe, self.s("exps"), i * GROUP)
        for g in range(GROUP):
            mm = product(pe, [c.psum[0:S, g, 0:CP]], self.qm_hi[:, m * GROUP + g, :], self.qm_lo[:, m * GROUP + g, :],
                         [(self.k_hi[:, q, m, :], self.k_lo[:, q, m, :])], True, True)
        mm.then_inc(self.s("s_units"), 1)

    def act_exps(self, c, act, i):
        act.wait_ge(self.s("shifts"), i + 1)
        wait(act, self.s("t_units"), i)
        for g in range(GROUP):
            act.activation(self.probs[:, g, :], c.psum[0:S, g, 0:C], ACT.Exp, bias=self.shift[:, g:g + 1],
                           scale=self.SCALE, accum_out=self.total[:, g:g + 1]).then_inc(self.s("exps"), 1)

    def act_before_batches(self, c, act):
        self.act_exps(c, act, 0)

    def dve_before_batches(self, c, dve):
        self.dve_maxima(c, dve, 0)

    def act_batch(self, c, act, b, q, more, two_more):
        turned = self.turned(c)
        for m in range(KD):
            i = b * 4 + m
            if more:
                self.act_keys(act, b + 1, 1 - q, m)
            if two_more and m == 1:
                self.split_context_high(act, b + 2, q)
            act.wait_ge(self.s("t_units"), i + 1)
            wait(act, self.s("pv_units"), i)
            act.activation(turned[:, 0:2, :], c.psum[:, 4:6, 0:GROUP * S], ACT.Copy).then_inc(self.s("turned_01"), 1)
            if more and m == 2:
                act.wait_ge(self.s("s_units"), b * 4 + 4)
                self.act_queries(c, act, b + 1)
            if m < 3 or more:
                self.act_exps(c, act, i + 1)
            act.wait_ge(self.s("pv_units"), i + 1)
            act.activation(c.xn_hi[:, m, tokens_of(b)], c.psum[:, 4 + m % 2, 400:400 + S], ACT.Copy).then_inc(
                self.s("o_hi"), 1)

    def dve_maxima(self, c, dve, i):
        dve.wait_ge(self.s("s_units"), i + 1)
        dve.tensor_reduce(self.highest[:, :], c.psum[0:S, 0:GROUP, 0:C], AX.X, ALU.max).then_inc(self.s("maxima"), 1)
        dve.wait_ge(self.s("maxima"), i + 1)
        dve.tensor_scalar(self.shift[:, :], self.highest[:, :], -self.SCALE, None, ALU.mult).then_inc(self.s("shifts"), 1)

    def dve_batch(self, c, dve, b, q, more):
        turned = self.turned(c)
        for m in range(KD):
            i = b * 4 + m
            dve.wait_ge(self.s("exps"), i * GROUP + GROUP)
            dve.reciprocal(self.inverse[:, :], self.total[:, :]).then_inc(self.s("inverses"), 1)
            dve.wait_ge(self.s("inverses"), i + 1)
            for g in range(GROUP):
                dve.tensor_scalar(self.probs[:, g, :], self.probs[:, g, :], self.inverse[:, g:g + 1], None,
                                  ALU.mult).then_inc(self.s("normalised"), 1)
            if more:
                self.dve_keys(dve, b + 1, 1 - q, m)
            n = KEY_TILES[2][1] - KEY_TILES[2][0]
            dve.wait_ge(self.s("t_units"), i + 1)
            wait(dve, self.s("pv_units"), i)
            dve.tensor_copy(turned[0:n, 2, :], c.psum[0:n, 6, 0:GROUP * S]).then_inc(self.s("turned_2"), 1)
            if more and m == 2:
                self.dve_queries(c, dve, b + 1)
            if m < 3 or more:
                self.dve_maxima(c, dve, i + 1)
            if more and m < 3:
                self.dve_values(dve, b + 1, 1 - q, m)
            dve.wait_ge(self.s("o_hi"), i + 1)
            dve.tensor_tensor(c.xn_lo[:, m, tokens_of(b)], c.psum[:, 4 + m % 2, 400:400 + S],
                              c.xn_hi[:, m, tokens_of(b)], ALU.subtract).then_inc(self.s("o_lo"), 1)



class BoundedAttention(Attention):
    BOUND = 50.0
    EPS = 1e-8
    SCALE_MAX = 0.3

    def __init__(self, name, index, slabs_at):
        super().__init__(name, index, slabs_at)
        self.biases = ["bq", "bk", "bo", "gamma", "beta"]

    def own_buffers(self, c, own):
        n = self.name
        self.qm_hi, self.qm_lo = (c.sb(own, n + x, [P, HEADS, S], F32R) for x in ("_qm_hi", "_qm_lo"))
        self.clipped = c.sb(own, n + "_clipped", [P, 3, GROUP * S])
        self.mask = c.sb(own, n + "_mask", [P, 3, B], I32)
        self.key_scale, self.key_shift = (c.sb(own, n + x, [P, 3, B]) for x in ("_key_scale", "_key_shift"))
        self.out_scale = c.sb(own, n + "_out_scale", [P, 1])
        self.norm = c.sb(own, n + "_norm", [P, 2, S])
        self.o = c.sb(own, n + "_o", [P, 2, S])

    def exps(self, c, m):
        return c.ln_squares[:, :, :].rearrange("p k t -> p (k t)")[:, m % 2 * 1200:m % 2 * 1200 + 1200].rearrange(
            "p (t n) -> p t n", t=3)

    def sync_more(self, c, sp):
        sp.dma_start(self.mask[:, :, :], c.a["context_mask"]).then_inc(self.s("mask_landed"), 16)
        sp.dma_start(self.out_scale[:, :], c.a["out_scale"]).then_inc(self.s("out_scale_landed"), 16)

    def pe_batch(self, c, pe, b, q, more):
        for m in range(KD):
            i = b * 4 + m
            if more:
                self.pe_keys(pe, b + 1, 1 - q, m)
            if m < 3:
                self.pe_scores(c, pe, b, q, m + 1)
            elif more:
                self.pe_scores(c, pe, b + 1, 1 - q, 0)
            if more and m < 3:
                self.pe_values(pe, b + 1, 1 - q, m)
            pe.wait_ge(self.s("exps"), i * 3 + 3)
            if m == 0:
                pe.wait_ge(self.s("v_added"), b * 3 + 3)
            wait(pe, self.s("o"), i)
            exps = self.exps(c, m)
            for g in range(GROUP):
                head = slice((m * GROUP + g) * HD, (m * GROUP + g + 1) * HD)
                for x in range(2):
                    for t, (a, z) in enumerate(KEY_TILES):
                        at = m % 2 * 200 + x * S
                        mm = pe.matmul(c.psum[g * HD:(g + 1) * HD, 6, at:at + S],
                                       c.ones[0:z - a, 0:HD] if x else self.v[0:z - a, q, t, head],
                                       exps[0:z - a, t, g * S:(g + 1) * S], start=t == 0, stop=t == 2)
            mm.then_inc(self.s("pv_units"), 1)

    def pe_scores(self, c, pe, b, q, m):
        i = b * 4 + m
        if m == 0:
            pe.wait_ge(self.s("qm_hi"), b * 4 + 4)
            pe.wait_ge(self.s("qm_lo"), b * 4 + 4)
        pe.wait_ge(self.s("k_lo"), i + 1)
        wait(pe, self.s("clipped"), (i - 1) * 2)
        for t, (a, z) in enumerate(KEY_TILES):
            mm = product(pe, [c.psum[0:z - a, m % 2 * 3 + t, 0:GROUP * S]], self.k_hi[:, q, m, a:z], self.k_lo[:, q, m, a:z],
                         [tuple(x[:, m * GROUP:(m + 1) * GROUP, :].rearrange("p h s -> p (h s)")
                                for x in (self.qm_hi, self.qm_lo))], True, True)
        mm.then_inc(self.s("s_units"), 1)

    def act_exps(self, c, act, b, m):
        i = b * 4 + m
        act.wait_ge(self.s("clipped"), i * 2 + 2)
        wait(act, self.s("pv_units"), i - 1)
        c.apart(act)
        for t, (a, z) in enumerate(KEY_TILES):
            scale, shift = (x[0:z - a, t, b:b + 1] if isinstance(b, int) else x[0:z - a, t, bass.DynSlice(b, 1)]
                            for x in (self.key_scale, self.key_shift))
            act.activation(self.exps(c, m)[0:z - a, t, :], self.clipped[0:z - a, t, :], ACT.Exp, bias=shift,
                           scale=scale).then_inc(self.s("exps"), 1)

    def act_batch(self, c, act, b, q, more, two_more):
        for m in range(KD):
            i = b * 4 + m
            if more:
                self.act_keys(act, b + 1, 1 - q, m)
            if more and m == 2:
                act.wait_ge(self.s("s_units"), b * 4 + 4)
                self.act_queries(c, act, b + 1)
            if two_more and m == 1:
                self.split_context_high(act, b + 2, q)
            if m < 3:
                self.act_exps(c, act, b, m + 1)
            elif more:
                self.act_exps(c, act, b + 1, 0)
            act.wait_ge(self.s("o"), i + 1)
            act.activation(c.xn_hi[:, m, tokens_of(b)], self.o[:, m % 2, :], ACT.Copy).then_inc(self.s("o_hi"), 1)

    def dve_clip(self, c, dve, i, m):
        bound = self.BOUND / self.SCALE
        bank, n = m % 2 * 3, KEY_TILES[2][1] - KEY_TILES[2][0]
        dve.wait_ge(self.s("s_units"), i + 1)
        wait(dve, self.s("exps"), i * 3)
        dve.tensor_scalar(self.clipped[:, 0:2, :], c.psum[:, bank:bank + 2, 0:GROUP * S], -bound, bound,
                          ALU.max, ALU.min).then_inc(self.s("clipped"), 1)
        dve.tensor_scalar(self.clipped[0:n, 2, :], c.psum[0:n, bank + 2, 0:GROUP * S], -bound, bound,
                          ALU.max, ALU.min).then_inc(self.s("clipped"), 1)

    def dve_batch(self, c, dve, b, q, more):
        def low(m, i):
            dve.wait_ge(self.s("o_hi"), i + 1)
            dve.tensor_tensor(c.xn_lo[:, m, tokens_of(b)], self.o[:, m % 2, :], c.xn_hi[:, m, tokens_of(b)],
                              ALU.subtract).then_inc(self.s("o_lo"), 1)
        for m in range(KD):
            i = b * 4 + m
            if more:
                self.dve_keys(dve, b + 1, 1 - q, m)
            if m < 3 or more:
                self.dve_clip(c, dve, i + 1, (m + 1) % 4)
            if more and m < 3:
                self.dve_values(dve, b + 1, 1 - q, m)
            if more and m == 2:
                self.dve_queries(c, dve, b + 1)
            if m:
                low(m - 1, i - 1)
            at = m % 2 * 200
            weighted, total = c.psum[:, 6, at:at + S], c.psum[:, 6, at + S:at + 2 * S]
            n, step = self.norm, self.s("norm_steps")
            dve.wait_ge(self.s("pv_units"), i + 1)
            dve.tensor_scalar(n[:, 0, :], total, self.EPS, None, ALU.mult).then_inc(step, 1)
            dve.wait_ge(step, i * 3 + 1)
            dve.tensor_tensor(n[:, 0, :], n[:, 0, :], total, ALU.add).then_inc(step, 1)
            dve.wait_ge(step, i * 3 + 2)
            dve.reciprocal(n[:, 1, :], n[:, 0, :]).then_inc(step, 1)
            dve.wait_ge(step, i * 3 + 3)
            wait(dve, self.s("o_lo"), i - 1)
            dve.tensor_tensor(self.o[:, m % 2, :], weighted, n[:, 1, :], ALU.mult).then_inc(self.s("o"), 1)
        low(KD - 1, b * 4 + KD - 1)

    def act_before_batches(self, c, act):
        self.act_exps(c, act, 0, 0)

    def dve_before_batches(self, c, dve):
        self.dve_clip(c, dve, 0, 0)

    def dve_start(self, c, dve):
        dve.wait_ge(self.s("mask_landed"), 16)
        dve.wait_ge(self.s("out_scale_landed"), 16)
        step = self.s("mask_steps")
        dve.tensor_scalar(self.key_scale[:, :, :], self.mask[:, :, :], 0.5, None, ALU.is_gt).then_inc(step, 1)
        dve.tensor_scalar(self.out_scale[:, :], self.out_scale[:, :], 0.0, self.SCALE_MAX, ALU.max,
                          ALU.min).then_inc(step, 1)
        dve.wait_ge(step, 1)
        dve.tensor_scalar(self.key_shift[:, :, :], self.key_scale[:, :, :], self.BOUND, -self.BOUND, ALU.mult,
                          ALU.add).then_inc(step, 1)
        dve.wait_ge(step, 3)
        dve.tensor_scalar(self.key_scale[:, :, :], self.key_scale[:, :, :], self.SCALE, None, ALU.mult).then_inc(
            step, 1)
        dve.wait_ge(step, 4)
        super().dve_start(c, dve)

    def pe_finish(self, c, pe):
        for h in range(2):
            pe.wait_ge(self.s("out_read"), KD)
            for k in range(KD):
                mm = pe.matmul(c.psum[:, 4 + h, 0:HALF], c.mean_matrix[:, :], c.xn[:, k, h * HALF:(h + 1) * HALF],
                               start=k == 0, stop=k == KD - 1)
            mm.then_inc(self.s("mean"), 1)
        for h in range(2):
            pe.wait_ge(self.s("squares"), h + 1)
            for k in range(KD):
                mm = pe.matmul(c.psum[:, 6 + h, 0:HALF], c.mean_matrix[:, :],
                               c.ln_squares[:, k, h * HALF:(h + 1) * HALF], start=k == 0, stop=k == KD - 1)
            mm.then_inc(self.s("variance"), 1)

    def act_finish(self, c, act):
        for h in range(2):
            t = slice(h * HALF, (h + 1) * HALF)
            act.wait_ge(self.s("centered"), h + 1)
            act.activation(c.ln_squares[:, :, t], c.xn[:, :, t], ACT.Square).then_inc(self.s("squares"), 1)
        for h in range(2):
            act.wait_ge(self.s("variance"), h + 1)
            act.activation(c.ln_std[:, h * HALF:(h + 1) * HALF], c.psum[:, 6 + h, 0:HALF], ACT.Sqrt,
                           bias=c.eps[:, 0:1]).then_inc(self.s("std"), 1)

    def dve_finish(self, c, dve):
        for m in range(KD):
            bank = 2 * (m % 2)
            dve.wait_ge(self.s("out_units"), m + 1)
            dve.tensor_scalar(c.xn[:, m, :].rearrange("p (h t) -> p h t", h=2), c.psum[:, bank:bank + 2, 0:HALF],
                              self.bias("bo", m), self.out_scale[:, 0:1], ALU.add, ALU.mult).then_inc(
                                  self.s("out_read"), 1)
        dve.wait_ge(self.s("out_read"), KD)
        for h in range(2):
            t = slice(h * HALF, (h + 1) * HALF)
            dve.wait_ge(self.s("mean"), h + 1)
            dve.tensor_tensor(c.xn[:, :, t], c.xn[:, :, t], c.psum[:, 4 + h, 0:HALF].unsqueeze(1).broadcast_to(
                [P, KD, HALF]), ALU.subtract).then_inc(self.s("centered"), 1)
        for h in range(2):
            t = slice(h * HALF, (h + 1) * HALF)
            dve.wait_ge(self.s("std"), h + 1)
            dve.reciprocal(c.ln_rstd[:, t], c.ln_std[:, t]).then_inc(self.s("rstd"), 1)
            dve.wait_ge(self.s("rstd"), h + 1)
            dve.tensor_tensor(c.xn[:, :, t], c.xn[:, :, t], c.ln_rstd[:, t].unsqueeze(1).broadcast_to([P, KD, HALF]),
                              ALU.mult).then_inc(self.s("delta"), 1)
        dve.wait_ge(self.s("delta"), 2)
        for m in range(KD):
            dve.tensor_scalar(c.xn[:, m, :], c.xn[:, m, :], self.bias("gamma", m), self.bias("beta", m), ALU.mult,
                              ALU.add).then_inc(self.s("delta"), 1)
        for m in range(KD):
            dve.wait_ge(self.s("delta"), 3 + m)
            dve.tensor_tensor(c.residual[:, m, :], c.residual[:, m, :], c.xn[:, m, :], ALU.add).then_inc(
                self.s("delta"), 1)
        dve.wait_ge(self.s("delta"), 2 + 2 * KD)



class LinearAttention(Attention):
    EPS = 1e-8
    PAIRS = HEADS // 2
    VALUES_BANK = 6

    def own_buffers(self, c, own):
        n = self.name
        self.maps = c.sb(own, n + "_maps", [P, 4, P])
        self.maps_hi, self.maps_lo = (c.sb(own, n + x, [P, 4, P], F32R) for x in ("_maps_hi", "_maps_lo"))
        self.qf_high = c.sb(own, n + "_qf_high", [P, self.PAIRS // 2, T])
        self.mask = c.sb(own, n + "_mask", [P, 3, B])
        self.norm = c.sb(own, n + "_norm", [P, 2, S])
        self.o = c.sb(own, n + "_o", [P, S])

    def query_features(self, c, pair):
        return c.xn[:, pair, :] if pair < KD else self.qf_high[:, pair - KD, :]

    def key_features(self, c, m):
        return c.ln_squares[:, :, :].rearrange("p k t -> p (k t)")[:, m % 2 * 768:m % 2 * 768 + 768].rearrange(
            "p (t f) -> p t f", t=3)

    def sums(self, c, m, x):
        at = 1536 + (m % 2 * 2 + x) * 384
        return c.ln_squares[:, :, :].rearrange("p k t -> p (k t)")[:, at:at + 384]

    def act_before_batches(self, c, act):
        pass

    def dve_before_batches(self, c, dve):
        self.dve_features(c, dve, 0, 0)

    def sync_more(self, c, sp):
        sp.dma_start(self.mask[:, :, :], c.a["key_mask"]).then_inc(self.s("mask_landed"), 16)
        sp.dma_start(self.maps[:, :, :], c.a["feature_maps"]).then_inc(self.s("maps_landed"), 16)

    def pool_start(self, c, pool):
        pass

    def act_start(self, c, act):
        act.wait_ge(self.s("maps_landed"), 16)
        act.activation(self.maps_hi[:, :, :], self.maps[:, :, :], ACT.Copy).then_inc(self.s("maps_hi"), 1)
        act.wait_ge(self.s("q_copied"), KD)
        act.activation(c.xn_hi[:, :, :], c.xn[:, :, :], ACT.Copy).then_inc(self.s("q_hi"), 1)
        for pair in range(self.PAIRS):
            bank = 2 * (pair % 2)
            act.wait_ge(self.s("qf_units"), pair + 1)
            if pair == 0:
                act.wait_ge(self.s("q_lo"), 1)
            act.activation(self.query_features(c, pair).rearrange("p (h t) -> p h t", h=2),
                           c.psum[:, bank:bank + 2, 0:HALF], ACT.Relu).then_inc(self.s("qf_copied"), 1)

    def dve_start(self, c, dve):
        dve.wait_ge(self.s("mask_landed"), 16)
        dve.wait_ge(self.s("maps_hi"), 1)
        dve.tensor_tensor(self.maps_lo[:, :, :], self.maps[:, :, :], self.maps_hi[:, :, :], ALU.subtract).then_inc(
            self.s("maps_lo"), 1)
        dve.wait_ge(self.s("q_hi"), 1)
        dve.tensor_tensor(c.xn_lo[:, :, :], c.xn[:, :, :], c.xn_hi[:, :, :], ALU.subtract).then_inc(self.s("q_lo"), 1)
        for m in range(2):
            for x in range(2):
                dve.memset(self.sums(c, m, x), 0.0).then_inc(self.s("sums_zero"), 1)
        dve.wait_ge(self.s("sums_zero"), 4)

    def pe_start(self, c, pe):
        pe.wait_ge(self.s("maps_lo"), 1)
        pe.wait_ge(self.s("q_lo"), 1)
        for pair in range(self.PAIRS):
            bank = 2 * (pair % 2)
            wait(pe, self.s("qf_copied"), pair - 1)
            mm = product(pe, [c.psum[:, bank + h, 0:HALF] for h in range(2)], self.maps_hi[:, pair % 2, :],
                         self.maps_lo[:, pair % 2, :],
                         [tuple(x[:, pair // 2, h * HALF:(h + 1) * HALF] for x in (c.xn_hi, c.xn_lo)) for h in range(2)],
                         True, True)
            mm.then_inc(self.s("qf_units"), 1)
        pe.wait_ge(self.s("qf_copied"), self.PAIRS)
        self.pe_key_features(c, pe, 0, 0, 0)

    def pe_key_features(self, c, pe, b, q, m):
        i = b * 4 + m
        pe.wait_ge(self.s("k_lo"), i + 1)
        wait(pe, self.s("kf"), i * 3)
        for t, (a, z) in enumerate(KEY_TILES):
            mm = product(pe, [c.psum[0:z - a, t, 0:2 * P]], self.k_hi[:, q, m, a:z], self.k_lo[:, q, m, a:z],
                         [tuple(x[:, 2:4, :].rearrange("p a n -> p (a n)") for x in (self.maps_hi, self.maps_lo))],
                         True, True)
        mm.then_inc(self.s("kf_units"), 1)

    def pe_batch(self, c, pe, b, q, more):
        for m in range(KD):
            i = b * 4 + m
            if more:
                self.pe_keys(pe, b + 1, 1 - q, m)
            if m < 3:
                self.pe_key_features(c, pe, b, q, m + 1)
            elif more:
                self.pe_key_features(c, pe, b + 1, 1 - q, 0)
            if more and m < 3:
                self.pe_values(pe, b + 1, 1 - q, m)
            if m == 0:
                pe.wait_ge(self.s("v_added"), b * 3 + 3)
            pe.wait_ge(self.s("kf"), i * 3 + 3)
            wait(pe, self.s("sums"), i * 4)
            kf = self.key_features(c, m)
            for p in range(2):
                for x in range(2):
                    at = p * 96 + x * 64
                    n = 32 if x else 64
                    head = (m * 2 + p) * 64
                    for t, (a, z) in enumerate(KEY_TILES):
                        mm = pe.matmul(c.psum[:, 3, at:at + n], kf[0:z - a, t, p * P:(p + 1) * P],
                                       c.ones[0:z - a, 0:32] if x else self.v[0:z - a, q, t, head:head + 64],
                                       start=t == 0, stop=t == 2)
            mm.then_inc(self.s("kv_units"), 1)
            if m:
                self.pe_output(c, pe, b, m - 1)
            elif not isinstance(b, int) or b:
                self.pe_output(c, pe, b - 1, KD - 1)

    def pe_output(self, c, pe, b, m):
        i = b * 4 + m
        pe.wait_ge(self.s("sums"), i * 4 + 4)
        wait(pe, self.s("o"), i - 1)
        for x in range(2):
            for p in range(2):
                mm = pe.matmul(c.psum[:, 4 + m % 2, x * S:(x + 1) * S], self.sums(c, m, x)[:, p * P:(p + 1) * P],
                               self.query_features(c, m * 2 + p)[:, tokens_of(b)], start=p == 0, stop=p == 1)
        mm.then_inc(self.s("o_units"), 1)

    def act_batch(self, c, act, b, q, more, two_more):
        for m in range(KD):
            i = b * 4 + m
            if more:
                self.act_keys(act, b + 1, 1 - q, m)
            if two_more and m == 1:
                self.split_context_high(act, b + 2, q)
            act.wait_ge(self.s("kv_units"), i + 1)
            wait(act, self.s("o_units"), i - 1)
            for x in range(2):
                for head in range(2):
                    rows = slice(head * 64, head * 64 + 64)
                    dst = self.sums(c, m, x)[rows, :].rearrange("f (p e) -> f p e", p=2)[:, :, head * 32:head * 32 + 32]
                    at = 64 if x else head * 32
                    src = c.psum[rows, 3, 0:192].rearrange("f (p e) -> f p e", p=2)[:, :, at:at + 32]
                    act.activation(dst, src, ACT.Copy).then_inc(self.s("sums"), 1)
            if m:
                self.act_output(c, act, b, m - 1)
            elif not isinstance(b, int) or b:
                self.act_output(c, act, b - 1, KD - 1)

    def act_output(self, c, act, b, m):
        act.wait_ge(self.s("o"), b * 4 + m + 1)
        act.activation(c.xn_hi[:, m, tokens_of(b)], self.o[:, :], ACT.Copy).then_inc(self.s("o_hi"), 1)

    def dve_features(self, c, dve, b, m):
        i = b * 4 + m
        dve.wait_ge(self.s("kf_units"), i + 1)
        wait(dve, self.s("kv_units"), i - 1)
        for t, (a, z) in enumerate(KEY_TILES):
            mask = (self.mask[0:z - a, t, b:b + 1] if isinstance(b, int)
                    else self.mask[0:z - a, t, bass.DynSlice(b, 1)])
            dve.tensor_scalar(self.key_features(c, m)[0:z - a, t, :], c.psum[0:z - a, t, 0:2 * P], 0.0, mask,
                              ALU.max, ALU.mult).then_inc(self.s("kf"), 1)

    def dve_batch(self, c, dve, b, q, more):
        for m in range(KD):
            if more:
                self.dve_keys(dve, b + 1, 1 - q, m)
            if m < 3:
                self.dve_features(c, dve, b, m + 1)
            elif more:
                self.dve_features(c, dve, b + 1, 0)
            if more and m < 3:
                self.dve_values(dve, b + 1, 1 - q, m)
            if m:
                self.dve_output(c, dve, b, m - 1)
            elif not isinstance(b, int) or b:
                self.dve_output(c, dve, b - 1, KD - 1)

    def dve_output(self, c, dve, b, m):
        i, step, bank = b * 4 + m, self.s("norm_steps"), 4 + m % 2
        dve.wait_ge(self.s("o_units"), i + 1)
        dve.tensor_scalar(self.norm[:, 0, :], c.psum[:, bank, S:2 * S], self.EPS, None, ALU.add).then_inc(step, 1)
        dve.wait_ge(step, i * 2 + 1)
        dve.reciprocal(self.norm[:, 1, :], self.norm[:, 0, :]).then_inc(step, 1)
        dve.wait_ge(step, i * 2 + 2)
        wait(dve, self.s("o_hi"), i)
        wait(dve, self.s("o_lo"), i)
        dve.tensor_tensor(self.o[:, :], c.psum[:, bank, 0:S], self.norm[:, 1, :], ALU.mult).then_inc(self.s("o"), 1)
        dve.wait_ge(self.s("o_hi"), i + 1)
        dve.tensor_tensor(c.xn_lo[:, m, tokens_of(b)], self.o[:, :], c.xn_hi[:, m, tokens_of(b)],
                          ALU.subtract).then_inc(self.s("o_lo"), 1)

    def pe_after_batches(self, c, pe):
        self.pe_output(c, pe, B - 1, KD - 1)

    def act_finish(self, c, act):
        self.act_output(c, act, B - 1, KD - 1)

    def dve_finish(self, c, dve):
        self.dve_output(c, dve, B - 1, KD - 1)
        super().dve_finish(c, dve)



class BitFfn:
    INNER = 2048
    KI = INNER // P
    CHUNKS = INNER // 512
    LEVELS = 127.0
    EPS = 1e-5
    ROUND = 1.5 * 2.0 ** 23

    def __init__(self, name, index):
        self.name, self.index = name, index

    def s(self, name):
        return self.c.sem(f"{self.name}_{name}")

    def buffers(self, c, own):
        n, self.c = self.name, c
        self.w_raw = [c.sb(own, f"{n}_w{x}_raw", [P, KD * self.INNER]) for x in (1, 2)]
        self.w = [c.sb(own, f"{n}_w{x}", [P, KD * self.INNER], BF16) for x in (1, 2)]
        self.sums = c.sb(own, n + "_sums", [P, 2, KD])
        self.sum = c.sb(own, n + "_sum", [P, 2])
        self.step_w = c.sb(own, n + "_step_w", [P, 2])
        self.border = c.sb(own, n + "_border", [P, 2, 2])
        self.stage = c.sb(own, n + "_stage", [P, KD, S])
        self.rows = c.sb(own, n + "_rows", [S, D])
        self.x_whole = c.sb(own, n + "_x_whole", [S, D], BF16)
        self.x_turned = c.sb(own, n + "_x_turned", [P, KD, S], BF16)
        self.inner = c.sb(own, n + "_inner", [S, self.INNER])
        self.inner_whole = c.sb(own, n + "_inner_whole", [S, self.INNER], BF16)
        self.inner_turned = c.sb(own, n + "_inner_turned", [P, self.KI, S], BF16)
        self.out = c.sb(own, n + "_out", [S, D])
        self.identity = c.sb(own, n + "_identity", [P, P], BF16)
        self.x_max, self.x_scale, self.x_step, self.h_max, self.h_scale, self.h_step = (
            c.sb(own, n + x, [S, B]) for x in ("_x_max", "_x_scale", "_x_step", "_h_max", "_h_scale", "_h_step"))

    def one(self, buffer, b):
        return buffer[:, b:b + 1] if isinstance(b, int) else buffer[:, bass.DynSlice(b, 1)]

    def schedule(self, engine, first, body):
        first()
        body(0, False, True, True)
        body(1, True, True, True)
        with engine.Fori(2, B - 1) as i:
            body(i, True, True, True)
        body(B - 1, True, True, False)
        body(B, True, False, False)

    def sync(self, c, sp):
        sp.wait_ge(c.sem("residual_ready"), self.index + 1)
        for x in range(2):
            for k in range(KD):
                cut = slice(k * self.INNER, (k + 1) * self.INNER)
                sp.dma_start(self.w_raw[x][:, cut], c.a[f"bit_w{x + 1}"][:, cut]).then_inc(self.s(f"w{x}{k}_landed"), 16)

    def pool(self, c, pool):
        pool.wait_ge(c.sem("residual_ready"), self.index + 1)
        pool.wait_ge(self.s("borders"), 4)
        self.whole_weight(pool, 1)

    def whole_weight(self, engine, x):
        for k in range(KD):
            cut = slice(k * self.INNER, (k + 1) * self.INNER)
            raw, whole = self.w_raw[x][:, cut], self.w[x][:, cut]
            engine.tensor_scalar(whole, raw, self.border[:, 1, x:x + 1], None, ALU.is_lt).then_inc(self.s(f"w{x}_below"), 1)
            if x:
                engine.wait_ge(self.s("w1_below"), k + 1)
                engine.tensor_scalar(raw, raw, self.border[:, 0, x:x + 1], None, ALU.is_gt).then_inc(self.s("w1_above"), 1)
                engine.wait_ge(self.s("w1_above"), k + 1)
                engine.tensor_tensor(whole, raw, whole, ALU.subtract).then_inc(self.s(f"w{x}_whole"), 1)
            else:
                engine.wait_ge(self.s("w0_below"), k + 1)
                engine.scalar_tensor_tensor(whole, raw, self.border[:, 0, x:x + 1], whole, ALU.is_gt,
                                            ALU.subtract).then_inc(self.s(f"w{x}_whole"), 1)

    def pe(self, c, pe):
        ln_pe(c, pe, self)
        pe.wait_ge(self.s("sum"), 2)
        pe.matmul(c.psum[:, 4, 0:2], c.ones[:, :], self.sum[:, :], start=True, stop=True).then_inc(self.s("total"), 1)

        def turn_x(b):
            pe.wait_ge(self.s("staged"), b + 1)
            wait(pe, self.s("x_turned"), b)
            for k in range(KD):
                mm = pe.transpose(c.psum[0:S, 7, k * P:(k + 1) * P], self.stage[:, k, :], c.identity[:, :])
            mm.then_inc(self.s("x_units"), 1)

        def turn_x_whole(b):
            pe.wait_ge(self.s("identity"), 1)
            pe.wait_ge(self.s("x_whole"), b + 1)
            bank = c.psum[:, 7, :].bitcast(BF16)
            for k in range(KD):
                mm = pe.transpose(bank[:, k * S:(k + 1) * S], self.x_whole[:, k * P:(k + 1) * P], self.identity[0:S, 0:S])
            mm.then_inc(self.s("x_whole_units"), 1)

        def first():
            turn_x(0)
            turn_x_whole(0)
            pe.wait_ge(self.s("w0_whole"), KD)

        def body(i, before, now, after):
            if now:
                pe.wait_ge(self.s("x_turned"), i + 1)
                wait(pe, self.s("inner"), i)
                for n in range(self.CHUNKS):
                    for k in range(KD):
                        at = k * self.INNER + n * 512
                        mm = pe.matmul(c.psum[0:S, n, :], self.x_turned[:, k, :], self.w[0][:, at:at + 512],
                                       start=k == 0, stop=k == KD - 1)
                mm.then_inc(self.s("inner_units"), 1)
            if after:
                turn_x(i + 1)
            if before:
                pe.wait_ge(self.s("w1_whole"), KD)
                pe.wait_ge(self.s("inner_turned"), (i - 1) * 2 + 2)
                wait(pe, self.s("added"), i - 1)
                for k in range(self.KI):
                    mm = pe.matmul(c.psum[0:S, 6, :], self.inner_turned[:, k, :], self.w[1][:, k * D:(k + 1) * D],
                                   start=k == 0, stop=k == self.KI - 1)
                mm.then_inc(self.s("out_units"), 1)
            if after:
                turn_x_whole(i + 1)
            if before:
                pe.wait_ge(self.s("out"), i)
                for k in range(KD):
                    mm = pe.transpose(c.psum[:, 6, k * S:(k + 1) * S], self.out[:, k * P:(k + 1) * P], c.identity[0:S, 0:S])
                mm.then_inc(self.s("out_turned_units"), 1)
            if now:
                pe.wait_ge(self.s("inner_whole"), i + 1)
                wait(pe, self.s("inner_turned"), i * 2)
                for k in range(self.KI):
                    bank = c.psum[:, 4 + k // 8, :].bitcast(BF16)
                    mm = pe.transpose(bank[:, k % 8 * S:(k % 8 + 1) * S], self.inner_whole[:, k * P:(k + 1) * P],
                                      self.identity[0:S, 0:S])
                mm.then_inc(self.s("inner_whole_units"), 1)
        self.schedule(pe, first, body)

    def act(self, c, act):
        ln_act(c, act, self)
        for x in range(2):
            for k in range(KD):
                act.wait_ge(self.s(f"w{x}{k}_landed"), 16)
                cut = slice(k * self.INNER, (k + 1) * self.INNER)
                act.activation(self.w[x][:, cut], self.w_raw[x][:, cut], ACT.Abs,
                               accum_out=self.sums[:, x, k:k + 1]).then_inc(self.s("magnitudes"), 1)

        def stage(b):
            wait(act, self.s("x_units"), b)
            act.activation(self.stage[:, :, :], c.xn[:, :, tokens_of(b)], ACT.Copy).then_inc(self.s("staged"), 1)

        def turned(b):
            act.wait_ge(self.s("x_whole_units"), b + 1)
            wait(act, self.s("inner_units"), b)
            act.activation(self.x_turned[:, :, :].rearrange("p k s -> p (k s)"),
                           c.psum[:, 7, :].bitcast(BF16)[:, 0:KD * S], ACT.Copy).then_inc(self.s("x_turned"), 1)

        def first():
            for h in range(2):
                act.wait_ge(c.sem("ln_xn"), 2 * self.index + h + 1)
            stage(0)
            turned(0)

        def body(i, before, now, after):
            if after:
                stage(i + 1)
            if now:
                act.wait_ge(self.s("inner_units"), i + 1)
                act.wait_ge(self.s("x_steps"), i + 1)
                wait(act, self.s("inner_whole"), i)
                act.activation(self.inner[:, :], c.psum[0:S, 0:self.CHUNKS, :].rearrange("s n w -> s (n w)"),
                               ACT.Relu, scale=self.one(self.x_step, i)).then_inc(self.s("inner"), 1)
            if after:
                turned(i + 1)
            if before:
                act.wait_ge(self.s("out_units"), i)
                act.wait_ge(self.s("h_steps"), i)
                wait(act, self.s("out_turned_units"), i - 1)
                act.activation(self.out[:, :], c.psum[0:S, 6, :], ACT.Copy, scale=self.one(self.h_step, i - 1)).then_inc(
                    self.s("out"), 1)
            if now:
                act.wait_ge(self.s("inner_whole_units"), i + 1)
                if before:
                    act.wait_ge(self.s("out_units"), i)
                for half in range(2):
                    act.activation(self.inner_turned[:, half * 8:half * 8 + 8, :].rearrange("p k s -> p (k s)"),
                                   c.psum[:, 4 + half, :].bitcast(BF16)[:, 0:8 * S], ACT.Copy).then_inc(
                                       self.s("inner_turned"), 1)
        self.schedule(act, first, body)

    def dve(self, c, dve):
        ln_dve(c, dve, self)
        dve.wait_ge(c.sem("constants"), 3)
        dve.tensor_copy(self.identity[:, :], c.identity[:, :]).then_inc(self.s("identity"), 1)
        dve.wait_ge(self.s("magnitudes"), 2 * KD)
        dve.tensor_reduce(self.sum[:, :], self.sums[:, :, :], AX.X, ALU.add).then_inc(self.s("sum"), 2)
        dve.wait_ge(self.s("total"), 1)
        dve.tensor_scalar(self.step_w[:, :], c.psum[:, 4, 0:2], 1.0 / (D * self.INNER), self.EPS, ALU.mult,
                          ALU.max).then_inc(self.s("step_w"), 1)
        dve.wait_ge(self.s("step_w"), 1)
        for x, half in enumerate((0.5, -0.5)):
            dve.tensor_scalar(self.border[:, x, :], self.step_w[:, :], half, None, ALU.mult).then_inc(self.s("borders"), 2)
        dve.wait_ge(self.s("borders"), 4)
        self.whole_weight(dve, 0)

        def scales(largest, scale, step, weight, b, step_sem, name):
            small = self.s(name)
            dve.tensor_scalar(self.one(largest, b), self.one(largest, b), self.EPS, None, ALU.max).then_inc(small, 1)
            dve.wait_ge(small, b * 3 + 1)
            dve.reciprocal(self.one(scale, b), self.one(largest, b)).then_inc(small, 1)
            dve.tensor_scalar(self.one(step, b), self.one(largest, b), 1.0 / self.LEVELS, self.step_w[0:S, weight:weight + 1],
                              ALU.mult, ALU.mult).then_inc(step_sem, 1)
            dve.wait_ge(small, b * 3 + 2)
            dve.tensor_scalar(self.one(scale, b), self.one(scale, b), self.LEVELS, None, ALU.mult).then_inc(small, 1)
            dve.wait_ge(small, b * 3 + 3)

        def whole_x(b):
            dve.wait_ge(self.s("x_units"), b + 1)
            dve.tensor_reduce(self.one(self.x_max, b), c.psum[0:S, 7, :], AX.X, ALU.max,
                              apply_absolute_value=True).then_inc(self.s("x_max"), 1)
            dve.wait_ge(self.s("x_max"), b + 1)
            scales(self.x_max, self.x_scale, self.x_step, 0, b, self.s("x_steps"), "x_scales")
            dve.tensor_scalar(self.rows[:, :], c.psum[0:S, 7, :], self.one(self.x_scale, b), self.ROUND, ALU.mult,
                              ALU.add).then_inc(self.s("rows"), 1)
            dve.wait_ge(self.s("rows"), b + 1)
            dve.tensor_scalar(self.x_whole[:, :], self.rows[:, :], self.ROUND, None, ALU.subtract).then_inc(
                self.s("x_whole"), 1)

        def body(i, before, now, after):
            if after:
                whole_x(i + 1)
            if now:
                dve.wait_ge(self.s("inner"), i + 1)
                dve.tensor_reduce(self.one(self.h_max, i), self.inner[:, :], AX.X, ALU.max).then_inc(self.s("h_max"), 1)
                dve.wait_ge(self.s("h_max"), i + 1)
                scales(self.h_max, self.h_scale, self.h_step, 1, i, self.s("h_steps"), "h_scales")
                dve.tensor_scalar(self.inner[:, :], self.inner[:, :], self.one(self.h_scale, i), self.ROUND, ALU.mult,
                                  ALU.add).then_inc(self.s("inner_scaled"), 1)
                dve.wait_ge(self.s("inner_scaled"), i + 1)
                dve.tensor_scalar(self.inner_whole[:, :], self.inner[:, :], self.ROUND, None, ALU.subtract).then_inc(
                    self.s("inner_whole"), 1)
            if before:
                dve.wait_ge(self.s("out_turned_units"), i)
                into = c.residual[:, :, tokens_of(i - 1)]
                dve.tensor_tensor(into, into, c.psum[:, 6, 0:KD * S].rearrange("p (k s) -> p k s", k=KD),
                                  ALU.add).then_inc(self.s("added"), 1)
        self.schedule(dve, lambda: whole_x(0), body)
        dve.wait_ge(self.s("added"), B)
        dve.nop().then_inc(c.sem("residual_ready"), 1)



class LatentAttention:
    HEADS, DH, ROT = 16, 128, 64
    LOOKBACK, NEG = 8, 1e30
    SCALE = 1.0 / float(DH + ROT) ** 0.5
    PAIRS = HEADS // 2
    KVC, KR = 3, 4
    RAW = 3
    FIRST = 4
    LAST = FIRST + 3 * PAIRS

    def __init__(self, name, index, slabs_at):
        self.name, self.index, self.slabs_at = name, index, slabs_at

    def s(self, name):
        return self.c.sem(f"{self.name}_{name}")

    def buffers(self, c, own):
        n, self.c = self.name, c
        self.q_rot = c.sb(own, n + "_q_rot", [P, self.PAIRS, T])
        self.q_latent = c.sb(own, n + "_q_latent", [P, self.HEADS - 4, T])
        self.w_hi, self.w_lo = (c.sb(own, n + x, [P, 5, 512], F32R) for x in ("_w_hi", "_w_lo"))
        self.w_raw = c.sb(own, n + "_w_raw", [P, self.RAW, 512])
        self.cos_q, self.sin_q = (c.sb(own, n + x, [P, S]) for x in ("_cos_q", "_sin_q"))
        with ExitStack() as early:
            self.qc_hi, self.qc_lo = (c.sb(early, n + x, [P, 2, T], F32R) for x in ("_qc_hi", "_qc_lo"))
            self.fused_hi, self.fused_lo = (c.sb(early, n + x, [P, 2, 2 * P], F32R) for x in ("_fused_hi", "_fused_lo"))
        with ExitStack() as late:
            self.out_w_hi, self.out_w_lo = (c.sb(late, n + x, [P, 2, 2, D], F32R) for x in ("_out_w_hi", "_out_w_lo"))
            self.o_hi, self.o_lo = (c.sb(late, n + x, [P, 2, 2, T], F32R) for x in ("_o_hi", "_o_lo"))
        self.ql_hi, self.ql_lo = (c.sb(own, n + x, [P, self.HEADS, S], F32R) for x in ("_ql_hi", "_ql_lo"))
        self.qr_hi, self.qr_lo = (c.sb(own, n + x, [P, self.HEADS, S], F32R) for x in ("_qr_hi", "_qr_lo"))
        self.ctx_raw = c.sb(own, n + "_ctx_raw", [P, KD, CP])
        self.ctx_hi, self.ctx_lo = (c.sb(own, n + x, [P, KD, CP], F32R) for x in ("_ctx_hi", "_ctx_lo"))
        self.latent = c.sb(own, n + "_latent", [P, CP])
        self.l_hi, self.l_lo, self.kr_hi, self.kr_lo = (
            c.sb(own, n + x, [P, 2, CP], F32R) for x in ("_l_hi", "_l_lo", "_kr_hi", "_kr_lo"))
        self.l_turned = c.sb(own, n + "_l_turned", [P, 2, 3, P])
        spare = c.ln_squares[:, :, :].rearrange("p k t -> p (k t)")[:, 2 * T:]
        self.k_rot = spare[:, 0:2 * CP].rearrange("p (x t) -> p x t", x=2)
        self.early_enough = spare[0:S, 2 * CP:2 * CP + C]
        self.cos_k, self.sin_k = (c.sb(own, n + x, [P, CP]) for x in ("_cos_k", "_sin_k"))
        self.probs = c.sb(own, n + "_probs", [S, 4, C])
        self.ids = c.sb(own, n + "_ids", [S, B], I32)
        self.ids_f = c.sb(own, n + "_ids_f", [S, B])
        self.positions = c.sb(own, n + "_positions", [S, C])
        self.distance = c.sb(own, n + "_distance", [S, C])
        self.outside = c.sb(own, n + "_outside", [S, 2, C])
        self.highest, self.shift, self.total, self.inverse = (
            c.sb(own, n + x, [S, 4]) for x in ("_highest", "_shift", "_total", "_inverse"))

    def turned(self, c):
        return c.ln_squares[:, :, :].rearrange("p k t -> p (k t)")[:, 0:1200].rearrange("p (t n) -> p t n", t=3)

    def rotated(self, c, x):
        return c.ln_squares[:, x, :]

    def q_latent_of(self, c, head):
        if isinstance(head, int):
            return c.xn[:, head, :] if head < 4 else self.q_latent[:, head - 4, :]
        return self.q_latent[:, bass.DynSlice(head - 4, 1), :].rearrange("p a t -> p (a t)")

    def steps(self, engine, body):
        body(0, 0, True)
        body(1, 1, True)
        with engine.Fori(1, self.PAIRS // 2 - 1) as i:
            body(i * 2, 0, True)
            body(i * 2 + 1, 1, True)
        body(self.PAIRS - 2, 0, True)
        body(self.PAIRS - 1, 1, False)

    def slab_landed(self, engine, n, j=0):
        engine.wait_ge(self.s(f"w_landed{n % 3}"), (j + n // 3 + 1) * 16)

    def sync(self, c, sp):
        sp.wait_ge(c.sem("residual_ready"), self.index + 1)

        def slab(n, j=0):
            if not isinstance(j, int) or n + 3 * j >= 3:
                sp.wait_ge(self.s("w_split"), j * 3 + n - 2)
            src = (c.slabs[self.slabs_at + n + 3 * j, :, :] if isinstance(j, int) else
                   c.slabs[bass.DynSlice(j * 3 + (self.slabs_at + n), 1), :, :].rearrange("a p n -> p (a n)"))
            sp.dma_start(self.w_raw[:, n % 3, :], src).then_inc(self.s(f"w_landed{n % 3}"), 16)
        sp.dma_start(self.ctx_raw[:, :, :], c.a["ctx"][0, :, :, :]).then_inc(self.s("ctx_landed"), 16)
        for n in range(self.FIRST):
            slab(n)
        for name, buffer in (("cos_q", self.cos_q), ("sin_q", self.sin_q), ("cos_k", self.cos_k), ("sin_k", self.sin_k),
                             ("ids", self.ids), ("positions", self.positions)):
            sp.dma_start(buffer[:, :], c.a[name]).then_inc(self.s(name + "_landed"), 16)

        def step(first):
            def body(j, q, more):
                for x in range(3):
                    slab(first + x, j)
            return body
        self.steps(sp, step(self.FIRST))
        sp.wait_ge(self.s("ctx_split"), 1)
        sp.dma_start(self.ctx_raw[:, :, :], c.a["ctx"][1, :, :, :]).then_inc(self.s("ctx_landed"), 16)

        def batch(b, q, more, two_more):
            if two_more:
                sp.wait_ge(self.s("ctx_split"), b + 2)
                sp.dma_start(self.ctx_raw[:, :, :], c.a["ctx"][bass.DynSlice(b + 2, 1), :, :, :].rearrange(
                    "a p k t -> p (a k) t") if not isinstance(b, int) else c.a["ctx"][b + 2, :, :, :]).then_inc(
                        self.s("ctx_landed"), 16)
        batches(sp, batch)
        self.steps(sp, step(self.LAST))

    def pool(self, c, pool):
        pool.wait_ge(c.sem("residual_ready"), self.index + 1)

        def low(place, n, j=0):
            pool.wait_ge(self.s("w_hi"), j * 3 + n + 1)
            pool.tensor_tensor(self.w_lo[:, place, :], self.w_raw[:, n % 3, :], self.w_hi[:, place, :],
                               ALU.subtract).then_inc(self.s("w_split"), 1)
        pool.wait_ge(self.s("ctx_landed"), 16)
        pool.tensor_copy(self.ctx_hi[:, :, :], self.ctx_raw[:, :, :]).then_inc(self.s("ctx_hi"), 1)
        self.context_low(pool, 0)
        for n, place in ((0, self.KVC), (1, self.KR)):
            self.slab_landed(pool, n)
            pool.tensor_copy(self.w_hi[:, place, :], self.w_raw[:, n % 3, :]).then_inc(self.s("w_hi"), 1)
            low(place, n)
        low(0, 2)
        low(1, 3)

        def step(first):
            def body(j, q, more):
                for x in range(3):
                    low(x, first + x, j)
            return body
        self.steps(pool, step(self.FIRST))
        pool.wait_ge(self.s("ql_units"), self.HEADS)
        for buffer in (self.qr_hi, self.qr_lo):
            pool.memset(buffer[:, :, :].bitcast(F32), 0.0).then_inc(self.s("qr_zero"), 1)
        pool.wait_ge(self.s("ids_landed"), 16)
        pool.wait_ge(self.s("positions_landed"), 16)
        pool.tensor_copy(self.ids_f[:, :], self.ids[:, :]).then_inc(self.s("ids_f"), 1)
        pool.wait_ge(self.s("ids_f"), 1)
        pool.tensor_scalar(self.ids_f[:, :], self.ids_f[:, :], -1.0, None, ALU.mult).then_inc(self.s("ids_f"), 1)
        self.make_mask(c, pool, 0, 0)
        self.make_mask(c, pool, 1, 1)
        self.context_low(pool, 1)

        def batch(b, q, more, two_more):
            if two_more:
                self.context_low(pool, b + 2)
            if more:
                self.low_queries(c, pool, b + 1)
                pool.wait_ge(self.s("q_split"), b * 4 + 8)
                c.apart(pool)
            if two_more:
                self.make_mask(c, pool, b + 2, q)
        batches(pool, batch)
        self.steps(pool, step(self.LAST))

    def context_low(self, pool, b):
        pool.wait_ge(self.s("ctx_hi"), b + 1)
        pool.tensor_tensor(self.ctx_lo[:, :, :], self.ctx_raw[:, :, :], self.ctx_hi[:, :, :], ALU.subtract).then_inc(
            self.s("ctx_split"), 1)

    def act_distance(self, c, act, b):
        act.wait_ge(self.s("ids_f"), 2)
        wait(act, self.s("masks"), b)
        mine = self.ids_f[:, b:b + 1] if isinstance(b, int) else self.ids_f[:, bass.DynSlice(b, 1)]
        act.activation(self.distance[:, :], self.positions[:, :], ACT.Identity, bias=mine).then_inc(
            self.s("distances"), 1)

    def make_mask(self, c, pool, b, q):
        out, early, step = self.outside[:, q, :], self.early_enough, self.s("mask_steps")
        pool.wait_ge(self.s("distances"), b + 1)
        wait(pool, self.s("masked"), (b - 1) * 16)
        c.apart(pool)
        pool.tensor_scalar(early, self.distance[:, :], 0.0, None, ALU.is_le).then_inc(step, 1)
        pool.tensor_scalar(out, self.distance[:, :], -float(self.LOOKBACK), None, ALU.is_ge).then_inc(step, 1)
        pool.wait_ge(step, b * 3 + 2)
        pool.tensor_tensor(out, out, early, ALU.mult).then_inc(step, 1)
        pool.wait_ge(step, b * 3 + 3)
        c.apart(pool)
        pool.tensor_scalar(out, out, self.NEG, -self.NEG, ALU.mult, ALU.add).then_inc(self.s("masks"), 1)

    def pe(self, c, pe):
        ln_pe(c, pe, self)
        for h in range(2):
            pe.wait_ge(c.sem("ln_xn_lo"), 2 * self.index + h + 1)
        pe.wait_ge(self.s("w_split"), self.FIRST)
        for m in range(2):
            for k in range(KD):
                w = slice(k * P, (k + 1) * P)
                mm = product(pe, [c.psum[:, 2 * m + h, 0:HALF] for h in range(2)], self.w_hi[:, m, w], self.w_lo[:, m, w],
                             [tuple(x[:, k, h * HALF:(h + 1) * HALF] for x in (c.xn_hi, c.xn_lo)) for h in range(2)],
                             k == 0, k == KD - 1)
            mm.then_inc(self.s("qc_units"), 1)
        pe.wait_ge(self.s("qc_lo"), 2)
        qc = [[tuple(x[:, k, h * HALF:(h + 1) * HALF] for x in (self.qc_hi, self.qc_lo)) for h in range(2)]
              for k in range(2)]

        def step(j, q, more):
            pe.wait_ge(self.s("w_split"), j * 3 + self.FIRST + 2)
            wait(pe, self.s("ql_copied"), j * 2 - 1)
            for x in range(2):
                uk = slice(2 * P, 3 * P)
                for k in range(2):
                    at = (x * 2 + k) * P
                    uq = slice(k * P, (k + 1) * P)
                    mm = product(pe, [c.psum[:, 4, at:at + P]], self.w_hi[:, x, uq], self.w_lo[:, x, uq],
                                 [(self.w_hi[:, x, uk], self.w_lo[:, x, uk])], True, True)
            mm.then_inc(self.s("fused_units"), 1)
            pe.wait_ge(self.s("w_split"), j * 3 + self.FIRST + 3)
            wait(pe, self.s("rot_read"), j * 2)
            for x in range(2):
                for k in range(2):
                    w = slice((x * 2 + k) * P, (x * 2 + k + 1) * P)
                    mm = product(pe, [c.psum[:, 2 * x + h, 0:HALF] for h in range(2)], self.w_hi[:, 2, w],
                                 self.w_lo[:, 2, w], qc[k], k == 0, k == 1)
                mm.then_inc(self.s("rot_units"), 1)
            pe.wait_ge(self.s("fused_lo"), j + 1)
            for x in range(2):
                if x:
                    wait(pe, self.s("ql_copied"), j * 2)
                for k in range(2):
                    w = slice(k * P, (k + 1) * P)
                    mm = product(pe, [c.psum[:, 4 + 2 * x + h, 0:HALF] for h in range(2)], self.fused_hi[:, x, w],
                                 self.fused_lo[:, x, w], qc[k], k == 0, k == 1)
                mm.then_inc(self.s("ql_units"), 1)
        self.steps(pe, step)
        pe.wait_ge(self.s("ql_copied"), self.HEADS)
        pe.wait_ge(self.s("rot_read"), self.HEADS)
        for m in range(4):
            self.pe_piece(c, pe, 0, 0, m)
        self.pe_scores(c, pe, 0, 0, 0)
        batches(pe, lambda b, q, more, two_more: self.pe_batch(c, pe, b, q, more))
        pe.wait_ge(self.s("o_copied"), B * 4)

        def fuse_output(j, q):
            pe.wait_ge(self.s("w_split"), j * 3 + self.LAST + 3)
            wait(pe, self.s("out_w_lo"), j)
            for x in range(2):
                uv = slice(x * P, (x + 1) * P)
                mm = product(pe, [c.psum[:, 4 + x, :]], self.w_hi[:, 0, uv], self.w_lo[:, 0, uv],
                             [(self.w_hi[:, 1 + x, :], self.w_lo[:, 1 + x, :])], True, True)
            mm.then_inc(self.s("out_w_units"), 1)

        def out(j, q, more):
            if more:
                fuse_output(j + 1, 1 - q)
            pe.wait_ge(self.s("out_w_lo"), j + 1)
            pe.wait_ge(self.s("o_lo"), j + 1)
            for m in range(KD):
                wait(pe, self.s("added"), j * 4 + m - 1)
                for x in range(2):
                    w = slice(m * P, (m + 1) * P)
                    mm = product(pe, [c.psum[:, 2 * (m % 2) + h, 0:HALF] for h in range(2)], self.out_w_hi[:, q, x, w],
                                 self.out_w_lo[:, q, x, w],
                                 [tuple(o[:, q, x, h * HALF:(h + 1) * HALF] for o in (self.o_hi, self.o_lo))
                                  for h in range(2)], x == 0, x == 1)
                mm.then_inc(self.s("out_units"), 1)
        fuse_output(0, 0)
        self.steps(pe, out)

    def pe_piece(self, c, pe, b, q, m):
        bank = c.psum[:, 7, 0:CP]
        if m == 0:
            pe.wait_ge(self.s("ctx_split"), b + 1)
            for k in range(KD):
                w = slice(k * P, (k + 1) * P)
                mm = product(pe, [bank], self.w_hi[:, self.KVC, w], self.w_lo[:, self.KVC, w],
                             [(self.ctx_hi[:, k, :], self.ctx_lo[:, k, :])], k == 0, k == KD - 1)
        elif m < 3:
            pe.wait_ge(self.s("l_lo"), b + 1)
            if m == 2:
                pe.wait_ge(self.s("k_rotated"), b * 2 + 1)
            w = slice((m - 1) * P, m * P)
            mm = product(pe, [bank], self.w_hi[:, self.KR, w], self.w_lo[:, self.KR, w],
                         [(self.l_hi[:, q, :], self.l_lo[:, q, :])], True, True)
        else:
            pe.wait_ge(self.s("k_rotated"), b * 2 + 2)
            for t, (a, z) in enumerate(KEY_TILES):
                mm = pe.transpose(c.psum[0:z - a, 7, t * P:(t + 1) * P], self.latent[:, a:z], c.identity[:, :])
        mm.then_inc(self.s(f"piece{m}"), 1)

    def pe_scores(self, c, pe, b, q, m):
        i = b * 4 + m
        if m == 0:
            pe.wait_ge(self.s("q_split"), b * 4 + 4)
            pe.wait_ge(self.s("kr_lo"), b + 1)
            pe.wait_ge(self.s("l_lo"), b + 1)
        wait(pe, self.s("masked"), i * 4)
        for g in range(4):
            head = m * 4 + g
            bank = [c.psum[0:S, g, 0:CP]]
            product(pe, bank, self.ql_hi[:, head, :], self.ql_lo[:, head, :],
                    [(self.l_hi[:, q, :], self.l_lo[:, q, :])], True, False)
            mm = product(pe, bank, self.qr_hi[:, head, :], self.qr_lo[:, head, :],
                         [(self.kr_hi[:, q, :], self.kr_lo[:, q, :])], False, True)
        mm.then_inc(self.s("s_units"), 1)

    def pe_batch(self, c, pe, b, q, more):
        turned = self.turned(c)
        for m in range(4):
            i = b * 4 + m
            wait(pe, self.s("o_copied"), i)
            if more:
                self.pe_piece(c, pe, b + 1, 1 - q, m)
            if m < 3:
                self.pe_scores(c, pe, b, q, m + 1)
            elif more:
                self.pe_scores(c, pe, b + 1, 1 - q, 0)
            pe.wait_ge(self.s("normalised"), i * 4 + 4)
            wait(pe, self.s("turned_01"), i)
            wait(pe, self.s("turned_2"), i)
            for g in range(4):
                for t, (a, z) in enumerate(KEY_TILES):
                    mm = pe.transpose(c.psum[0:z - a, 4 + t, g * S:(g + 1) * S], self.probs[:, g, a:z],
                                      c.identity[0:S, 0:S])
            mm.then_inc(self.s("t_units"), 1)
            pe.wait_ge(self.s("turned_01"), i + 1)
            pe.wait_ge(self.s("turned_2"), i + 1)
            if m == 0:
                pe.wait_ge(self.s("l_turned"), b * 2 + 2)
            if more:
                if m == 0:
                    pe.wait_ge(self.s("l_lo"), b + 2)
                elif m < 3:
                    pe.wait_ge(self.s("k_rotated"), (b + 1) * 2 + m)
                else:
                    pe.wait_ge(self.s("l_turned"), (b + 1) * 2 + 2)
            for t, (a, z) in enumerate(KEY_TILES):
                mm = pe.matmul(c.psum[:, 7, 0:4 * S], self.l_turned[0:z - a, q, t, :], turned[0:z - a, t, :],
                               start=t == 0, stop=t == 2)
            mm.then_inc(self.s("pv_units"), 1)

    def act(self, c, act):
        ln_act(c, act, self)

        def high(place, n, j=0):
            self.slab_landed(act, n, j)
            act.activation(self.w_hi[:, place, :], self.w_raw[:, n % 3, :], ACT.Copy).then_inc(self.s("w_hi"), 1)
        act.wait_ge(self.s("w_hi"), 2)
        high(0, 2)
        high(1, 3)
        for m in range(2):
            act.wait_ge(self.s("qc_units"), m + 1)
            act.activation(self.qc_hi[:, m, :].rearrange("p (h t) -> p h t", h=2), c.psum[:, 2 * m:2 * m + 2, 0:HALF],
                           ACT.Copy).then_inc(self.s("qc_hi"), 1)
        for x in range(3):
            high(x, self.FIRST + x)

        def step(j, q, more):
            act.wait_ge(self.s("fused_units"), j + 1)
            act.activation(self.fused_hi[:, :, :].rearrange("p x n -> p (x n)"), c.psum[:, 4, :], ACT.Copy).then_inc(
                self.s("fused_hi"), 1)
            if more:
                for x in range(3):
                    if x == 2:
                        act.wait_ge(self.s("rot_units"), j * 2 + 2)
                    high(x, self.FIRST + 3 + x, j)
            for x in range(2):
                act.wait_ge(self.s("ql_units"), j * 2 + x + 1)
                act.activation(self.q_latent_of(c, j * 2 + x).rearrange("p (h t) -> p h t", h=2),
                               c.psum[:, 4 + 2 * x:6 + 2 * x, 0:HALF], ACT.Copy).then_inc(self.s("ql_copied"), 1)
        self.steps(act, step)
        self.act_distance(c, act, 0)
        for m in range(4):
            self.act_piece(c, act, 0, 0, m)
        self.act_context(act, 1)
        self.act_distance(c, act, 1)
        act.wait_ge(self.s("qr_zero"), 2)
        act.wait_ge(self.s("q_rotated"), self.PAIRS)
        act.wait_ge(self.s("ql_copied"), self.HEADS)
        self.act_queries(c, act, 0)
        self.act_exps(c, act, 0)
        batches(act, lambda b, q, more, two_more: self.act_batch(c, act, b, q, more, two_more))
        act.wait_ge(self.s("pv_units"), B * 4)
        act.wait_ge(self.s("o_copied"), B * 4)
        for x in range(3):
            high(x, self.LAST + x)

        def split_output(j, q):
            act.wait_ge(self.s("out_w_units"), j + 1)
            act.activation(self.out_w_hi[:, q, :, :], c.psum[:, 4:6, :], ACT.Copy).then_inc(self.s("out_w_hi"), 1)
            for x in range(2):
                act.activation(self.o_hi[:, q, x, :], self.q_latent_of(c, j * 2 + x), ACT.Copy).then_inc(self.s("o_hi"), 1)

        def out(j, q, more):
            if not isinstance(j, int) or j:
                act.wait_ge(self.s("out_units"), j * 4)
            if more:
                split_output(j + 1, 1 - q)
                if isinstance(j, int) and j + 2 >= self.PAIRS:
                    return
                for x in range(3):
                    high(x, self.LAST + 6 + x, j)
        split_output(0, 0)
        for x in range(3):
            high(x, self.LAST + 3 + x)
        self.steps(act, out)

    def act_context(self, act, b):
        act.wait_ge(self.s("ctx_landed"), (b + 1) * 16)
        act.wait_ge(self.s("piece0"), b)
        act.activation(self.ctx_hi[:, :, :], self.ctx_raw[:, :, :], ACT.Copy).then_inc(self.s("ctx_hi"), 1)

    def act_piece(self, c, act, b, q, m):
        bank = c.psum[:, 7, 0:CP]
        if m == 0:
            act.wait_ge(self.s("piece0"), b + 1)
            wait(act, self.s("piece3"), b)
            act.activation(self.latent[:, :], bank, ACT.Copy).then_inc(self.s("latent"), 1)
            act.activation(self.l_hi[:, q, :], bank, ACT.Copy).then_inc(self.s("l_hi"), 1)
        if m == 2:
            act.wait_ge(self.s("k_whole"), b + 1)
            act.activation(self.kr_hi[:, q, :], self.k_rot[:, 0, :], ACT.Copy).then_inc(self.s("kr_hi"), 1)
        if m == 3:
            act.wait_ge(self.s("piece3"), b + 1)
            act.activation(self.l_turned[:, q, 0:2, :], c.psum[:, 7, 0:2 * P].rearrange("p (t l) -> p t l", t=2),
                           ACT.Copy).then_inc(self.s("l_turned"), 1)

    def queries_of(self, c, b):
        t = tokens_of(b)
        return [(c.xn[:, :, t], self.ql_hi[:, 0:4, :], self.ql_lo[:, 0:4, :]),
                (self.q_latent[:, :, t], self.ql_hi[:, 4:, :], self.ql_lo[:, 4:, :]),
                (self.q_rot[0:64, :, t], self.qr_hi[0:64, 0::2, :], self.qr_lo[0:64, 0::2, :]),
                (self.q_rot[64:128, :, t], self.qr_hi[64:128, 1::2, :], self.qr_lo[64:128, 1::2, :])]

    def act_queries(self, c, act, b):
        for whole, high, _ in self.queries_of(c, b):
            act.activation(high, whole, ACT.Copy).then_inc(self.s("q_hi"), 1)

    def act_exps(self, c, act, i):
        act.wait_ge(self.s("shifts"), i + 1)
        for g in range(4):
            act.activation(self.probs[:, g, :], self.probs[:, g, :], ACT.Exp, bias=self.shift[:, g:g + 1],
                           scale=self.SCALE, accum_out=self.total[:, g:g + 1]).then_inc(self.s("exps"), 1)

    def act_batch(self, c, act, b, q, more, two_more):
        turned = self.turned(c)
        for m in range(4):
            i = b * 4 + m
            if more:
                self.act_piece(c, act, b + 1, 1 - q, m)
            if two_more and m == 1:
                self.act_context(act, b + 2)
                self.act_distance(c, act, b + 2)
            act.wait_ge(self.s("t_units"), i + 1)
            wait(act, self.s("pv_units"), i)
            act.activation(turned[:, 0:2, :], c.psum[:, 4:6, 0:4 * S], ACT.Copy).then_inc(self.s("turned_01"), 1)
            if more and m == 2:
                act.wait_ge(self.s("s_units"), b * 4 + 4)
                self.act_queries(c, act, b + 1)
            act.wait_ge(self.s("pv_units"), i + 1)
            into = (c.xn if m == 0 else self.q_latent)[:, (0 if m == 0 else m * 4 - 4):(4 if m == 0 else m * 4), tokens_of(b)]
            if m == 0:
                act.wait_ge(self.s("q_split"), b * 4 + 4)
            c.apart(act)
            act.activation(into, c.psum[:, 7, 0:4 * S].rearrange("p (g s) -> p g s", g=4), ACT.Copy).then_inc(
                self.s("o_copied"), 1)
            if m < 3 or more:
                self.act_exps(c, act, i + 1)

    def dve(self, c, dve):
        ln_dve(c, dve, self)
        for m in range(2):
            dve.wait_ge(self.s("qc_hi"), m + 1)
            dve.tensor_tensor(self.qc_lo[:, m, :].rearrange("p (h t) -> p h t", h=2), c.psum[:, 2 * m:2 * m + 2, 0:HALF],
                              self.qc_hi[:, m, :].rearrange("p (h t) -> p h t", h=2), ALU.subtract).then_inc(
                                  self.s("qc_lo"), 1)
        for x in ("cos_q", "sin_q", "cos_k", "sin_k"):
            dve.wait_ge(self.s(x + "_landed"), 16)

        def step(j, q, more):
            dve.wait_ge(self.s("fused_hi"), j + 1)
            dve.tensor_tensor(self.fused_lo[:, :, :].rearrange("p x n -> p (x n)"), c.psum[:, 4, :],
                              self.fused_hi[:, :, :].rearrange("p x n -> p (x n)"), ALU.subtract).then_inc(
                                  self.s("fused_lo"), 1)
            for x, table in enumerate((self.cos_q, self.sin_q)):
                dve.wait_ge(self.s("rot_units"), j * 2 + x + 1)
                wait(dve, self.s("q_rotated"), j)
                for h in range(2):
                    dst = self.rotated(c, x)[:, h * HALF:(h + 1) * HALF].rearrange("p (b s) -> p b s", s=S)
                    ins = dve.tensor_tensor(dst, c.psum[:, 2 * x + h, 0:HALF].rearrange("p (b s) -> p b s", s=S),
                                            table[:, :].unsqueeze(1).broadcast_to([P, HALF // S, S]), ALU.mult)
                    if h == 0:
                        ins.then_inc(self.s("rot_first_half"), 1)
                ins.then_inc(self.s("rot_read"), 1)
            dve.wait_ge(self.s("rot_read"), j * 2 + 2)
            dve.wait_ge(self.s("rot_first_half"), j * 2 + 2)
            out = self.q_rot[:, j, :] if isinstance(j, int) else self.q_rot[:, bass.DynSlice(j, 1), :].rearrange(
                "p a t -> p (a t)")
            dve.tensor_tensor(out, self.rotated(c, 0), self.rotated(c, 1), ALU.add).then_inc(self.s("q_rotated"), 1)
        self.steps(dve, step)
        for m in range(4):
            self.dve_piece(c, dve, 0, 0, m)
        self.low_queries(c, dve, 0)
        self.dve_mask(c, dve, 0, 0, 0)
        batches(dve, lambda b, q, more, two_more: self.dve_batch(c, dve, b, q, more))

        def split_output(j, q):
            dve.wait_ge(self.s("out_w_hi"), j + 1)
            dve.tensor_tensor(self.out_w_lo[:, q, :, :], c.psum[:, 4:6, :], self.out_w_hi[:, q, :, :],
                              ALU.subtract).then_inc(self.s("out_w_lo"), 1)
            for x in range(2):
                dve.wait_ge(self.s("o_hi"), j * 2 + x + 1)
                ins = dve.tensor_tensor(self.o_lo[:, q, x, :], self.q_latent_of(c, j * 2 + x), self.o_hi[:, q, x, :],
                                        ALU.subtract)
                if x == 0:
                    ins.then_inc(self.s("o_lo_first"), 1)
            ins.then_inc(self.s("o_lo"), 1)

        def out(j, q, more):
            if more:
                split_output(j + 1, 1 - q)
            for m in range(KD):
                dve.wait_ge(self.s("out_units"), j * 4 + m + 1)
                if not isinstance(j, int) or j:
                    dve.wait_ge(self.s("added"), j * 4 + m - 3)
                into = c.residual[:, m, :].rearrange("p (h t) -> p h t", h=2)
                dve.tensor_tensor(into, into, c.psum[:, 2 * (m % 2):2 * (m % 2) + 2, 0:HALF], ALU.add).then_inc(
                    self.s("added"), 1)
        split_output(0, 0)
        self.steps(dve, out)
        dve.wait_ge(self.s("added"), self.PAIRS * 4)
        dve.nop().then_inc(c.sem("residual_ready"), 1)

    def dve_piece(self, c, dve, b, q, m):
        bank = c.psum[:, 7, 0:CP]
        if m == 0:
            dve.wait_ge(self.s("l_hi"), b + 1)
            dve.wait_ge(self.s("latent"), b + 1)
            dve.tensor_tensor(self.l_lo[:, q, :], bank, self.l_hi[:, q, :], ALU.subtract).then_inc(self.s("l_lo"), 1)
        elif m < 3:
            dve.wait_ge(self.s(f"piece{m}"), b + 1)
            if m == 1:
                wait(dve, self.s("kr_lo"), b)
                wait(dve, self.s("kr_hi"), b)
            dve.tensor_tensor(self.k_rot[:, m - 1, :], bank, (self.cos_k if m == 1 else self.sin_k)[:, :],
                              ALU.mult).then_inc(self.s("k_rotated"), 1)
            if m == 2:
                dve.wait_ge(self.s("k_rotated"), b * 2 + 2)
                dve.tensor_tensor(self.k_rot[:, 0, :], self.k_rot[:, 0, :], self.k_rot[:, 1, :], ALU.add).then_inc(
                    self.s("k_whole"), 1)
        else:
            n = KEY_TILES[2][1] - KEY_TILES[2][0]
            dve.wait_ge(self.s("kr_hi"), b + 1)
            dve.tensor_tensor(self.kr_lo[:, q, :], self.k_rot[:, 0, :], self.kr_hi[:, q, :], ALU.subtract).then_inc(
                self.s("kr_lo"), 1)
            dve.wait_ge(self.s("l_turned"), b * 2 + 1)
            dve.tensor_copy(self.l_turned[0:n, q, 2, :], c.psum[0:n, 7, 2 * P:3 * P]).then_inc(self.s("l_turned"), 1)

    def low_queries(self, c, engine, b):
        for n, (whole, high, low) in enumerate(self.queries_of(c, b)):
            engine.wait_ge(self.s("q_hi"), b * 4 + n + 1)
            if n:
                engine.wait_ge(self.s("q_split"), b * 4 + n)
            c.apart(engine)
            engine.tensor_tensor(low, whole, high, ALU.subtract).then_inc(self.s("q_split"), 1)

    def dve_mask(self, c, dve, b, q, m):
        i = b * 4 + m
        dve.wait_ge(self.s("s_units"), i + 1)
        if m == 0:
            dve.wait_ge(self.s("masks"), b + 1)
        wait(dve, self.s("t_units"), i)
        c.apart(dve)
        for g in range(4):
            dve.tensor_tensor_reduce(self.probs[:, g, :], c.psum[0:S, g, 0:C], self.outside[:, q, :], 1.0, -3.0e38,
                                     ALU.add, ALU.max, self.highest[:, g:g + 1]).then_inc(self.s("masked"), 1)
        dve.wait_ge(self.s("masked"), i * 4 + 4)
        dve.tensor_scalar(self.shift[:, :], self.highest[:, :], -self.SCALE, None, ALU.mult).then_inc(self.s("shifts"), 1)

    def dve_batch(self, c, dve, b, q, more):
        turned = self.turned(c)
        for m in range(4):
            i = b * 4 + m
            dve.wait_ge(self.s("exps"), i * 4 + 4)
            dve.reciprocal(self.inverse[:, :], self.total[:, :]).then_inc(self.s("inverses"), 1)
            dve.wait_ge(self.s("inverses"), i + 1)
            for g in range(4):
                dve.tensor_scalar(self.probs[:, g, :], self.probs[:, g, :], self.inverse[:, g:g + 1], None,
                                  ALU.mult).then_inc(self.s("normalised"), 1)
            if more:
                self.dve_piece(c, dve, b + 1, 1 - q, m)
            n = KEY_TILES[2][1] - KEY_TILES[2][0]
            dve.wait_ge(self.s("t_units"), i + 1)
            wait(dve, self.s("pv_units"), i)
            dve.tensor_copy(turned[0:n, 2, :], c.psum[0:n, 6, 0:4 * S]).then_inc(self.s("turned_2"), 1)
            if m < 3:
                self.dve_mask(c, dve, b, q, m + 1)
            elif more:
                self.dve_mask(c, dve, b + 1, 1 - q, 0)


def program(nc, a, out, stages):
    with ExitStack() as ctx:
        c = Core(nc, ctx, stages)
        c.a = a
        c.slabs = a["slabs"]
        c.psum = ctx.enter_context(nc.psum_tensor("psum", [P, 8, 512], F32))
        c.residual = c.sb(ctx, "residual", [P, KD, T])
        c.xn = c.sb(ctx, "xn", [P, KD, T])
        c.ln_rstd = c.sb(ctx, "ln_rstd", [P, T])
        c.ln_std = c.sb(ctx, "ln_std", [P, T])
        c.eps = c.sb(ctx, "eps", [P, 1])
        c.mean_matrix = c.sb(ctx, "mean_matrix", [P, P])
        c.ones = c.sb(ctx, "ones", [P, P])
        c.identity = c.sb(ctx, "identity", [P, P])
        c.ln_squares = c.sb(ctx, "ln_squares", [P, KD, T])
        with ExitStack() as shared:
            c.xn_hi = c.sb(shared, "xn_hi", [P, KD, T], F32R)
            c.xn_lo = c.sb(shared, "xn_lo", [P, KD, T], F32R)
            for st in stages:
                if not isinstance(st, LatentAttention):
                    with ExitStack() as own:
                        st.buffers(c, own)
        for st in stages:
            if isinstance(st, LatentAttention):
                with ExitStack() as own:
                    st.buffers(c, own)

        block = ctx.enter_context(nc.Block())

        @block.sync
        def _(sp):
            sp.dma_start(c.residual[:, :, :], a["x"]).then_inc(c.sem("x_landed"), 16)
            sp.dma_start(c.identity[:, :], a["identity"]).then_inc(c.sem("identity_landed"), 16)
            for st in stages:
                c.enter(sp, st)
                st.sync(c, sp)
                c.clear_set(sp, st)
            sp.wait_ge(c.sem("residual_ready"), len(stages) + 1)
            sp.dma_start(out, c.residual[:, :, :]).then_inc(c.sem("out_written"), 16)
            sp.wait_ge(c.sem("out_written"), 16)

        @block.gpsimd
        def _(pool):
            for st in stages:
                c.enter(pool, st)
                st.pool(c, pool)
                c.leave(pool, "pool")

        @block.tensor
        def _(pe):
            for st in stages:
                c.enter(pe, st)
                st.pe(c, pe)
                c.leave(pe, "tensor")

        @block.scalar
        def _(act):
            for st in stages:
                c.enter(act, st)
                st.act(c, act)
                c.leave(act, "scalar")

        @block.vector
        def _(dve):
            dve.memset(c.mean_matrix[:, :], 1.0 / D).then_inc(c.sem("constants"), 1)
            dve.memset(c.ones[:, :], 1.0).then_inc(c.sem("constants"), 1)
            dve.memset(c.eps[:, :], EPS_LN).then_inc(c.sem("constants"), 1)
            dve.wait_ge(c.sem("constants"), 3)
            dve.wait_ge(c.sem("x_landed"), 16)
            dve.wait_ge(c.sem("identity_landed"), 16)
            dve.nop().then_inc(c.sem("residual_ready"), 1)
            for st in stages:
                c.enter(dve, st)
                st.dve(c, dve)
                c.leave(dve, "vector")



def tiles(w, rows, cols):
    full = np.zeros((rows * P, cols * P), w.dtype)
    full[:w.shape[0], :w.shape[1]] = w
    return full.reshape(rows, P, cols, P).transpose(0, 2, 1, 3)


def slabs(blocks):
    blocks = np.stack(blocks)
    pad = -len(blocks) % 4
    if pad:
        blocks = np.concatenate([blocks, np.zeros((pad, P, P), blocks.dtype)])
    return blocks.reshape(-1, 4, P, P).transpose(0, 2, 1, 3).reshape(-1, P, 512)


def ffn_slabs(chunks):
    out = []
    for gate, up, down in chunks:
        nb = -(-gate.shape[1] // P)
        g, u, d = tiles(gate, KD, nb), tiles(up, KD, nb), tiles(down, nb, KD)
        for j in range(nb):
            out.append(slabs([g[k, j] for k in range(KD)]))
            out.append(slabs([u[k, j] for k in range(KD)]))
        out.append(slabs([d[k, m] for m in range(KD) for k in range(nb)]))
    return np.concatenate(out)


def l2f_slabs(i):
    gate_up, down = i["L2_ffn_w_gate_up"].T, i["L2_ffn_w_down"].T
    inner, w = down.shape[0], 2 * P
    return ffn_slabs([(gate_up[:, j:j + w], gate_up[:, inner + j:inner + j + w], down[j:j + w])
                      for j in range(0, inner, w)])


def feature_major(x):
    return np.ascontiguousarray(x.reshape(-1, KD, P).transpose(2, 1, 0))


def l0f_slabs(i):
    experts = [(w[:, :w.shape[1] // 2], w[:, w.shape[1] // 2:], d)
               for w, d in zip(i["L0_ffn_gate_up_w"], i["L0_ffn_down_w"])]
    return ffn_slabs(experts + [(i["L0_ffn_shared_gate_w"], i["L0_ffn_shared_up_w"], i["L0_ffn_shared_down_w"])])


def l3f_slabs(i):
    return ffn_slabs([(g.T, u.T, d.T) for g, u, d in zip(i["L3_ffn_gate_weight"], i["L3_ffn_up_weight"],
                                                         i["L3_ffn_down_weight"])])


def l0f_arrays(i):
    e = i["L0_ffn_router_w"].shape[1]
    return {"router": np.ascontiguousarray(i["L0_ffn_router_w"].reshape(KD, P, e).transpose(1, 0, 2)),
            "earlier": np.ascontiguousarray(np.broadcast_to(np.tril(np.ones((e, e), np.float32), -1), (S, e, e)))}


def l3f_arrays(i):
    def grouped(x):
        return np.ascontiguousarray(x.reshape(-1, P, x.shape[-1]).transpose(1, 0, 2))
    e = i["L3_ffn_gate_weight"].shape[0]
    return {"names": grouped(i["L3_ffn_topk_idx"]), "name_weights": grouped(i["L3_ffn_topk_weight"]),
            "expert_ids": np.ascontiguousarray(np.broadcast_to(np.arange(e, dtype=np.float32), (P, e)))}


def attention_slabs(i, layer):
    q, k, v, o = (tiles(i[f"{layer}_xattn_W{x}"].T, KD, KD) for x in "qkvo")
    columns = lambda w: [slabs([w[k, m] for k in range(KD)]) for m in range(KD)]
    return np.concatenate(columns(k) + [slabs([v[k, m] for m in range(KD)]) for k in range(KD)] + columns(q) + columns(o))


def attention_arrays(i, layer, name, more=()):
    vectors = [i[f"{layer}_xattn_{x}"].reshape(KD, P).T for x in ("bq", "bk", "bo", *more)]
    return {name + "_vectors": np.ascontiguousarray(np.stack(vectors, 1)),
            name + "_bv": np.ascontiguousarray(np.broadcast_to(i[f"{layer}_xattn_bv"], (P, D)))}


def context(i):
    x = i["ctx_2048"].reshape(B, C, KD, P).transpose(0, 3, 2, 1)
    out = np.zeros((B, P, KD, CP), x.dtype)
    out[..., :C] = x
    return out


def by_key(x):
    out = np.zeros((3 * P, B), x.dtype)
    out[:C] = x.T
    return np.ascontiguousarray(out.reshape(3, P, B).transpose(1, 0, 2))


def l1x_arrays(i):
    return {**attention_arrays(i, "L1", "l1x", ("ln_gamma", "ln_beta")), "context_mask": by_key(i["mask_BxS2_ik0"]),
            "out_scale": np.ascontiguousarray(np.broadcast_to(i["L1_xattn_residual_scale"], (P, 1)))}


def l3x_arrays(i):
    wq, wk = i["L3_xattn_Wqf"], i["L3_xattn_Wkf"]
    maps = np.zeros((P, 4 * P), wq.dtype)
    for h in range(GROUP):
        rows = slice(h * HD, (h + 1) * HD)
        maps[rows, h * 64:(h + 1) * 64] = wq.T
        maps[rows, 2 * P + h * 64:2 * P + (h + 1) * 64] = wk.T
    return {**attention_arrays(i, "L3", "l3x"), "key_mask": by_key(i["mask_BxS2_ff1"]),
            "feature_maps": maps.reshape(P, 4, P)}


def bit_arrays(i):
    return {f"bit_w{x}": np.ascontiguousarray(w.T.reshape(-1, P, w.shape[0]).transpose(1, 0, 2)).reshape(P, -1)
            for x, w in ((1, i["L1_ffn_w1"]), (2, i["L1_ffn_w2"]))}


def l0x_slabs(i):
    kvc, dq = i["L0_xattn_W_kvc"], i["L0_xattn_W_dq"]
    uq, qr, uk, kr, uv, o = (i[f"L0_xattn_W_{x}"] for x in ("uq", "qr", "uk", "kr", "uv", "o"))
    heads, rot = LatentAttention.HEADS, LatentAttention.ROT
    exchanged = np.concatenate([np.arange(rot // 2, rot), np.arange(rot // 2)])
    out = [slabs([t for t in tiles(kvc, KD, 1)[:, 0]]),
           slabs([np.concatenate([w, w], 1) for w in (kr, kr[:, exchanged])])]
    q_latent = tiles(dq, KD, 2)
    out += [slabs([q_latent[k, m] for k in range(KD)]) for m in range(2)]
    head = lambda w, h: w[:, h * P:(h + 1) * P]
    for j in range(heads // 2):
        for h in (2 * j, 2 * j + 1):
            up = tiles(head(uq, h).T, 1, 2)[0]
            out.append(slabs([up[0], up[1], head(uk, h).T]))
        pair = qr[:, 2 * j * rot:2 * (j + 1) * rot].reshape(-1, 2, rot)
        as_is, swapped = (tiles(x.reshape(-1, P), 2, 1)[:, 0] for x in (pair, pair[:, :, exchanged]))
        out.append(slabs([as_is[0], as_is[1], swapped[0], swapped[1]]))
    for j in range(heads // 2):
        out.append(slabs([head(uv, 2 * j).T, head(uv, 2 * j + 1).T]))
        out += [slabs(list(tiles(o[h * P:(h + 1) * P], 1, KD)[0])) for h in (2 * j, 2 * j + 1)]
    return np.concatenate(out)


def l0x_arrays(i):
    half = LatentAttention.ROT // 2
    inv_freq = np.float32(1.0) / np.float32(10000.0) ** (np.arange(half, dtype=np.float32) / np.float32(half))
    angle = np.arange(CP, dtype=np.float32)[None, :] * inv_freq[:, None]
    cos, sin = np.cos(angle).astype(np.float32), np.sin(angle).astype(np.float32)
    cos, sin = np.concatenate([cos] * 4), np.concatenate([-sin, sin] * 2)
    return {"cos_q": np.ascontiguousarray(cos[:, :S]), "sin_q": np.ascontiguousarray(sin[:, :S]), "cos_k": cos, "sin_k": sin,
            "ids": np.ascontiguousarray(i["itok_BxS_0_1023"].T),
            "positions": np.ascontiguousarray(np.broadcast_to(np.arange(C, dtype=np.float32), (S, C)))}



def all_stages():
    at, stages = 0, []
    for make, n in ((lambda i, at: LatentAttention("l0x", i, at), 52),
                    (lambda i, at: RoutedFfn("l0f", i, 9, 2, T, "before", at, experts=9), 54),
                    (lambda i, at: BoundedAttention("l1x", i, at), 16),
                    (lambda i, at: BitFfn("l1f", i), 0),
                    (lambda i, at: Attention("l2x", i, at), 16),
                    (lambda i, at: Ffn("l2f", i, 8, 2, T, "none", at), 48),
                    (lambda i, at: LinearAttention("l3x", i, at), 16),
                    (lambda i, at: ChosenFfn("l3f", i, 16, 3, 512, "after", at, experts=16), 144)):
        stages.append(make(len(stages), at))
        at += n
    return stages


def laid_out(i):
    weights = (l0x_slabs(i), l0f_slabs(i), attention_slabs(i, "L1"), attention_slabs(i, "L2"), l2f_slabs(i),
               attention_slabs(i, "L3"), l3f_slabs(i))
    return {"x": feature_major(i["x"]), "ctx": context(i), "identity": np.eye(P, dtype=np.float32),
            "slabs": np.concatenate(weights), **l0x_arrays(i), **l0f_arrays(i), **l1x_arrays(i), **bit_arrays(i),
            **attention_arrays(i, "L2", "l2x"), **l3x_arrays(i), **l3f_arrays(i)}


def kernel(**inputs):
    import concourse.bacc as _bacc
    from concourse.bass_utils import run_bass_kernel_spmd as _run

    inputs = {name: np.asarray(a) for name, a in inputs.items()}
    nc = _bacc.Bacc("TRN2", target_bir_lowering=False, num_devices=1)
    arrays, aps = {}, {}
    for name, a in laid_out(inputs).items():
        a = arrays[f"in_{name}_dram"] = np.ascontiguousarray(a)
        aps[name] = nc.dram_tensor(f"in_{name}_dram", a.shape, mybir.dt.from_np(a.dtype), kind="ExternalInput").ap()
    out = nc.dram_tensor("out_dram", (P, KD, T), F32, kind="ExternalOutput").ap()
    program(nc, aps, out, all_stages())
    r = _run(nc, [arrays], core_ids=[0])
    return np.ascontiguousarray(r.results[0]["out_dram"].transpose(2, 1, 0).reshape(B, S, D))
```

```python
from contextlib import ExitStack

import concourse.bass as bass
import numpy as np
from concourse import mybir

ALU = mybir.AluOpType
ACT = mybir.ActivationFunctionType
AX = mybir.AxisListType
F32 = mybir.dt.float32
F32R = mybir.dt.float32r
BF16 = mybir.dt.bfloat16
I32 = mybir.dt.int32

P = 128
D = 512
KD = D // P
B, S = 8, 100
T = B * S
HALF = T // 2
C = 361
CP = C + C % 2
EPS_LN = 1e-5


class Core:
    SHARED, SET_SIZES = 32, (72, 48)

    def __init__(self, nc, ctx, stages):
        self.nc, self.ctx, self.sems = nc, ctx, {}
        self.holders = [nc.alloc_semaphore(name=f"held_{n}") for n in range(self.SHARED + sum(self.SET_SIZES))]
        self.stages = {st.name: st.index for st in stages}
        self.mean_banks = [0] + [st.FREE_BANKS for st in stages[:-1]]
        self.splits_before = [sum(x.SPLIT_INPUT for x in stages[:n]) for n in range(len(stages))]
        self.used = {name: 0 for name in [*self.stages, "shared"]}

    def first_of(self, parity):
        return self.SHARED + (self.SET_SIZES[0] if parity else 0)

    def sem(self, name):
        if name not in self.sems:
            owner = name.split("_")[0] if name.split("_")[0] in self.stages else "shared"
            n, size = self.used[owner], self.SHARED
            self.used[owner] += 1
            if owner != "shared":
                parity = self.stages[owner] % 2
                size, at = self.SET_SIZES[parity], self.first_of(parity) + n
            else:
                at = n
            assert n < size, f"too many semaphores for {owner}"
            number = self.holders[at].num
            self.nc.release_semaphore(self.holders[at])
            self.sems[name] = self.holders[at] = self.nc.alloc_semaphore(name=name, num=number)
        return self.sems[name]

    def apart(self, engine):
        engine.nop().then_inc(self.sem("waits_passed"), 1)

    def enter(self, engine, st):
        if st.index >= 2:
            engine.wait_ge(self.sem("sets_cleared"), st.index - 1)
            engine.nop().then_inc(self.sem("stages_entered"), 1)

    def leave(self, engine, name):
        engine.nop().then_inc(self.sem(f"{name}_left_stages"), 1)

    def clear_set(self, sp, st):
        if st.index:
            for name in ("pool", "tensor", "scalar", "vector"):
                sp.wait_ge(self.sem(f"{name}_left_stages"), st.index)
            parity = (st.index - 1) % 2
            first = self.holders[self.first_of(parity)].num
            sp.sem_clear(range(first, first + self.SET_SIZES[parity])).then_inc(self.sem("sets_cleared"), 1)

    def sb(self, ctx, name, shape, dt=F32):
        return ctx.enter_context(self.nc.sbuf_tensor(name, shape, dt))


def wait(engine, semaphore, value):
    if isinstance(value, int) and value <= 0:
        return
    engine.wait_ge(semaphore, value)


def product(pe, outs, weight_hi, weight_lo, moving, first, last):
    n = len(outs)
    for i in range(n):
        pe.matmul(outs[i], weight_hi, moving[i][0], start=first, stop=False)
        pe.matmul(outs[i], weight_hi, moving[i][1], start=False, stop=False)
    for i in range(n):
        mm = pe.matmul(outs[i], weight_lo, moving[i][0], start=False, stop=last)
    return mm



QUARTERS = [slice(n * T // 4, (n + 1) * T // 4) for n in range(4)]


def ln_mean_of(c, st, n):
    return c.psum[:, c.mean_banks[st.index] + n // 2, n % 2 * (T // 4):(n % 2 + 1) * (T // 4)]


def ln_variance_of(c, st, n):
    return c.psum[:, 4 - c.mean_banks[st.index] + n, 0:T // 4]


def ln_mean_pe(c, pe, index, tile_ready):
    if index >= len(c.mean_banks):
        return
    for k in range(KD):
        tile_ready(k)
        for h in range(2):
            mm = pe.matmul(c.psum[:, c.mean_banks[index] + h, 0:HALF], c.mean_matrix[:, :],
                           c.residual[:, k, h * HALF:(h + 1) * HALF], start=k == 0, stop=k == KD - 1)
    mm.then_inc(c.sem("ln_mean"), 1)


def ln_pe(c, pe, st):
    for n, t in enumerate(QUARTERS):
        pe.wait_ge(c.sem("ln_squares"), 4 * st.index + n + 1)
        for k in range(KD):
            mm = pe.matmul(ln_variance_of(c, st, n), c.mean_matrix[:, :], c.ln_squares[:, k, t],
                           start=k == 0, stop=k == KD - 1)
        mm.then_inc(c.sem("ln_variance"), 1)


def ln_dve(c, dve, st, before_last=None):
    before = 4 * st.index
    split_before = 4 * c.splits_before[st.index]
    centered, shape = c.sem("ln_centered"), [P, KD, T // 4]
    dve.wait_ge(c.sem("ln_mean"), st.index + 1)
    for n, t in enumerate(QUARTERS):
        mean = ln_mean_of(c, st, n).unsqueeze(1).broadcast_to(shape)
        dve.tensor_tensor(c.xn[:, :, t], c.residual[:, :, t], mean, ALU.subtract).then_inc(centered, 1)

    def low(n):
        dve.wait_ge(c.sem("ln_xn_hi"), split_before + n + 1)
        dve.tensor_tensor(c.xn_lo[:, :, QUARTERS[n]], c.xn[:, :, QUARTERS[n]], c.xn_hi[:, :, QUARTERS[n]],
                          ALU.subtract).then_inc(c.sem("ln_xn_lo"), 1)
    for n, t in enumerate(QUARTERS):
        if n == 3 and before_last:
            low(2)
            before_last()
        dve.wait_ge(c.sem("ln_std"), before + n + 1)
        dve.reciprocal(c.ln_rstd[:, t], c.ln_std[:, t]).then_inc(c.sem("ln_rstd"), 1)
        dve.wait_ge(c.sem("ln_rstd"), before + n + 1)
        dve.wait_ge(centered, before + n + 1)
        rstd = c.ln_rstd[:, t].unsqueeze(1).broadcast_to(shape)
        dve.tensor_tensor(c.xn[:, :, t], c.xn[:, :, t], rstd, ALU.mult).then_inc(c.sem("ln_xn"), 1)
        if n and st.SPLIT_INPUT and not (n == 3 and before_last):
            low(n - 1)
    if st.SPLIT_INPUT:
        low(3)


def ln_act(c, act, st, before_std=None, before_high=None):
    before = 4 * st.index
    for n, t in enumerate(QUARTERS):
        act.wait_ge(c.sem("ln_centered"), before + n + 1)
        act.activation(c.ln_squares[:, :, t], c.xn[:, :, t], ACT.Square).then_inc(
            c.sem("ln_squares"), 1)
    if before_std:
        before_std()
    for n, t in enumerate(QUARTERS):
        act.wait_ge(c.sem("ln_variance"), before + n + 1)
        act.activation(c.ln_std[:, t], ln_variance_of(c, st, n), ACT.Sqrt, bias=c.eps[:, 0:1]).then_inc(
            c.sem("ln_std"), 1)
    for n, t in enumerate(QUARTERS):
        if before_high:
            before_high(n)
        if st.SPLIT_INPUT:
            act.wait_ge(c.sem("ln_xn"), before + n + 1)
            act.activation(c.xn_hi[:, :, t], c.xn[:, :, t], ACT.Copy).then_inc(c.sem("ln_xn_hi"), 1)


def wait_for_banks(c, pe, st):
    pe.wait_ge(c.sem("ln_std"), 4 * st.index + 4)


def wait_for_input(c, pe, st, quarters=4):
    pe.wait_ge(c.sem("ln_xn_lo"), 4 * c.splits_before[st.index] + quarters)



class Ffn:
    SPLIT_INPUT, FREE_BANKS = True, 0

    def __init__(self, name, index, chunks, blocks, tokens, scale, slabs_at, experts=0):
        self.name, self.index, self.chunks, self.blocks = name, index, chunks, blocks
        self.tokens = tokens
        self.scale = scale
        self.slabs_at, self.experts = slabs_at, experts
        self.halves = [(0, HALF), (HALF, T)] if tokens == T else [(0, tokens)]
        self.gu_slabs, self.dn_slabs = 2 * blocks, blocks
        self.per_chunk = 3 * blocks

    def buffers(self, c, own):
        n = self.name
        self.raw_dn = c.sb(own, n + "_raw_dn", [P, self.dn_slabs, 512])
        self.w = [c.sb(own, n + "_" + x, [P, self.gu_slabs if "gu" in x else self.dn_slabs, 512], F32R)
                  for x in ("w_gu_hi", "w_gu_lo", "w_dn_hi", "w_dn_lo")]
        self.h_hi, self.h_lo = (c.sb(own, n + x, [P, 2, self.blocks, self.tokens], F32R) for x in ("_h_hi", "_h_lo"))
        self.raw_gu = c.sb(own, n + "_raw_gu", [P, self.gu_slabs, 512])
        self.h, self.silu, self.up, self.gate = (c.sb(own, n + x, [P, 2, self.tokens]) for x in ("_h", "_silu", "_up", "_gate"))
        self.scales = c.sb(own, n + "_scales", [P, self.tokens])
        if self.experts:
            self.ones = c.sb(own, n + "_ones", [self.experts, P], F32R)
            self.row_hi, self.row_lo = (c.sb(own, n + x, [self.experts, 2, self.tokens], F32R)
                                        for x in ("_row_hi", "_row_lo"))
            self.expert_weights = c.sb(own, n + "_expert_weights", [self.experts, self.tokens])

    def prefetch(self, c, sp):
        for j in range(self.gu_slabs):
            sp.dma_start(self.raw_gu[:, j, :], c.slabs[self.slabs_at + j, :, :]).then_inc(
                c.sem(f"{self.name}_gu_landed{j}"), 16)

    def nearly_over(self, c, sp):
        pass

    def sync(self, c, sp):
        ffn_sync(c, sp, self)

    def pool(self, c, pool):
        ffn_pool(c, pool, self)

    def pe(self, c, pe):
        ln_pe(c, pe, self)
        self.prepare_pe(c, pe)
        ffn_pe(c, pe, self)

    def act(self, c, act):
        def first_slabs(n):
            for j in range(n * self.gu_slabs // 4, (n + 1) * self.gu_slabs // 4):
                ffn_high_gu(c, act, self, 0, j)
        ln_act(c, act, self, lambda: self.act_before_std(c, act), first_slabs)
        self.prepare_act(c, act)
        ffn_act(c, act, self)

    def dve(self, c, dve):
        ln_dve(c, dve, self, lambda: self.dve_before_last_quarter(c, dve))
        self.prepare_dve(c, dve)
        ffn_dve(c, dve, self)

    def act_before_std(self, c, act):
        pass

    def dve_before_last_quarter(self, c, dve):
        pass

    def prepare_pe(self, c, pe):
        pass

    def prepare_act(self, c, act):
        pass

    def prepare_dve(self, c, dve):
        pass

    def views(self, c, bank):
        return [c.psum[:, bank + n, 0:b - a] for n, (a, b) in enumerate(self.halves)]

    def span(self, c, bank):
        if len(self.halves) == 1:
            return c.psum[:, bank, 0:self.tokens]
        return c.psum[:, bank:bank + 2, 0:HALF]

    def cut(self, ap):
        return ap if len(self.halves) == 1 else ap.rearrange("p (h t) -> p h t", h=2)


def ffn_schedule(engine, st, gate_up, down):
    n = st.chunks
    gate_up(0, 0)
    gate_up(1, 1)
    down(0, 0)
    turns = (n - 3) // 2
    with engine.Fori(0, turns) as i:
        gate_up(i * 2 + 2, 0)
        down(i * 2 + 1, 1)
        gate_up(i * 2 + 3, 1)
        down(i * 2 + 2, 0)
    for x in range(2 * turns + 1, n):
        if x + 1 < n:
            gate_up(x + 1, (x + 1) % 2)
        down(x, x % 2)


def ffn_sync(c, sp, st):
    def load(raw, landed, split, count, at, n_of_kind, chunk):
        for j in range(count):
            wait(sp, split, (chunk - 1) * count + j + 1 if not isinstance(chunk, int) or chunk else 0)
            sp.dma_start(raw[:, j, :], c.slabs[bass.DynSlice(at + j, 1), :, :].rearrange("a p n -> p (a n)")
                         if not isinstance(at, int) else c.slabs[at + j, :, :]).then_inc(
                             c.sem(f"{landed}{j}"), 16)

    def gate_up(chunk, q):
        if isinstance(chunk, int) and chunk == 0:
            return
        load(st.raw_gu, st.name + "_gu_landed", c.sem(st.name + "_gu_split"), st.gu_slabs,
             chunk * st.per_chunk + st.slabs_at, st.gu_slabs, chunk)

    def down(chunk, q):
        load(st.raw_dn, st.name + "_dn_landed", c.sem(st.name + "_dn_split"), st.dn_slabs,
             chunk * st.per_chunk + st.slabs_at + st.gu_slabs, st.dn_slabs, chunk)
    sp.wait_ge(c.sem("residual_ready"), st.index + 1)
    ffn_schedule(sp, st, gate_up, down)


def ffn_pool(c, pool, st):
    def split(raw, hi, lo, kind, count, chunk):
        for j in range(count):
            pool.wait_ge(c.sem(f"{st.name}_{kind}_hi"), chunk * count + j + 1)
            pool.tensor_tensor(lo[:, j, :], raw[:, j, :], hi[:, j, :], ALU.subtract).then_inc(
                c.sem(f"{st.name}_{kind}_split"), 1)

    pool.wait_ge(c.sem("residual_ready"), st.index + 1)
    ffn_schedule(pool, st, lambda chunk, q: split(st.raw_gu, st.w[0], st.w[1], "gu", st.gu_slabs, chunk),
                 lambda chunk, q: split(st.raw_dn, st.w[2], st.w[3], "dn", st.dn_slabs, chunk))


def ffn_high_gu(c, act, st, chunk, j):
    if not isinstance(chunk, int) or chunk:
        units = 2 * st.blocks + (st.scale != "none")
        act.wait_ge(c.sem(st.name + "_gu_units"), (chunk - 1) * units + j + 1 + (units - st.gu_slabs))
    act.wait_ge(c.sem(f"{st.name}_gu_landed{j}"), (chunk + 1) * 16)
    act.activation(st.w[0][:, j, :], st.raw_gu[:, j, :], ACT.Copy).then_inc(c.sem(st.name + "_gu_hi"), 1)


def ffn_high_dn(c, act, st, chunk, j):
    if not isinstance(chunk, int) or chunk:
        act.wait_ge(c.sem(st.name + "_dn_units"), (chunk - 1) * KD + (4 * j + 3) // st.blocks + 1)
    act.wait_ge(c.sem(f"{st.name}_dn_landed{j}"), (chunk + 1) * 16)
    act.activation(st.w[2][:, j, :], st.raw_dn[:, j, :], ACT.Copy).then_inc(c.sem(st.name + "_dn_hi"), 1)


def ffn_pe(c, pe, st):
    nb = st.blocks
    gate_read = "_gate_scaled" if st.scale == "before" else "_g_read"
    up_read = "_h" if st.scale == "none" else "_u_read"

    def gate_up(chunk, q):
        if st.scale != "none":
            pe.wait_ge(c.sem(st.name + "_row"), chunk + 1)
            if not isinstance(chunk, int) or chunk:
                pe.wait_ge(c.sem(st.name + "_u_read"), chunk * nb)
            for (a, b), out in zip(st.halves, st.views(c, 2)):
                pe.wait_ge(c.sem(st.name + "_ones"), 1)
                ones = st.ones[0:st.experts, :]
                pe.matmul(out, ones, st.row_hi[0:st.experts, q, a:b], start=True, stop=False)
                mm = pe.matmul(out, ones, st.row_lo[0:st.experts, q, a:b], start=False, stop=True)
            mm.then_inc(c.sem(st.name + "_gu_units"), 1)
        start = 0
        if isinstance(chunk, int) and chunk == 0 and st.scale == "none":
            start = 2
            for h, (a, b) in enumerate(st.halves):
                wait_for_input(c, pe, st, 2 * h + 2)
                for j in range(2):
                    pe.wait_ge(c.sem(st.name + "_gu_split"), j + 1)
                    for k in range(KD):
                        w = slice(k * P, (k + 1) * P)
                        mm = product(pe, [st.views(c, 2 * j)[h]], st.w[0][:, j, w], st.w[1][:, j, w],
                                     [(c.xn_hi[:, k, a:b], c.xn_lo[:, k, a:b])], k == 0, k == KD - 1)
                    if h:
                        mm.then_inc(c.sem(st.name + "_gu_units"), 1)
        for j in range(start, 2 * nb):
            pe.wait_ge(c.sem(st.name + "_gu_split"), chunk * st.gu_slabs + j + 1)
            if j % 2 == 0:
                wait(pe, c.sem(st.name + gate_read), chunk * nb + j // 2)
            else:
                wait(pe, c.sem(st.name + up_read), chunk * nb + j // 2)
                if j == 1 and st.scale != "none":
                    pe.wait_ge(c.sem(st.name + "_scale_copied"), chunk + 1)
            outs = st.views(c, 0 if j % 2 == 0 else 2)
            for k in range(KD):
                w = slice(k * P, (k + 1) * P)
                mm = product(pe, outs, st.w[0][:, j, w], st.w[1][:, j, w],
                             [(c.xn_hi[:, k, a:b], c.xn_lo[:, k, a:b]) for a, b in st.halves],
                             k == 0, k == KD - 1)
            mm.then_inc(c.sem(st.name + "_gu_units"), 1)

    def down(chunk, q):
        pe.wait_ge(c.sem(st.name + "_h_lo"), (chunk + 1) * nb)
        for m in range(KD):
            pe.wait_ge(c.sem(st.name + "_dn_split"), chunk * st.dn_slabs + (m * nb + nb - 1) // 4 + 1)
            if m < 2:
                wait(pe, c.sem(st.name + "_added"), chunk * KD + m - 1 if not isinstance(chunk, int) or chunk else 0)
            else:
                pe.wait_ge(c.sem(st.name + "_added"), chunk * KD + m - 1)
            outs = st.views(c, 4 + 2 * (m % 2))
            for k in range(nb):
                tile = m * nb + k
                j, w = tile // 4, slice(tile % 4 * P, (tile % 4 + 1) * P)
                mm = product(pe, outs, st.w[2][:, j, w], st.w[3][:, j, w],
                             [(st.h_hi[:, q, k, a:b], st.h_lo[:, q, k, a:b]) for a, b in st.halves],
                             k == 0, k == nb - 1)
            mm.then_inc(c.sem(st.name + "_dn_units"), 1)
    if st.scale != "none":
        wait_for_input(c, pe, st, -(-st.tokens // (T // 4)))
    ffn_schedule(pe, st, gate_up, down)
    ln_mean_pe(c, pe, st.index + 1, lambda k: pe.wait_ge(c.sem(st.name + "_added"), (st.chunks - 1) * KD + k + 1))


def ffn_act(c, act, st):
    nb, n = st.blocks, st.tokens

    def more(chunk):
        return not isinstance(chunk, int) or chunk + 1 < st.chunks

    def gate_up(chunk, q):
        if st.scale != "none":
            units = chunk * (2 * nb + 1)
            act.wait_ge(c.sem(st.name + "_gu_units"), units + 1)
            if not isinstance(chunk, int) or chunk:
                act.wait_ge(c.sem(st.name + "_u_read"), chunk * nb)
            act.activation(st.cut(st.scales[:, 0:n]), st.span(c, 2), ACT.Copy).then_inc(
                c.sem(st.name + "_scale_copied"), 1)

        def split_high(j):
            act.wait_ge(c.sem(st.name + "_h"), chunk * nb + j + 1)
            act.activation(st.h_hi[:, q, j, 0:n], st.h[:, (q * nb + j) % 2, 0:n], ACT.Copy).then_inc(
                c.sem(st.name + "_h_hi"), 1)
        for j in range(nb):
            b = (q * nb + j) % 2
            if not (isinstance(chunk, int) and chunk == 0 and j < 2):
                act.wait_ge(c.sem(st.name + "_h"), chunk * nb + j - 1)
            if st.scale == "before":
                act.wait_ge(c.sem(st.name + "_gate_scaled"), chunk * nb + j + 1)
                act.activation(st.silu[:, b, 0:n], st.gate[:, b, 0:n], ACT.Silu).then_inc(
                    c.sem(st.name + "_silu"), 1)
            else:
                first = 1 if st.scale != "none" else 0
                act.wait_ge(c.sem(st.name + "_gu_units"), chunk * (2 * nb + first) + first + 2 * j + 1)
                act.activation(st.cut(st.silu[:, b, 0:n]), st.span(c, 0), ACT.Silu).then_inc(
                    c.sem(st.name + "_g_read"), 1)
            if more(chunk):
                for slab in range(max(2 * j - 1, 0), 2 * j + 1):
                    ffn_high_gu(c, act, st, chunk + 1, slab)
            if j:
                split_high(j - 1)
        split_high(nb - 1)
        if more(chunk):
            ffn_high_gu(c, act, st, chunk + 1, 2 * nb - 1)

    def down(chunk, q):
        if more(chunk):
            for j in range(st.dn_slabs):
                ffn_high_dn(c, act, st, chunk + 1, j)
    for j in range(st.dn_slabs):
        ffn_high_dn(c, act, st, 0, j)
    ffn_schedule(act, st, gate_up, down)


def ffn_row(c, dve, st, chunk, q):
    if not isinstance(chunk, int) or chunk >= 2:
        dve.wait_ge(c.sem(st.name + "_gu_units"), (chunk - 2) * (2 * st.blocks + 1) + 1)
    e, n = st.experts, st.tokens
    if isinstance(chunk, int) and chunk == 0:
        dve.tensor_copy(st.ones[:, :], c.ones[0:e, :]).then_inc(c.sem(st.name + "_ones"), 1)
    column = (c.identity[0:e, chunk:chunk + 1] if isinstance(chunk, int)
              else c.identity[0:e, bass.DynSlice(chunk, 1)])
    dve.tensor_scalar(st.row_hi[0:e, q, 0:n], st.expert_weights[0:e, 0:n], column, None,
                      ALU.mult).then_inc(c.sem(st.name + "_row_hi"), 1)
    dve.wait_ge(c.sem(st.name + "_row_hi"), chunk + 1)
    c.apart(dve)
    dve.scalar_tensor_tensor(st.row_lo[0:e, q, 0:n], st.expert_weights[0:e, 0:n], column, st.row_hi[0:e, q, 0:n],
                             ALU.mult, ALU.subtract).then_inc(c.sem(st.name + "_row"), 1)


def ffn_dve(c, dve, st):
    nb, n = st.blocks, st.tokens
    first = 1 if st.scale != "none" else 0
    silu_done = c.sem(st.name + ("_silu" if st.scale == "before" else "_g_read"))

    def gate_up(chunk, q):
        units = chunk * (2 * nb + first) + first

        def finish(j):
            b = (q * nb + j) % 2
            dve.wait_ge(silu_done, chunk * nb + j + 1)
            if st.scale == "none":
                dve.wait_ge(c.sem(st.name + "_gu_units"), units + 2 * j + 2)
                if not (isinstance(chunk, int) and chunk == 0 and j < 2):
                    dve.wait_ge(c.sem(st.name + "_h_hi"), chunk * nb + j - 1)
                    dve.wait_ge(c.sem(st.name + "_h_lo"), chunk * nb + j - 1)
                dve.tensor_tensor(st.cut(st.h[:, b, 0:n]), st.cut(st.silu[:, b, 0:n]), st.span(c, 2),
                                  ALU.mult).then_inc(c.sem(st.name + "_h"), 1)
            else:
                if not (isinstance(chunk, int) and chunk == 0 and j < 2):
                    dve.wait_ge(c.sem(st.name + "_h_hi"), chunk * nb + j - 1)
                    dve.wait_ge(c.sem(st.name + "_h_lo"), chunk * nb + j - 1)
                dve.wait_ge(c.sem(st.name + "_u_read"), chunk * nb + j + 1)
                dve.tensor_tensor(st.h[:, b, 0:n], st.silu[:, b, 0:n], st.up[:, b, 0:n],
                                  ALU.mult).then_inc(c.sem(st.name + "_h"), 1)

        def split_low(j):
            b = (q * nb + j) % 2
            dve.wait_ge(c.sem(st.name + "_h_hi"), chunk * nb + j + 1)
            dve.tensor_tensor(st.h_lo[:, q, j, 0:n], st.h[:, b, 0:n], st.h_hi[:, q, j, 0:n],
                              ALU.subtract).then_inc(c.sem(st.name + "_h_lo"), 1)
        if first:
            ffn_row(c, dve, st, chunk + 1, 1 - q)
            dve.wait_ge(c.sem(st.name + "_scale_copied"), chunk + 1)
        for j in range(nb):
            b = (q * nb + j) % 2
            if st.scale == "before":
                dve.wait_ge(c.sem(st.name + "_gu_units"), units + 2 * j + 1)
                if not (isinstance(chunk, int) and chunk == 0 and j < 2):
                    dve.wait_ge(c.sem(st.name + "_silu"), chunk * nb + j - 1)
                dve.tensor_tensor(st.cut(st.gate[:, b, 0:n]), st.cut(st.scales[:, 0:n]), st.span(c, 0),
                                  ALU.mult).then_inc(c.sem(st.name + "_gate_scaled"), 1)
            if first:
                dve.wait_ge(c.sem(st.name + "_gu_units"), units + 2 * j + 2)
                dve.tensor_tensor(st.cut(st.up[:, b, 0:n]), st.cut(st.scales[:, 0:n]), st.span(c, 2),
                                  ALU.mult).then_inc(c.sem(st.name + "_u_read"), 1)
            finish(j)
            if j:
                split_low(j - 1)
        split_low(nb - 1)

    def down(chunk, q):
        for m in range(KD):
            dve.wait_ge(c.sem(st.name + "_dn_units"), chunk * KD + m + 1)
            if not (isinstance(chunk, int) and chunk == 0):
                dve.wait_ge(c.sem(st.name + "_added"), (chunk - 1) * KD + m + 1)
            into = st.cut(c.residual[:, m, 0:n])
            dve.tensor_tensor(into, into, st.span(c, 4 + 2 * (m % 2)), ALU.add).then_inc(
                c.sem(st.name + "_added"), 1)
    if st.scale == "before":
        ffn_row(c, dve, st, 0, 0)
    ffn_schedule(dve, st, gate_up, down)
    dve.wait_ge(c.sem(st.name + "_added"), st.chunks * KD)
    dve.nop().then_inc(c.sem("residual_ready"), 1)



class RoutedFfn(Ffn):
    ROUTED, TOP = 8, 2

    def buffers(self, c, own):
        super().buffers(c, own)
        n, e = self.name, self.ROUTED
        self.router = c.sb(own, n + "_router", [P, KD, e])
        self.router_hi, self.router_lo = (c.sb(own, n + x, [P, KD, e], F32R) for x in ("_router_hi", "_router_lo"))
        self.logits = c.sb(own, n + "_logits", [S, B, e])
        self.sigmoid = c.sb(own, n + "_sigmoid", [S, B, e])
        self.above = c.sb(own, n + "_above", [S, B, e, e])
        self.equal = c.sb(own, n + "_equal", [S, B, e, e])
        self.earlier = c.sb(own, n + "_earlier", [S, e, e])
        self.rank = c.sb(own, n + "_rank", [S, B, e])
        self.probs = c.sb(own, n + "_probs", [S, B, e + 1])

    def sync(self, c, sp):
        sp.wait_ge(c.sem("residual_ready"), self.index + 1)
        sp.dma_start(self.router[:, :, :], c.a["router"]).then_inc(c.sem(self.name + "_router_landed"), 16)
        sp.dma_start(self.earlier[:, :, :], c.a["earlier"]).then_inc(c.sem(self.name + "_earlier_landed"), 16)
        super().sync(c, sp)

    def act_before_std(self, c, act):
        act.wait_ge(c.sem(self.name + "_router_landed"), 16)
        act.activation(self.router_hi[:, :, :], self.router[:, :, :], ACT.Copy).then_inc(
            c.sem(self.name + "_router_split"), 1)

    def pool(self, c, pool):
        pool.wait_ge(c.sem(self.name + "_router_split"), 1)
        pool.tensor_tensor(self.router_lo[:, :, :], self.router[:, :, :], self.router_hi[:, :, :],
                           ALU.subtract).then_inc(c.sem(self.name + "_router_split"), 1)
        super().pool(c, pool)

    def prepare_pe(self, c, pe):
        pe.wait_ge(c.sem(self.name + "_router_split"), 2)
        for b in range(B):
            t = slice(b * S, (b + 1) * S)
            wait_for_input(c, pe, self, b // 2 + 1)
            for k in range(KD):
                mm = product(pe, [c.psum[0:S, 4, b * self.ROUTED:(b + 1) * self.ROUTED]], c.xn_hi[:, k, t],
                             c.xn_lo[:, k, t], [(self.router_hi[:, k, :], self.router_lo[:, k, :])],
                             k == 0, k == KD - 1)
        mm.then_inc(c.sem(self.name + "_logits"), 1)
        pe.wait_ge(c.sem(self.name + "_probs"), 2)
        for b in range(B):
            mm = pe.transpose(c.psum[0:self.experts, 6 + b // 4, b % 4 * S:(b % 4 + 1) * S],
                              self.probs[:, b, :], c.identity[0:S, 0:S])
        mm.then_inc(c.sem(self.name + "_probs_turned"), 1)

    def prepare_act(self, c, act):
        act.wait_ge(c.sem(self.name + "_logits_copied"), 1)
        act.activation(self.sigmoid[:, :, :], self.logits[:, :, :], ACT.Sigmoid).then_inc(
            c.sem(self.name + "_sigmoid"), 1)

    def prepare_dve(self, c, dve):
        e, step = self.ROUTED, c.sem(self.name + "_ranking")
        dve.wait_ge(c.sem(self.name + "_logits"), 1)
        dve.tensor_copy(self.logits[:, :, :], c.psum[0:S, 4, 0:B * e].rearrange("s (b e) -> s b e", b=B)).then_inc(
            c.sem(self.name + "_logits_copied"), 1)
        dve.wait_ge(c.sem(self.name + "_logits_copied"), 1)
        other = self.logits[:, :, :].unsqueeze(2).broadcast_to([S, B, e, e])
        mine = self.logits[:, :, :].unsqueeze(3).broadcast_to([S, B, e, e])
        dve.tensor_tensor(self.above[:, :, :, :], other, mine, ALU.is_gt).then_inc(step, 1)
        dve.tensor_tensor(self.equal[:, :, :, :], other, mine, ALU.is_equal).then_inc(step, 1)
        dve.wait_ge(c.sem(self.name + "_earlier_landed"), 16)
        dve.wait_ge(step, 2)
        dve.tensor_tensor(self.equal[:, :, :, :], self.equal[:, :, :, :],
                          self.earlier[:, :, :].unsqueeze(1).broadcast_to([S, B, e, e]), ALU.mult).then_inc(step, 1)
        dve.wait_ge(step, 3)
        dve.tensor_tensor(self.above[:, :, :, :], self.above[:, :, :, :], self.equal[:, :, :, :],
                          ALU.add).then_inc(step, 1)
        dve.wait_ge(step, 4)
        dve.tensor_reduce(self.rank[:, :, :], self.above[:, :, :, :], AX.X, ALU.add).then_inc(step, 1)
        dve.memset(self.probs[:, :, e:e + 1], 1.0).then_inc(c.sem(self.name + "_probs"), 1)
        dve.wait_ge(step, 5)
        dve.wait_ge(c.sem(self.name + "_sigmoid"), 1)
        dve.scalar_tensor_tensor(self.probs[:, :, 0:e], self.rank[:, :, :], float(self.TOP), self.sigmoid[:, :, :],
                                 ALU.is_lt, ALU.mult).then_inc(c.sem(self.name + "_probs"), 1)
        dve.wait_ge(c.sem(self.name + "_probs_turned"), 1)
        dve.tensor_copy(self.cut(self.expert_weights[:, :]), c.psum[0:self.experts, 6:8, 0:HALF]).then_inc(
            c.sem(self.name + "_weights"), 1)
        dve.wait_ge(c.sem(self.name + "_weights"), 1)


class ChosenFfn(Ffn):
    NAMES = 4

    def buffers(self, c, own):
        super().buffers(c, own)
        n, g = self.name, self.tokens // P
        self.groups = g

    def early_buffers(self, c, ctx):
        n, g = self.name, self.tokens // P
        self.names = c.sb(ctx, n + "_names", [P, g, self.NAMES], I32)
        self.names_f = c.sb(ctx, n + "_names_f", [P, g, self.NAMES])
        self.name_weights = c.sb(ctx, n + "_name_weights", [P, g, self.NAMES])
        self.expert_ids = c.sb(ctx, n + "_expert_ids", [P, self.experts])
        self.matches = c.ln_squares[:, :, :].rearrange("p k t -> p (k t)")[:, 0:g * self.NAMES * self.experts].rearrange(
            "p (g k e) -> p g k e", g=g, k=self.NAMES)
        self.token_weights = c.sb(ctx, n + "_token_weights", [P, g, self.experts])

    def early_sync(self, c, sp):
        for name, buffer in (("names", self.names), ("name_weights", self.name_weights)):
            sp.dma_start(buffer[:, :, :], c.a[name]).then_inc(c.sem(f"{name}_landed"), 16)
        sp.dma_start(self.expert_ids[:, :], c.a["expert_ids"]).then_inc(c.sem("expert_ids_landed"), 16)

    def early_dve(self, c, dve):
        dve.wait_ge(c.sem("names_landed"), 16)
        dve.wait_ge(c.sem("name_weights_landed"), 16)
        dve.wait_ge(c.sem("expert_ids_landed"), 16)
        dve.tensor_copy(self.names_f[:, :, :], self.names[:, :, :]).then_inc(c.sem("names_f"), 1)
        dve.wait_ge(c.sem("names_f"), 1)
        for g in range(self.groups):
            for k in range(self.NAMES):
                dve.tensor_scalar(self.matches[:, g, k, :], self.expert_ids[:, :], self.names_f[:, g, k:k + 1],
                                  self.name_weights[:, g, k:k + 1], ALU.is_equal, ALU.mult).then_inc(
                                      c.sem("name_matches"), 1)
        dve.wait_ge(c.sem("name_matches"), self.groups * self.NAMES)
        dve.tensor_reduce(self.token_weights[:, :, :], self.matches[:, :, :, :].rearrange("p g k e -> p g e k"),
                          AX.X, ALU.add).then_inc(c.sem("token_weights"), 1)

    def prepare_pe(self, c, pe):
        pe.wait_ge(c.sem("token_weights"), 1)
        wait_for_banks(c, pe, self)
        for g in range(self.groups):
            mm = pe.transpose(c.psum[0:self.experts, 6, g * P:(g + 1) * P], self.token_weights[:, g, :],
                              c.identity[:, :])
        mm.then_inc(c.sem(self.name + "_turned"), 1)

    def dve_before_last_quarter(self, c, dve):
        dve.wait_ge(c.sem(self.name + "_turned"), 1)
        dve.tensor_copy(self.expert_weights[:, :], c.psum[0:self.experts, 6, 0:self.tokens]).then_inc(
            c.sem(self.name + "_weights"), 1)
        dve.wait_ge(c.sem(self.name + "_weights"), 1)
        ffn_row(c, dve, self, 0, 0)



HEADS, HD = 16, 32
GROUP = P // HD
KEY_TILES = [(0, P), (P, 2 * P), (2 * P, C)]


def batches(engine, body):
    turns = (B - 4) // 2
    body(0, 0, True, True)
    with engine.Fori(0, turns) as i:
        body(i * 2 + 1, 1, True, True)
        body(i * 2 + 2, 0, True, True)
    for b in range(2 * turns + 1, B):
        body(b, b % 2, b + 1 < B, b + 2 < B)


def tokens_of(b):
    return slice(b * S, (b + 1) * S) if isinstance(b, int) else bass.DynSlice(b * S, S)


class Attention:
    SPLIT_INPUT, FREE_BANKS = True, 4
    K_AT, V_AT, Q_AT = 4, 8, 0
    RAW = 6
    VALUES_BANK = 7
    SCALE = 1.0 / float(HD) ** 0.5

    def __init__(self, name, index, slabs_at):
        self.name, self.index, self.slabs_at = name, index, slabs_at
        self.places = ([self.K_AT + j for j in range(4)] + [self.V_AT + j for j in range(4)]
                       + [self.Q_AT + j for j in range(4)] + [self.Q_AT + j for j in range(4)])
        self.biases = ["bq", "bk", "bo"]

    def buffers(self, c, own):
        n = self.name
        self.c = c
        self.w_hi, self.w_lo = (c.sb(own, n + x, [P, 12, 512], F32R) for x in ("_w_hi", "_w_lo"))
        self.out_raw = c.sb(own, n + "_out_raw", [P, 2, 512])
        self.ctx_hi, self.ctx_lo = (c.sb(own, n + x, [P, 2, KD, CP], F32R) for x in ("_ctx_hi", "_ctx_lo"))
        self.k_hi, self.k_lo = (c.sb(own, n + x, [P, 2, KD, CP], F32R) for x in ("_k_hi", "_k_lo"))
        self.v = c.sb(own, n + "_v", [P, 2, 3, D])
        self.bv = c.sb(own, n + "_bv", [P, D])
        self.vectors = c.sb(own, n + "_vectors", [P, len(self.biases), KD])
        self.ctx_raw = c.sb(own, n + "_ctx_raw", [P, KD, CP])
        with ExitStack() as start:
            self.w_raw = c.sb(start, n + "_w_raw", [P, self.RAW, 512])
        self.own_buffers(c, own)

    def own_buffers(self, c, own):
        n = self.name
        self.qm_hi, self.qm_lo = (c.sb(own, n + x, [P, HEADS, S], F32R) for x in ("_qm_hi", "_qm_lo"))
        self.probs = c.sb(own, n + "_probs", [S, GROUP, C])
        self.highest = c.sb(own, n + "_highest", [S, GROUP])
        self.shift = c.sb(own, n + "_shift", [S, GROUP])
        self.total = c.sb(own, n + "_total", [S, GROUP])
        self.inverse = c.sb(own, n + "_inverse", [S, GROUP])

    def turned(self, c):
        return c.ln_squares[:, :, :].rearrange("p k t -> p (k t)")[:, 0:3 * GROUP * S].rearrange(
            "p (t n) -> p t n", t=3)

    def s(self, name):
        return self.c.sem(f"{self.name}_{name}")

    def raw(self, i):
        return self.w_raw[:, i % self.RAW, :] if i < 12 else self.out_raw[:, i % 2, :]

    def landed(self, i):
        if i < 12:
            return self.s(f"w_landed{i % self.RAW}"), 16 * (i // self.RAW + 1)
        return self.s(f"out_w_landed{i % 2}"), 16 * ((i - 12) // 2 + 1)

    def bias(self, name, m):
        return self.vectors[:, self.biases.index(name), m:m + 1]

    def slab(self, c, sp, i):
        sp.dma_start(self.raw(i), c.slabs[self.slabs_at + i, :, :]).then_inc(self.landed(i)[0], 16)

    def prefetch(self, c, sp):
        wait(sp, c.sem("residual_ready"), self.index)
        sp.dma_start(self.ctx_raw[:, :, :], c.a["ctx"][0, :, :, :]).then_inc(self.s("ctx_landed"), 16)
        for i in range(self.RAW):
            self.slab(c, sp, i)

    def nearly_over(self, c, sp):
        sp.wait_ge(self.s("o_lo"), B * KD)

    def sync(self, c, sp):
        sp.wait_ge(c.sem("residual_ready"), self.index + 1)
        for i in range(self.RAW - 1, 14):
            if i == self.RAW - 1:
                sp.dma_start(self.vectors[:, :, :], c.a[self.name + "_vectors"]).then_inc(self.s("vectors_landed"), 16)
                sp.dma_start(self.bv[:, :], c.a[self.name + "_bv"]).then_inc(self.s("bv_landed"), 16)
                self.sync_more(c, sp)
                continue
            if i == 12:
                sp.wait_ge(self.s("ctx_split"), 1)
                sp.dma_start(self.ctx_raw[:, :, :], c.a["ctx"][1, :, :, :]).then_inc(self.s("ctx_landed"), 16)
            if i < 12:
                wait(sp, self.s("w_split"), i - self.RAW + 1)
            self.slab(c, sp, i)

        def body(b, q, more, two_more):
            if two_more:
                sp.wait_ge(self.s("ctx_split"), b + 2)
                sp.dma_start(self.ctx_raw[:, :, :], c.a["ctx"][bass.DynSlice(b + 2, 1), :, :, :].rearrange(
                    "a p k t -> p (a k) t") if not isinstance(b, int) else c.a["ctx"][b + 2, :, :, :]).then_inc(
                        self.s("ctx_landed"), 16)
            if isinstance(b, int) and b == 0:
                for i in (14, 15):
                    sp.wait_ge(self.s("w_split"), i - 1)
                    self.slab(c, sp, i)
        batches(sp, body)

    def sync_more(self, c, sp):
        pass

    def split_weight(self, pool, i):
        pool.wait_ge(self.s("w_hi"), i + 1)
        pool.tensor_tensor(self.w_lo[:, self.places[i], :], self.raw(i),
                           self.w_hi[:, self.places[i], :], ALU.subtract).then_inc(self.s("w_split"), 1)

    def split_weight_high(self, act, i):
        act.wait_ge(*self.landed(i))
        act.activation(self.w_hi[:, self.places[i], :], self.raw(i), ACT.Copy).then_inc(
            self.s("w_hi"), 1)

    def pool(self, c, pool):
        pool.wait_ge(c.sem("residual_ready"), self.index + 1)
        self.split_context(pool, 0, 0)
        for i in range(12):
            self.split_weight(pool, i)
        pool.wait_ge(self.s("w_split"), 12)
        self.pool_start(c, pool)
        self.split_context(pool, 1, 1)
        self.split_weight(pool, 12)

        def body(b, q, more, two_more):
            if two_more:
                self.split_context(pool, b + 2, q)
            if isinstance(b, int) and b == 0:
                for i in range(13, 16):
                    self.split_weight(pool, i)
        batches(pool, body)

    def pool_start(self, c, pool):
        for buffer in (self.qm_hi, self.qm_lo):
            pool.memset(buffer[:, :, :].bitcast(F32), 0.0).then_inc(self.s("qm_zero"), 1)

    def split_output_weights(self, act, b, m):
        if isinstance(b, int) and b == 0:
            self.split_weight_high(act, 12 + m)

    def split_context(self, pool, b, q):
        pool.wait_ge(self.s("ctx_hi"), b + 1)
        pool.tensor_tensor(self.ctx_lo[:, q, :, :], self.ctx_raw[:, :, :], self.ctx_hi[:, q, :, :],
                           ALU.subtract).then_inc(self.s("ctx_split"), 1)

    def split_context_high(self, act, b, q):
        act.wait_ge(self.s("ctx_landed"), 16 * (b + 1))
        if not isinstance(b, int) or b >= 2:
            act.wait_ge(self.s("k_units"), 4 * (b - 1))
            act.wait_ge(self.s("v_units"), 3 * (b - 1))
        act.activation(self.ctx_hi[:, q, :, :], self.ctx_raw[:, :, :], ACT.Copy).then_inc(self.s("ctx_hi"), 1)

    def keys_bank(self, b, m):
        return m if isinstance(b, int) and b == 0 else 7

    def pe_keys(self, pe, b, q, m):
        c = self.c
        if m == 0:
            pe.wait_ge(self.s("ctx_split"), b + 1)
            wait(pe, self.s("v_added"), 3 * b)
        if isinstance(b, int) and b == 0:
            pass
        elif m == 0 or self.VALUES_BANK != 7:
            wait(pe, self.s("k_lo"), 4 * b + m)
        else:
            pe.wait_ge(self.s("v_added"), 3 * b + m)
        if isinstance(b, int) and b == 0:
            pe.wait_ge(self.s("w_split"), m + 1)
        for k in range(KD):
            w = slice(k * P, (k + 1) * P)
            mm = product(pe, [c.psum[:, self.keys_bank(b, m), 0:CP]], self.w_hi[:, self.K_AT + m, w], self.w_lo[:, self.K_AT + m, w],
                         [(self.ctx_hi[:, q, k, :], self.ctx_lo[:, q, k, :])], k == 0, k == KD - 1)
        mm.then_inc(self.s("k_units"), 1)

    def pe_values(self, pe, b, q, m):
        c, (a, z) = self.c, KEY_TILES[m]
        if self.VALUES_BANK == 7 and not (isinstance(b, int) and b == 0):
            pe.wait_ge(self.s("k_lo"), 4 * b + m + 1)
        else:
            wait(pe, self.s("v_added"), 3 * b + m)
        if isinstance(b, int) and b == 0:
            pe.wait_ge(self.s("w_split"), 8)
        for k in range(KD):
            mm = product(pe, [c.psum[0:z - a, self.VALUES_BANK, :]], self.ctx_hi[:, q, k, a:z], self.ctx_lo[:, q, k, a:z],
                         [(self.w_hi[:, self.V_AT + k, :], self.w_lo[:, self.V_AT + k, :])], k == 0, k == KD - 1)
        mm.then_inc(self.s("v_units"), 1)

    def act_keys(self, act, b, q, m):
        act.wait_ge(self.s("k_units"), 4 * b + m + 1)
        act.activation(self.k_hi[:, q, m, :], self.c.psum[:, self.keys_bank(b, m), 0:CP], ACT.Identity,
                       bias=self.bias("bk", m)).then_inc(
            self.s("k_hi"), 1)

    def dve_keys(self, dve, b, q, m):
        dve.wait_ge(self.s("k_hi"), 4 * b + m + 1)
        dve.scalar_tensor_tensor(self.k_lo[:, q, m, :], self.c.psum[:, self.keys_bank(b, m), 0:CP], self.bias("bk", m),
                                 self.k_hi[:, q, m, :], ALU.add, ALU.subtract).then_inc(self.s("k_lo"), 1)

    def dve_values(self, dve, b, q, m):
        a, z = KEY_TILES[m]
        dve.wait_ge(self.s("v_units"), 3 * b + m + 1)
        dve.tensor_tensor(self.v[0:z - a, q, m, :], self.c.psum[0:z - a, self.VALUES_BANK, :], self.bv[0:z - a, :],
                          ALU.add).then_inc(self.s("v_added"), 1)

    def pe_project(self, pe, units, freed, moving):
        c = self.c
        for m in range(KD):
            bank = 2 * (m % 2)
            wait(pe, self.s(freed), m - 1)
            for k in range(KD):
                w = slice(k * P, (k + 1) * P)
                mm = product(pe, [c.psum[:, bank + h, 0:HALF] for h in range(2)], self.w_hi[:, self.Q_AT + m, w],
                             self.w_lo[:, self.Q_AT + m, w],
                             [tuple(x[:, k, h * HALF:(h + 1) * HALF] for x in moving) for h in range(2)],
                             k == 0, k == KD - 1)
            mm.then_inc(self.s(units), 1)

    def pe(self, c, pe):
        ln_pe(c, pe, self)
        wait_for_banks(c, pe, self)
        for m in range(KD):
            self.pe_keys(pe, 0, 0, m)
        for m in range(3):
            self.pe_values(pe, 0, 0, m)
        pe.wait_ge(self.s("k_lo"), KD)
        wait_for_input(c, pe, self)
        pe.wait_ge(self.s("w_split"), 12)
        self.pe_project(pe, "q_units", "q_copied", (c.xn_hi, c.xn_lo))
        self.pe_start(c, pe)
        batches(pe, lambda b, q, more, two_more: self.pe_batch(c, pe, b, q, more))
        self.pe_after_batches(c, pe)
        pe.wait_ge(self.s("o_lo"), B * KD)
        pe.wait_ge(self.s("w_split"), 16)
        self.pe_project(pe, "out_units", "out_read", (c.xn_hi, c.xn_lo))
        self.pe_finish(c, pe)
        ln_mean_pe(c, pe, self.index + 1, lambda k: self.tile_added(pe, k))

    def tile_added(self, pe, k):
        pe.wait_ge(self.s("out_read"), k + 1)

    def pe_start(self, c, pe):
        pe.wait_ge(self.s("q_copied"), KD)
        self.pe_first_scores(c, pe)

    def pe_first_scores(self, c, pe):
        self.pe_scores(c, pe, 0, 0, 0)

    def pe_after_batches(self, c, pe):
        pass

    def pe_finish(self, c, pe):
        pass

    def act(self, c, act):
        def first_parts():
            self.split_context_high(act, 0, 0)
            self.split_weight_high(act, 0)

        def next_parts(n):
            for i in range(2 * n + 1, min(2 * n + 3, 8)):
                self.split_weight_high(act, i)
        ln_act(c, act, self, first_parts, next_parts)
        act.wait_ge(self.s("vectors_landed"), 16)
        for m in range(KD):
            self.act_keys(act, 0, 0, m)
            self.split_weight_high(act, 8 + m)
        self.split_context_high(act, 1, 1)
        for m in range(KD):
            bank = 2 * (m % 2)
            act.wait_ge(self.s("q_units"), m + 1)
            act.activation(c.xn[:, m, :].rearrange("p (h t) -> p h t", h=2), c.psum[:, bank:bank + 2, 0:HALF],
                           ACT.Identity, bias=self.bias("bq", m)).then_inc(self.s("q_copied"), 1)
        self.act_start(c, act)
        self.act_before_batches(c, act)
        batches(act, lambda b, q, more, two_more: self.act_batch(c, act, b, q, more, two_more))
        self.act_finish(c, act)

    def act_start(self, c, act):
        act.wait_ge(self.s("qm_zero"), 2)
        act.wait_ge(self.s("q_copied"), KD)
        self.act_queries(c, act, 0)

    def act_finish(self, c, act):
        pass

    def act_queries(self, c, act, b):
        for g in range(GROUP):
            rows = slice(g * HD, (g + 1) * HD)
            act.activation(self.qm_hi[rows, g:HEADS:GROUP, :], c.xn[rows, :, tokens_of(b)], ACT.Copy).then_inc(
                self.s("qm_hi"), 1)

    def dve_queries(self, c, dve, b):
        for g in range(GROUP):
            rows = slice(g * HD, (g + 1) * HD)
            dve.wait_ge(self.s("qm_hi"), b * 4 + g + 1)
            dve.tensor_tensor(self.qm_lo[rows, g:HEADS:GROUP, :], c.xn[rows, :, tokens_of(b)],
                              self.qm_hi[rows, g:HEADS:GROUP, :], ALU.subtract).then_inc(self.s("qm_lo"), 1)

    def dve(self, c, dve):
        ln_dve(c, dve, self)
        dve.wait_ge(self.s("vectors_landed"), 16)
        dve.wait_ge(self.s("bv_landed"), 16)
        for m in range(KD):
            self.dve_keys(dve, 0, 0, m)
        for m in range(3):
            self.dve_values(dve, 0, 0, m)
        self.dve_start(c, dve)
        self.dve_before_batches(c, dve)
        batches(dve, lambda b, q, more, two_more: self.dve_batch(c, dve, b, q, more))
        self.dve_finish(c, dve)
        dve.nop().then_inc(c.sem("residual_ready"), 1)

    def dve_start(self, c, dve):
        dve.wait_ge(self.s("qm_zero"), 2)
        self.dve_queries(c, dve, 0)

    def dve_finish(self, c, dve):
        for m in range(KD):
            bank = 2 * (m % 2)
            dve.wait_ge(self.s("out_units"), m + 1)
            into = c.residual[:, m, :].rearrange("p (h t) -> p h t", h=2)
            dve.scalar_tensor_tensor(into, c.psum[:, bank:bank + 2, 0:HALF], self.bias("bo", m), into,
                                     ALU.add, ALU.add).then_inc(self.s("out_read"), 1)
        dve.wait_ge(self.s("out_read"), KD)

    def pe_batch(self, c, pe, b, q, more):
        turned = self.turned(c)
        for m in range(KD):
            i = b * 4 + m
            if more:
                self.pe_keys(pe, b + 1, 1 - q, m)
            if m < 3:
                self.pe_scores(c, pe, b, q, m + 1)
            elif more:
                self.pe_scores(c, pe, b + 1, 1 - q, 0)
            pe.wait_ge(self.s("normalised"), i * GROUP + GROUP)
            wait(pe, self.s("turned_01"), i)
            wait(pe, self.s("turned_2"), i)
            for g in range(GROUP):
                for t, (a, z) in enumerate(KEY_TILES):
                    mm = pe.transpose(c.psum[0:z - a, 4 + t, g * S:(g + 1) * S], self.probs[:, g, a:z],
                                      c.identity[0:S, 0:S])
            mm.then_inc(self.s("t_units"), 1)
            if more and m < 3:
                self.pe_values(pe, b + 1, 1 - q, m)
            pe.wait_ge(self.s("turned_01"), i + 1)
            pe.wait_ge(self.s("turned_2"), i + 1)
            if m == 0:
                pe.wait_ge(self.s("v_added"), b * 3 + 3)
            wait(pe, self.s("o_lo"), i - 1)
            for g in range(GROUP):
                head = slice((m * GROUP + g) * HD, (m * GROUP + g + 1) * HD)
                for t, (a, z) in enumerate(KEY_TILES):
                    mm = pe.matmul(c.psum[g * HD:(g + 1) * HD, 4 + m % 2, 400:400 + S], self.v[0:z - a, q, t, head],
                                   turned[0:z - a, t, g * S:(g + 1) * S], start=t == 0, stop=t == 2)
            mm.then_inc(self.s("pv_units"), 1)

    def pe_scores(self, c, pe, b, q, m):
        i = b * 4 + m
        if m == 0:
            pe.wait_ge(self.s("qm_hi"), b * 4 + 4)
            pe.wait_ge(self.s("qm_lo"), b * 4 + 4)
        pe.wait_ge(self.s("k_lo"), i + 1)
        wait(pe, self.s("exps"), i * GROUP)
        for g in range(GROUP):
            mm = product(pe, [c.psum[0:S, g, 0:CP]], self.qm_hi[:, m * GROUP + g, :], self.qm_lo[:, m * GROUP + g, :],
                         [(self.k_hi[:, q, m, :], self.k_lo[:, q, m, :])], True, True)
        mm.then_inc(self.s("s_units"), 1)

    def act_exps(self, c, act, i):
        act.wait_ge(self.s("shifts"), i + 1)
        wait(act, self.s("t_units"), i)
        for g in range(GROUP):
            act.activation(self.probs[:, g, :], c.psum[0:S, g, 0:C], ACT.Exp, bias=self.shift[:, g:g + 1],
                           scale=self.SCALE, accum_out=self.total[:, g:g + 1]).then_inc(self.s("exps"), 1)

    def act_before_batches(self, c, act):
        self.act_exps(c, act, 0)

    def dve_before_batches(self, c, dve):
        self.dve_maxima(c, dve, 0)

    def act_batch(self, c, act, b, q, more, two_more):
        turned = self.turned(c)
        for m in range(KD):
            i = b * 4 + m
            if more:
                self.act_keys(act, b + 1, 1 - q, m)
            if two_more and m == 1:
                self.split_context_high(act, b + 2, q)
            act.wait_ge(self.s("t_units"), i + 1)
            wait(act, self.s("pv_units"), i)
            act.activation(turned[:, 0:2, :], c.psum[:, 4:6, 0:GROUP * S], ACT.Copy).then_inc(self.s("turned_01"), 1)
            if more and m == 2:
                act.wait_ge(self.s("s_units"), b * 4 + 4)
                self.act_queries(c, act, b + 1)
            if m < 3 or more:
                self.act_exps(c, act, i + 1)
            act.wait_ge(self.s("pv_units"), i + 1)
            act.activation(c.xn_hi[:, m, tokens_of(b)], c.psum[:, 4 + m % 2, 400:400 + S], ACT.Copy).then_inc(
                self.s("o_hi"), 1)
            self.split_output_weights(act, b, m)

    def dve_maxima(self, c, dve, i):
        dve.wait_ge(self.s("s_units"), i + 1)
        dve.tensor_reduce(self.highest[:, :], c.psum[0:S, 0:GROUP, 0:C], AX.X, ALU.max).then_inc(self.s("maxima"), 1)
        dve.wait_ge(self.s("maxima"), i + 1)
        dve.tensor_scalar(self.shift[:, :], self.highest[:, :], -self.SCALE, None, ALU.mult).then_inc(self.s("shifts"), 1)

    def dve_batch(self, c, dve, b, q, more):
        turned = self.turned(c)
        for m in range(KD):
            i = b * 4 + m
            dve.wait_ge(self.s("exps"), i * GROUP + GROUP)
            dve.reciprocal(self.inverse[:, :], self.total[:, :]).then_inc(self.s("inverses"), 1)
            dve.wait_ge(self.s("inverses"), i + 1)
            for g in range(GROUP):
                dve.tensor_scalar(self.probs[:, g, :], self.probs[:, g, :], self.inverse[:, g:g + 1], None,
                                  ALU.mult).then_inc(self.s("normalised"), 1)
            if more:
                self.dve_keys(dve, b + 1, 1 - q, m)
            n = KEY_TILES[2][1] - KEY_TILES[2][0]
            dve.wait_ge(self.s("t_units"), i + 1)
            wait(dve, self.s("pv_units"), i)
            dve.tensor_copy(turned[0:n, 2, :], c.psum[0:n, 6, 0:GROUP * S]).then_inc(self.s("turned_2"), 1)
            if m < 3 or more:
                self.dve_maxima(c, dve, i + 1)
            if more and m < 3:
                self.dve_values(dve, b + 1, 1 - q, m)
            if more and m == 2:
                self.dve_queries(c, dve, b + 1)
            dve.wait_ge(self.s("o_hi"), i + 1)
            dve.tensor_tensor(c.xn_lo[:, m, tokens_of(b)], c.psum[:, 4 + m % 2, 400:400 + S],
                              c.xn_hi[:, m, tokens_of(b)], ALU.subtract).then_inc(self.s("o_lo"), 1)



class BoundedAttention(Attention):
    BOUND = 50.0
    EPS = 1e-8
    SCALE_MAX = 0.3

    def __init__(self, name, index, slabs_at):
        super().__init__(name, index, slabs_at)
        self.biases = ["bq", "bk", "bo", "gamma", "beta"]

    def own_buffers(self, c, own):
        n = self.name
        self.qm_hi, self.qm_lo = (c.sb(own, n + x, [P, HEADS, S], F32R) for x in ("_qm_hi", "_qm_lo"))
        self.clipped = c.sb(own, n + "_clipped", [P, 3, GROUP * S])
        self.mask = c.sb(own, n + "_mask", [P, 3, B], I32)
        self.key_scale, self.key_shift = (c.sb(own, n + x, [P, 3, B]) for x in ("_key_scale", "_key_shift"))
        self.out_scale = c.sb(own, n + "_out_scale", [P, 1])
        self.norm = c.sb(own, n + "_norm", [P, 2, S])
        self.o = c.sb(own, n + "_o", [P, 2, S])

    def exps(self, c, m):
        return c.ln_squares[:, :, :].rearrange("p k t -> p (k t)")[:, m % 2 * 1200:m % 2 * 1200 + 1200].rearrange(
            "p (t n) -> p t n", t=3)

    def tile_added(self, pe, k):
        pe.wait_ge(self.s("delta"), 2 + KD + k + 1)

    def sync_more(self, c, sp):
        sp.dma_start(self.mask[:, :, :], c.a["context_mask"]).then_inc(self.s("mask_landed"), 16)
        sp.dma_start(self.out_scale[:, :], c.a["out_scale"]).then_inc(self.s("out_scale_landed"), 16)

    def pe_batch(self, c, pe, b, q, more):
        for m in range(KD):
            i = b * 4 + m
            if more:
                self.pe_keys(pe, b + 1, 1 - q, m)
            if m < 3:
                self.pe_scores(c, pe, b, q, m + 1)
            elif more:
                self.pe_scores(c, pe, b + 1, 1 - q, 0)
            if more and m < 3:
                self.pe_values(pe, b + 1, 1 - q, m)
            pe.wait_ge(self.s("exps"), i * 3 + 3)
            if m == 0:
                pe.wait_ge(self.s("v_added"), b * 3 + 3)
            wait(pe, self.s("o"), i)
            exps = self.exps(c, m)
            for g in range(GROUP):
                head = slice((m * GROUP + g) * HD, (m * GROUP + g + 1) * HD)
                for x in range(2):
                    for t, (a, z) in enumerate(KEY_TILES):
                        at = m % 2 * 200 + x * S
                        mm = pe.matmul(c.psum[g * HD:(g + 1) * HD, 6, at:at + S],
                                       c.ones[0:z - a, 0:HD] if x else self.v[0:z - a, q, t, head],
                                       exps[0:z - a, t, g * S:(g + 1) * S], start=t == 0, stop=t == 2)
            mm.then_inc(self.s("pv_units"), 1)

    def pe_scores(self, c, pe, b, q, m):
        i = b * 4 + m
        if m == 0:
            pe.wait_ge(self.s("qm_hi"), b * 4 + 4)
            pe.wait_ge(self.s("qm_lo"), b * 4 + 4)
        pe.wait_ge(self.s("k_lo"), i + 1)
        wait(pe, self.s("clipped"), (i - 1) * 2)
        for t, (a, z) in enumerate(KEY_TILES):
            mm = product(pe, [c.psum[0:z - a, m % 2 * 3 + t, 0:GROUP * S]], self.k_hi[:, q, m, a:z], self.k_lo[:, q, m, a:z],
                         [tuple(x[:, m * GROUP:(m + 1) * GROUP, :].rearrange("p h s -> p (h s)")
                                for x in (self.qm_hi, self.qm_lo))], True, True)
        mm.then_inc(self.s("s_units"), 1)

    def act_exps(self, c, act, b, m):
        i = b * 4 + m
        act.wait_ge(self.s("clipped"), i * 2 + 2)
        wait(act, self.s("pv_units"), i - 1)
        c.apart(act)
        for t, (a, z) in enumerate(KEY_TILES):
            scale, shift = (x[0:z - a, t, b:b + 1] if isinstance(b, int) else x[0:z - a, t, bass.DynSlice(b, 1)]
                            for x in (self.key_scale, self.key_shift))
            act.activation(self.exps(c, m)[0:z - a, t, :], self.clipped[0:z - a, t, :], ACT.Exp, bias=shift,
                           scale=scale).then_inc(self.s("exps"), 1)

    def act_batch(self, c, act, b, q, more, two_more):
        for m in range(KD):
            i = b * 4 + m
            if more:
                self.act_keys(act, b + 1, 1 - q, m)
            if more and m == 2:
                act.wait_ge(self.s("s_units"), b * 4 + 4)
                self.act_queries(c, act, b + 1)
            if two_more and m == 1:
                self.split_context_high(act, b + 2, q)
            if m < 3:
                self.act_exps(c, act, b, m + 1)
            elif more:
                self.act_exps(c, act, b + 1, 0)
            act.wait_ge(self.s("o"), i + 1)
            act.activation(c.xn_hi[:, m, tokens_of(b)], self.o[:, m % 2, :], ACT.Copy).then_inc(self.s("o_hi"), 1)
            self.split_output_weights(act, b, m)

    def dve_clip(self, c, dve, i, m):
        bound = self.BOUND / self.SCALE
        bank, n = m % 2 * 3, KEY_TILES[2][1] - KEY_TILES[2][0]
        dve.wait_ge(self.s("s_units"), i + 1)
        wait(dve, self.s("exps"), i * 3)
        dve.tensor_scalar(self.clipped[:, 0:2, :], c.psum[:, bank:bank + 2, 0:GROUP * S], -bound, bound,
                          ALU.max, ALU.min).then_inc(self.s("clipped"), 1)
        dve.tensor_scalar(self.clipped[0:n, 2, :], c.psum[0:n, bank + 2, 0:GROUP * S], -bound, bound,
                          ALU.max, ALU.min).then_inc(self.s("clipped"), 1)

    def dve_batch(self, c, dve, b, q, more):
        def low(m, i):
            dve.wait_ge(self.s("o_hi"), i + 1)
            dve.tensor_tensor(c.xn_lo[:, m, tokens_of(b)], self.o[:, m % 2, :], c.xn_hi[:, m, tokens_of(b)],
                              ALU.subtract).then_inc(self.s("o_lo"), 1)
        for m in range(KD):
            i = b * 4 + m
            if more:
                self.dve_keys(dve, b + 1, 1 - q, m)
            if m < 3 or more:
                self.dve_clip(c, dve, i + 1, (m + 1) % 4)
            if more and m < 3:
                self.dve_values(dve, b + 1, 1 - q, m)
            if more and m == 2:
                self.dve_queries(c, dve, b + 1)
            if m:
                low(m - 1, i - 1)
            at = m % 2 * 200
            weighted, total = c.psum[:, 6, at:at + S], c.psum[:, 6, at + S:at + 2 * S]
            n, step = self.norm, self.s("norm_steps")
            dve.wait_ge(self.s("pv_units"), i + 1)
            dve.tensor_scalar(n[:, 0, :], total, self.EPS, None, ALU.mult).then_inc(step, 1)
            dve.wait_ge(step, i * 3 + 1)
            dve.tensor_tensor(n[:, 0, :], n[:, 0, :], total, ALU.add).then_inc(step, 1)
            dve.wait_ge(step, i * 3 + 2)
            dve.reciprocal(n[:, 1, :], n[:, 0, :]).then_inc(step, 1)
            dve.wait_ge(step, i * 3 + 3)
            wait(dve, self.s("o_lo"), i - 1)
            dve.tensor_tensor(self.o[:, m % 2, :], weighted, n[:, 1, :], ALU.mult).then_inc(self.s("o"), 1)
        low(KD - 1, b * 4 + KD - 1)

    def act_before_batches(self, c, act):
        self.act_exps(c, act, 0, 0)

    def dve_before_batches(self, c, dve):
        self.dve_clip(c, dve, 0, 0)

    def dve_start(self, c, dve):
        dve.wait_ge(self.s("mask_landed"), 16)
        dve.wait_ge(self.s("out_scale_landed"), 16)
        step = self.s("mask_steps")
        dve.tensor_scalar(self.key_scale[:, :, :], self.mask[:, :, :], 0.5, None, ALU.is_gt).then_inc(step, 1)
        dve.tensor_scalar(self.out_scale[:, :], self.out_scale[:, :], 0.0, self.SCALE_MAX, ALU.max,
                          ALU.min).then_inc(step, 1)
        dve.wait_ge(step, 1)
        dve.tensor_scalar(self.key_shift[:, :, :], self.key_scale[:, :, :], self.BOUND, -self.BOUND, ALU.mult,
                          ALU.add).then_inc(step, 1)
        dve.wait_ge(step, 3)
        dve.tensor_scalar(self.key_scale[:, :, :], self.key_scale[:, :, :], self.SCALE, None, ALU.mult).then_inc(
            step, 1)
        dve.wait_ge(step, 4)
        super().dve_start(c, dve)

    def pe_finish(self, c, pe):
        for h in range(2):
            pe.wait_ge(self.s("out_read"), KD)
            for k in range(KD):
                mm = pe.matmul(c.psum[:, 4 + h, 0:HALF], c.mean_matrix[:, :], c.xn[:, k, h * HALF:(h + 1) * HALF],
                               start=k == 0, stop=k == KD - 1)
            mm.then_inc(self.s("mean"), 1)
        for h in range(2):
            pe.wait_ge(self.s("squares"), h + 1)
            for k in range(KD):
                mm = pe.matmul(c.psum[:, 6 + h, 0:HALF], c.mean_matrix[:, :],
                               c.ln_squares[:, k, h * HALF:(h + 1) * HALF], start=k == 0, stop=k == KD - 1)
            mm.then_inc(self.s("variance"), 1)

    def act_finish(self, c, act):
        for h in range(2):
            t = slice(h * HALF, (h + 1) * HALF)
            act.wait_ge(self.s("centered"), h + 1)
            act.activation(c.ln_squares[:, :, t], c.xn[:, :, t], ACT.Square).then_inc(self.s("squares"), 1)
        for h in range(2):
            act.wait_ge(self.s("variance"), h + 1)
            act.activation(c.ln_std[:, h * HALF:(h + 1) * HALF], c.psum[:, 6 + h, 0:HALF], ACT.Sqrt,
                           bias=c.eps[:, 0:1]).then_inc(self.s("std"), 1)

    def dve_finish(self, c, dve):
        for m in range(KD):
            bank = 2 * (m % 2)
            dve.wait_ge(self.s("out_units"), m + 1)
            dve.tensor_scalar(c.xn[:, m, :].rearrange("p (h t) -> p h t", h=2), c.psum[:, bank:bank + 2, 0:HALF],
                              self.bias("bo", m), self.out_scale[:, 0:1], ALU.add, ALU.mult).then_inc(
                                  self.s("out_read"), 1)
        dve.wait_ge(self.s("out_read"), KD)
        for h in range(2):
            t = slice(h * HALF, (h + 1) * HALF)
            dve.wait_ge(self.s("mean"), h + 1)
            dve.tensor_tensor(c.xn[:, :, t], c.xn[:, :, t], c.psum[:, 4 + h, 0:HALF].unsqueeze(1).broadcast_to(
                [P, KD, HALF]), ALU.subtract).then_inc(self.s("centered"), 1)
        for h in range(2):
            t = slice(h * HALF, (h + 1) * HALF)
            dve.wait_ge(self.s("std"), h + 1)
            dve.reciprocal(c.ln_rstd[:, t], c.ln_std[:, t]).then_inc(self.s("rstd"), 1)
            dve.wait_ge(self.s("rstd"), h + 1)
            dve.tensor_tensor(c.xn[:, :, t], c.xn[:, :, t], c.ln_rstd[:, t].unsqueeze(1).broadcast_to([P, KD, HALF]),
                              ALU.mult).then_inc(self.s("delta"), 1)
        dve.wait_ge(self.s("delta"), 2)
        for m in range(KD):
            dve.tensor_scalar(c.xn[:, m, :], c.xn[:, m, :], self.bias("gamma", m), self.bias("beta", m), ALU.mult,
                              ALU.add).then_inc(self.s("delta"), 1)
        for m in range(KD):
            dve.wait_ge(self.s("delta"), 3 + m)
            dve.tensor_tensor(c.residual[:, m, :], c.residual[:, m, :], c.xn[:, m, :], ALU.add).then_inc(
                self.s("delta"), 1)
        dve.wait_ge(self.s("delta"), 2 + 2 * KD)



class LinearAttention(Attention):
    EPS = 1e-8
    PAIRS = HEADS // 2
    VALUES_BANK = 6

    def own_buffers(self, c, own):
        n = self.name
        self.qf_high = c.sb(own, n + "_qf_high", [P, self.PAIRS // 2, T])
        self.maps = c.sb(own, n + "_maps", [P, 4, P])
        self.maps_hi, self.maps_lo = (c.sb(own, n + x, [P, 4, P], F32R) for x in ("_maps_hi", "_maps_lo"))
        self.mask = c.sb(own, n + "_mask", [P, 3, B])
        self.norm = c.sb(own, n + "_norm", [P, 2, S])
        self.o = c.sb(own, n + "_o", [P, S])

    def query_features(self, c, pair):
        return c.xn[:, pair, :] if pair < KD else self.qf_high[:, pair - KD, :]

    def key_features(self, c, m):
        return c.ln_squares[:, :, :].rearrange("p k t -> p (k t)")[:, m % 2 * 768:m % 2 * 768 + 768].rearrange(
            "p (t f) -> p t f", t=3)

    def sums(self, c, m, x):
        at = 1536 + (m % 2 * 2 + x) * 384
        return c.ln_squares[:, :, :].rearrange("p k t -> p (k t)")[:, at:at + 384]

    def act_before_batches(self, c, act):
        pass

    def dve_before_batches(self, c, dve):
        self.dve_features(c, dve, 0, 0)

    def sync_more(self, c, sp):
        sp.dma_start(self.mask[:, :, :], c.a["key_mask"]).then_inc(self.s("mask_landed"), 16)
        sp.dma_start(self.maps[:, :, :], c.a["feature_maps"]).then_inc(self.s("maps_landed"), 16)

    def pool_start(self, c, pool):
        pass

    def act_start(self, c, act):
        act.wait_ge(self.s("maps_landed"), 16)
        act.activation(self.maps_hi[:, :, :], self.maps[:, :, :], ACT.Copy).then_inc(self.s("maps_hi"), 1)
        act.wait_ge(self.s("q_units"), KD)
        for m in range(KD):
            act.wait_ge(self.s("q_copied"), m + 1)
            act.activation(c.xn_hi[:, m, :], c.xn[:, m, :], ACT.Copy).then_inc(self.s("q_hi"), 1)
        for pair in range(self.PAIRS):
            bank = 2 * (pair % 2)
            act.wait_ge(self.s("qf_units"), pair + 1)
            if pair < KD:
                act.wait_ge(self.s("q_lo"), pair + 1)
            act.activation(self.query_features(c, pair).rearrange("p (h t) -> p h t", h=2),
                           c.psum[:, bank:bank + 2, 0:HALF], ACT.Relu).then_inc(self.s("qf_copied"), 1)

    def dve_start(self, c, dve):
        dve.wait_ge(self.s("mask_landed"), 16)
        dve.wait_ge(self.s("maps_hi"), 1)
        dve.tensor_tensor(self.maps_lo[:, :, :], self.maps[:, :, :], self.maps_hi[:, :, :], ALU.subtract).then_inc(
            self.s("maps_lo"), 1)
        for m in range(2):
            for x in range(2):
                dve.memset(self.sums(c, m, x), 0.0).then_inc(self.s("sums_zero"), 1)
        for m in range(KD):
            dve.wait_ge(self.s("q_hi"), m + 1)
            dve.tensor_tensor(c.xn_lo[:, m, :], c.xn[:, m, :], c.xn_hi[:, m, :], ALU.subtract).then_inc(self.s("q_lo"), 1)
        dve.wait_ge(self.s("sums_zero"), 4)

    def pe_start(self, c, pe):
        pe.wait_ge(self.s("maps_lo"), 1)
        for pair in range(self.PAIRS):
            bank = 2 * (pair % 2)
            if pair % 2 == 0:
                pe.wait_ge(self.s("q_lo"), pair // 2 + 1)
            wait(pe, self.s("qf_copied"), pair - 1)
            mm = product(pe, [c.psum[:, bank + h, 0:HALF] for h in range(2)], self.maps_hi[:, pair % 2, :],
                         self.maps_lo[:, pair % 2, :],
                         [tuple(x[:, pair // 2, h * HALF:(h + 1) * HALF] for x in (c.xn_hi, c.xn_lo)) for h in range(2)],
                         True, True)
            mm.then_inc(self.s("qf_units"), 1)
        pe.wait_ge(self.s("qf_copied"), self.PAIRS)
        self.pe_key_features(c, pe, 0, 0, 0)

    def pe_key_features(self, c, pe, b, q, m):
        i = b * 4 + m
        pe.wait_ge(self.s("k_lo"), i + 1)
        wait(pe, self.s("kf"), i * 3)
        for t, (a, z) in enumerate(KEY_TILES):
            mm = product(pe, [c.psum[0:z - a, t, 0:2 * P]], self.k_hi[:, q, m, a:z], self.k_lo[:, q, m, a:z],
                         [tuple(x[:, 2:4, :].rearrange("p a n -> p (a n)") for x in (self.maps_hi, self.maps_lo))],
                         True, True)
        mm.then_inc(self.s("kf_units"), 1)

    def pe_batch(self, c, pe, b, q, more):
        for m in range(KD):
            i = b * 4 + m
            if more:
                self.pe_keys(pe, b + 1, 1 - q, m)
            if m < 3:
                self.pe_key_features(c, pe, b, q, m + 1)
            elif more:
                self.pe_key_features(c, pe, b + 1, 1 - q, 0)
            if more and m < 3:
                self.pe_values(pe, b + 1, 1 - q, m)
            if m == 0:
                pe.wait_ge(self.s("v_added"), b * 3 + 3)
            pe.wait_ge(self.s("kf"), i * 3 + 3)
            wait(pe, self.s("sums"), i * 4)
            kf = self.key_features(c, m)
            for p in range(2):
                for x in range(2):
                    at = p * 96 + x * 64
                    n = 32 if x else 64
                    head = (m * 2 + p) * 64
                    for t, (a, z) in enumerate(KEY_TILES):
                        mm = pe.matmul(c.psum[:, 3, at:at + n], kf[0:z - a, t, p * P:(p + 1) * P],
                                       c.ones[0:z - a, 0:32] if x else self.v[0:z - a, q, t, head:head + 64],
                                       start=t == 0, stop=t == 2)
            mm.then_inc(self.s("kv_units"), 1)
            if m:
                self.pe_output(c, pe, b, m - 1)
            elif not isinstance(b, int) or b:
                self.pe_output(c, pe, b - 1, KD - 1)

    def pe_output(self, c, pe, b, m):
        i = b * 4 + m
        pe.wait_ge(self.s("sums"), i * 4 + 4)
        wait(pe, self.s("o"), i - 1)
        for x in range(2):
            for p in range(2):
                mm = pe.matmul(c.psum[:, 4 + m % 2, x * S:(x + 1) * S], self.sums(c, m, x)[:, p * P:(p + 1) * P],
                               self.query_features(c, m * 2 + p)[:, tokens_of(b)], start=p == 0, stop=p == 1)
        mm.then_inc(self.s("o_units"), 1)

    def act_batch(self, c, act, b, q, more, two_more):
        for m in range(KD):
            i = b * 4 + m
            if more:
                self.act_keys(act, b + 1, 1 - q, m)
            if two_more and m == 1:
                self.split_context_high(act, b + 2, q)
            act.wait_ge(self.s("kv_units"), i + 1)
            wait(act, self.s("o_units"), i - 1)
            for x in range(2):
                for head in range(2):
                    rows = slice(head * 64, head * 64 + 64)
                    dst = self.sums(c, m, x)[rows, :].rearrange("f (p e) -> f p e", p=2)[:, :, head * 32:head * 32 + 32]
                    at = 64 if x else head * 32
                    src = c.psum[rows, 3, 0:192].rearrange("f (p e) -> f p e", p=2)[:, :, at:at + 32]
                    act.activation(dst, src, ACT.Copy).then_inc(self.s("sums"), 1)
            self.split_output_weights(act, b, m)
            if m:
                self.act_output(c, act, b, m - 1)
            elif not isinstance(b, int) or b:
                self.act_output(c, act, b - 1, KD - 1)

    def act_output(self, c, act, b, m):
        act.wait_ge(self.s("o"), b * 4 + m + 1)
        act.activation(c.xn_hi[:, m, tokens_of(b)], self.o[:, :], ACT.Copy).then_inc(self.s("o_hi"), 1)

    def dve_features(self, c, dve, b, m):
        i = b * 4 + m
        dve.wait_ge(self.s("kf_units"), i + 1)
        wait(dve, self.s("kv_units"), i - 1)
        for t, (a, z) in enumerate(KEY_TILES):
            mask = (self.mask[0:z - a, t, b:b + 1] if isinstance(b, int)
                    else self.mask[0:z - a, t, bass.DynSlice(b, 1)])
            dve.tensor_scalar(self.key_features(c, m)[0:z - a, t, :], c.psum[0:z - a, t, 0:2 * P], 0.0, mask,
                              ALU.max, ALU.mult).then_inc(self.s("kf"), 1)

    def dve_batch(self, c, dve, b, q, more):
        for m in range(KD):
            if more:
                self.dve_keys(dve, b + 1, 1 - q, m)
            if m < 3:
                self.dve_features(c, dve, b, m + 1)
            elif more:
                self.dve_features(c, dve, b + 1, 0)
            if more and m < 3:
                self.dve_values(dve, b + 1, 1 - q, m)
            if m:
                self.dve_output(c, dve, b, m - 1)
            elif not isinstance(b, int) or b:
                self.dve_output(c, dve, b - 1, KD - 1)

    def dve_output(self, c, dve, b, m):
        i, step, bank = b * 4 + m, self.s("norm_steps"), 4 + m % 2
        dve.wait_ge(self.s("o_units"), i + 1)
        dve.tensor_scalar(self.norm[:, 0, :], c.psum[:, bank, S:2 * S], self.EPS, None, ALU.add).then_inc(step, 1)
        dve.wait_ge(step, i * 2 + 1)
        dve.reciprocal(self.norm[:, 1, :], self.norm[:, 0, :]).then_inc(step, 1)
        dve.wait_ge(step, i * 2 + 2)
        wait(dve, self.s("o_hi"), i)
        wait(dve, self.s("o_lo"), i)
        dve.tensor_tensor(self.o[:, :], c.psum[:, bank, 0:S], self.norm[:, 1, :], ALU.mult).then_inc(self.s("o"), 1)
        dve.wait_ge(self.s("o_hi"), i + 1)
        dve.tensor_tensor(c.xn_lo[:, m, tokens_of(b)], self.o[:, :], c.xn_hi[:, m, tokens_of(b)],
                          ALU.subtract).then_inc(self.s("o_lo"), 1)

    def pe_after_batches(self, c, pe):
        self.pe_output(c, pe, B - 1, KD - 1)

    def act_finish(self, c, act):
        self.act_output(c, act, B - 1, KD - 1)

    def dve_finish(self, c, dve):
        self.dve_output(c, dve, B - 1, KD - 1)
        super().dve_finish(c, dve)



class BitFfn:
    SPLIT_INPUT, FREE_BANKS = False, 0
    INNER = 2048
    KI = INNER // P
    CHUNKS = INNER // 512
    LEVELS = 127.0
    EPS = 1e-5
    ROUND = 1.5 * 2.0 ** 23

    def __init__(self, name, index):
        self.name, self.index = name, index

    def s(self, name):
        return self.c.sem(f"{self.name}_{name}")

    def buffers(self, c, own):
        n, self.c = self.name, c
        self.w = [c.sb(own, f"{n}_w{x}", [P, KD * self.INNER], BF16) for x in (1, 2)]
        self.sums = c.sb(own, n + "_sums", [P, 2, KD])
        self.sum = c.sb(own, n + "_sum", [P, 2])
        self.step_w = c.sb(own, n + "_step_w", [P, 2])
        self.border = c.sb(own, n + "_border", [P, 2, 2])
        self.stage = c.sb(own, n + "_stage", [P, KD, S])
        self.rows = c.sb(own, n + "_rows", [S, D])
        self.x_whole = c.sb(own, n + "_x_whole", [S, D], BF16)
        self.x_turned = c.sb(own, n + "_x_turned", [P, KD, S], BF16)
        self.inner = c.sb(own, n + "_inner", [S, self.INNER])
        self.inner_whole = c.sb(own, n + "_inner_whole", [S, self.INNER], BF16)
        self.inner_turned = c.sb(own, n + "_inner_turned", [P, self.KI, S], BF16)
        self.out = c.sb(own, n + "_out", [S, D])
        self.identity = c.sb(own, n + "_identity", [P, P], BF16)
        self.x_max, self.x_scale, self.x_step, self.h_max, self.h_scale, self.h_step = (
            c.sb(own, n + x, [S, B]) for x in ("_x_max", "_x_scale", "_x_step", "_h_max", "_h_scale", "_h_step"))
        c.sb(own, n + "_gap", [P, 640])
        self.w_raw = [c.sb(own, f"{n}_w{x}_raw", [P, KD * self.INNER]) for x in (1, 2)]

    def one(self, buffer, b):
        return buffer[:, b:b + 1] if isinstance(b, int) else buffer[:, bass.DynSlice(b, 1)]

    def schedule(self, engine, first, body):
        first()
        body(0, False, True, True)
        body(1, True, True, True)
        with engine.Fori(2, B - 1) as i:
            body(i, True, True, True)
        body(B - 1, True, True, False)
        body(B, True, False, False)

    def nearly_over(self, c, sp):
        pass

    def sync(self, c, sp):
        pass

    def prefetch(self, c, sp):
        for x in range(2):
            for k in range(KD):
                cut = slice(k * self.INNER, (k + 1) * self.INNER)
                sp.dma_start(self.w_raw[x][:, cut], c.a[f"bit_w{x + 1}"][:, cut]).then_inc(self.s(f"w{x}{k}_landed"), 16)

    def pool(self, c, pool):
        pool.wait_ge(c.sem("residual_ready"), self.index + 1)
        pool.wait_ge(self.s("borders"), 4)
        self.whole_weight(pool, 1)

    def whole_weight(self, engine, x):
        for k in range(2 * x, KD):
            cut = slice(k * self.INNER, (k + 1) * self.INNER)
            raw, whole = self.w_raw[x][:, cut], self.w[x][:, cut]
            engine.tensor_scalar(whole, raw, self.border[:, 1, x:x + 1], None, ALU.is_lt).then_inc(self.s(f"w{x}_below"), 1)
            if x:
                engine.wait_ge(self.s("w1_below"), k - 1)
                engine.tensor_scalar(raw, raw, self.border[:, 0, x:x + 1], None, ALU.is_gt).then_inc(self.s("w1_above"), 1)
                engine.wait_ge(self.s("w1_above"), k - 1)
                engine.tensor_tensor(whole, raw, whole, ALU.subtract).then_inc(self.s(f"w{x}_whole"), 1)
            else:
                engine.wait_ge(self.s("w0_below"), k + 1)
                engine.scalar_tensor_tensor(whole, raw, self.border[:, 0, x:x + 1], whole, ALU.is_gt,
                                            ALU.subtract).then_inc(self.s(f"w{x}_whole"), 1)

    def whole_weight_start(self, dve):
        for k in range(2):
            cut = slice(k * self.INNER, (k + 1) * self.INNER)
            raw, whole = self.w_raw[1][:, cut], self.w[1][:, cut]
            dve.tensor_scalar(whole, raw, self.border[:, 1, 1:2], None, ALU.is_lt).then_inc(self.s("w1_start_below"), 1)
            dve.wait_ge(self.s("w1_start_below"), k + 1)
            dve.scalar_tensor_tensor(whole, raw, self.border[:, 0, 1:2], whole, ALU.is_gt,
                                     ALU.subtract).then_inc(self.s("w1_start_whole"), 1)

    def pe(self, c, pe):
        ln_pe(c, pe, self)
        pe.wait_ge(self.s("sum"), 2)
        pe.matmul(c.psum[:, 4, 0:2], c.ones[:, :], self.sum[:, :], start=True, stop=True).then_inc(self.s("total"), 1)

        def turn_x(b):
            pe.wait_ge(self.s("staged"), b + 1)
            wait(pe, self.s("x_turned"), b)
            for k in range(KD):
                mm = pe.transpose(c.psum[0:S, 7, k * P:(k + 1) * P], self.stage[:, k, :], c.identity[:, :])
            mm.then_inc(self.s("x_units"), 1)

        def turn_x_whole(b):
            pe.wait_ge(self.s("identity"), 1)
            pe.wait_ge(self.s("x_whole"), b + 1)
            bank = c.psum[:, 7, :].bitcast(BF16)
            for k in range(KD):
                mm = pe.transpose(bank[:, k * S:(k + 1) * S], self.x_whole[:, k * P:(k + 1) * P], self.identity[0:S, 0:S])
            mm.then_inc(self.s("x_whole_units"), 1)

        def first():
            turn_x(0)
            turn_x_whole(0)

        def body(i, before, now, after):
            if now:
                pe.wait_ge(self.s("x_turned"), i + 1)
                wait(pe, self.s("inner"), i)
                first_batch = isinstance(i, int) and i == 0
                order = ([(n, k) for k in range(KD) for n in range(self.CHUNKS)] if first_batch else
                         [(n, k) for n in range(self.CHUNKS) for k in range(KD)])
                for n, k in order:
                    if first_batch and n == 0:
                        pe.wait_ge(self.s("w0_whole"), k + 1)
                    at = k * self.INNER + n * 512
                    mm = pe.matmul(c.psum[0:S, n, :], self.x_turned[:, k, :], self.w[0][:, at:at + 512],
                                   start=k == 0, stop=k == KD - 1)
                mm.then_inc(self.s("inner_units"), 1)
            if after:
                turn_x(i + 1)
            if before:
                pe.wait_ge(self.s("w1_whole"), 2)
                pe.wait_ge(self.s("w1_start_whole"), 2)
                pe.wait_ge(self.s("inner_turned"), (i - 1) * 2 + 2)
                wait(pe, self.s("added"), i - 1)
                for k in range(self.KI):
                    mm = pe.matmul(c.psum[0:S, 6, :], self.inner_turned[:, k, :], self.w[1][:, k * D:(k + 1) * D],
                                   start=k == 0, stop=k == self.KI - 1)
                mm.then_inc(self.s("out_units"), 1)
            if after:
                turn_x_whole(i + 1)
            if before:
                pe.wait_ge(self.s("out"), i)
                for k in range(KD):
                    mm = pe.transpose(c.psum[:, 6, k * S:(k + 1) * S], self.out[:, k * P:(k + 1) * P], c.identity[0:S, 0:S])
                mm.then_inc(self.s("out_turned_units"), 1)
            if now:
                pe.wait_ge(self.s("inner_whole"), i + 1)
                wait(pe, self.s("inner_turned"), i * 2)
                for k in range(self.KI):
                    bank = c.psum[:, 4 + k // 8, :].bitcast(BF16)
                    mm = pe.transpose(bank[:, k % 8 * S:(k % 8 + 1) * S], self.inner_whole[:, k * P:(k + 1) * P],
                                      self.identity[0:S, 0:S])
                mm.then_inc(self.s("inner_whole_units"), 1)
        self.schedule(pe, first, body)
        ln_mean_pe(c, pe, self.index + 1, lambda k: pe.wait_ge(self.s("added"), B))

    def act(self, c, act):
        ln_act(c, act, self)
        for x in range(2):
            for k in range(KD if x == 0 else 1):
                act.wait_ge(self.s(f"w{x}{k}_landed"), 16)
                cut = slice(k * self.INNER, (k + 1) * self.INNER)
                act.activation(self.w[x][:, cut], self.w_raw[x][:, cut], ACT.Abs,
                               accum_out=self.sums[:, x, k:k + 1]).then_inc(self.s("magnitudes"), 1)

        def stage(b):
            wait(act, self.s("x_units"), b)
            act.activation(self.stage[:, :, :], c.xn[:, :, tokens_of(b)], ACT.Copy).then_inc(self.s("staged"), 1)

        def turned(b):
            act.wait_ge(self.s("x_whole_units"), b + 1)
            wait(act, self.s("inner_units"), b)
            act.activation(self.x_turned[:, :, :].rearrange("p k s -> p (k s)"),
                           c.psum[:, 7, :].bitcast(BF16)[:, 0:KD * S], ACT.Copy).then_inc(self.s("x_turned"), 1)

        def first():
            act.wait_ge(c.sem("ln_xn"), 4 * self.index + 4)
            stage(0)
            turned(0)

        def body(i, before, now, after):
            if after:
                stage(i + 1)
            if now:
                act.wait_ge(self.s("inner_units"), i + 1)
                act.wait_ge(self.s("x_steps"), i + 1)
                wait(act, self.s("inner_whole"), i)
                act.activation(self.inner[:, :], c.psum[0:S, 0:self.CHUNKS, :].rearrange("s n w -> s (n w)"),
                               ACT.Relu, scale=self.one(self.x_step, i)).then_inc(self.s("inner"), 1)
            if after:
                turned(i + 1)
            if before:
                act.wait_ge(self.s("out_units"), i)
                act.wait_ge(self.s("h_steps"), i)
                wait(act, self.s("out_turned_units"), i - 1)
                act.activation(self.out[:, :], c.psum[0:S, 6, :], ACT.Copy, scale=self.one(self.h_step, i - 1)).then_inc(
                    self.s("out"), 1)
            if now:
                act.wait_ge(self.s("inner_whole_units"), i + 1)
                if before:
                    act.wait_ge(self.s("out_units"), i)
                for half in range(2):
                    act.activation(self.inner_turned[:, half * 8:half * 8 + 8, :].rearrange("p k s -> p (k s)"),
                                   c.psum[:, 4 + half, :].bitcast(BF16)[:, 0:8 * S], ACT.Copy).then_inc(
                                       self.s("inner_turned"), 1)
        self.schedule(act, first, body)

    def dve(self, c, dve):
        ln_dve(c, dve, self)
        dve.wait_ge(c.sem("constants"), 3)
        dve.tensor_copy(self.identity[:, :], c.identity[:, :]).then_inc(self.s("identity"), 1)
        for k in range(1, KD):
            dve.wait_ge(self.s(f"w1{k}_landed"), 16)
            cut = slice(k * self.INNER, (k + 1) * self.INNER)
            dve.tensor_reduce(self.sums[:, 1, k:k + 1], self.w_raw[1][:, cut], AX.X, ALU.add,
                              apply_absolute_value=True).then_inc(self.s("magnitudes"), 1)
        dve.wait_ge(self.s("magnitudes"), 2 * KD)
        dve.tensor_reduce(self.sum[:, :], self.sums[:, :, :], AX.X, ALU.add).then_inc(self.s("sum"), 2)
        dve.wait_ge(self.s("total"), 1)
        dve.tensor_scalar(self.step_w[:, :], c.psum[:, 4, 0:2], 1.0 / (D * self.INNER), self.EPS, ALU.mult,
                          ALU.max).then_inc(self.s("step_w"), 1)
        dve.wait_ge(self.s("step_w"), 1)
        for x, half in enumerate((0.5, -0.5)):
            dve.tensor_scalar(self.border[:, x, :], self.step_w[:, :], half, None, ALU.mult).then_inc(self.s("borders"), 2)
        dve.wait_ge(self.s("borders"), 4)

        def scales(largest, scale, step, weight, b, step_sem, name):
            small = self.s(name)
            dve.tensor_scalar(self.one(largest, b), self.one(largest, b), self.EPS, None, ALU.max).then_inc(small, 1)
            dve.wait_ge(small, b * 3 + 1)
            dve.reciprocal(self.one(scale, b), self.one(largest, b)).then_inc(small, 1)
            dve.tensor_scalar(self.one(step, b), self.one(largest, b), 1.0 / self.LEVELS, self.step_w[0:S, weight:weight + 1],
                              ALU.mult, ALU.mult).then_inc(step_sem, 1)
            dve.wait_ge(small, b * 3 + 2)
            dve.tensor_scalar(self.one(scale, b), self.one(scale, b), self.LEVELS, None, ALU.mult).then_inc(small, 1)
            dve.wait_ge(small, b * 3 + 3)

        def whole_x(b):
            dve.wait_ge(self.s("x_units"), b + 1)
            dve.tensor_reduce(self.one(self.x_max, b), c.psum[0:S, 7, :], AX.X, ALU.max,
                              apply_absolute_value=True).then_inc(self.s("x_max"), 1)
            dve.wait_ge(self.s("x_max"), b + 1)
            scales(self.x_max, self.x_scale, self.x_step, 0, b, self.s("x_steps"), "x_scales")
            dve.tensor_scalar(self.rows[:, :], c.psum[0:S, 7, :], self.one(self.x_scale, b), self.ROUND, ALU.mult,
                              ALU.add).then_inc(self.s("rows"), 1)
            dve.wait_ge(self.s("rows"), b + 1)
            dve.tensor_scalar(self.x_whole[:, :], self.rows[:, :], self.ROUND, None, ALU.subtract).then_inc(
                self.s("x_whole"), 1)

        def body(i, before, now, after):
            if after:
                whole_x(i + 1)
            if now:
                dve.wait_ge(self.s("inner"), i + 1)
                dve.tensor_reduce(self.one(self.h_max, i), self.inner[:, :], AX.X, ALU.max).then_inc(self.s("h_max"), 1)
                dve.wait_ge(self.s("h_max"), i + 1)
                scales(self.h_max, self.h_scale, self.h_step, 1, i, self.s("h_steps"), "h_scales")
                dve.tensor_scalar(self.inner[:, :], self.inner[:, :], self.one(self.h_scale, i), self.ROUND, ALU.mult,
                                  ALU.add).then_inc(self.s("inner_scaled"), 1)
                dve.wait_ge(self.s("inner_scaled"), i + 1)
                dve.tensor_scalar(self.inner_whole[:, :], self.inner[:, :], self.ROUND, None, ALU.subtract).then_inc(
                    self.s("inner_whole"), 1)
            if isinstance(i, int) and i == 0:
                self.whole_weight_start(dve)
            if before:
                dve.wait_ge(self.s("out_turned_units"), i)
                into = c.residual[:, :, tokens_of(i - 1)]
                dve.tensor_tensor(into, into, c.psum[:, 6, 0:KD * S].rearrange("p (k s) -> p k s", k=KD),
                                  ALU.add).then_inc(self.s("added"), 1)
        def first():
            whole_x(0)
            self.whole_weight(dve, 0)
        self.schedule(dve, first, body)
        dve.wait_ge(self.s("added"), B)
        dve.nop().then_inc(c.sem("residual_ready"), 1)



class LatentAttention:
    SPLIT_INPUT, FREE_BANKS = True, 4
    HEADS, DH, ROT = 16, 128, 64
    LOOKBACK, NEG = 8, 1e30
    SCALE = 1.0 / float(DH + ROT) ** 0.5
    PAIRS = HEADS // 2
    KVC, KR = 3, 4
    RAW = 3
    FIRST = 4
    LAST = FIRST + 3 * PAIRS

    def __init__(self, name, index, slabs_at):
        self.name, self.index, self.slabs_at = name, index, slabs_at

    def s(self, name):
        return self.c.sem(f"{self.name}_{name}")

    def buffers(self, c, own):
        n, self.c = self.name, c
        self.q_rot = c.sb(own, n + "_q_rot", [P, self.PAIRS, T])
        self.q_latent = c.sb(own, n + "_q_latent", [P, self.HEADS - 4, T])
        self.w_hi, self.w_lo = (c.sb(own, n + x, [P, 5, 512], F32R) for x in ("_w_hi", "_w_lo"))
        self.w_raw = c.sb(own, n + "_w_raw", [P, self.RAW, 512])
        self.cos_q, self.sin_q = (c.sb(own, n + x, [P, S]) for x in ("_cos_q", "_sin_q"))
        with ExitStack() as early:
            self.qc_hi, self.qc_lo = (c.sb(early, n + x, [P, 2, T], F32R) for x in ("_qc_hi", "_qc_lo"))
            self.fused_hi, self.fused_lo = (c.sb(early, n + x, [P, 2, 2 * P], F32R) for x in ("_fused_hi", "_fused_lo"))
        with ExitStack() as late:
            self.out_w_hi, self.out_w_lo = (c.sb(late, n + x, [P, 2, 2, D], F32R) for x in ("_out_w_hi", "_out_w_lo"))
            self.o_hi, self.o_lo = (c.sb(late, n + x, [P, 2, 2, T], F32R) for x in ("_o_hi", "_o_lo"))
        self.ql_hi, self.ql_lo = (c.sb(own, n + x, [P, self.HEADS, S], F32R) for x in ("_ql_hi", "_ql_lo"))
        self.qr_hi, self.qr_lo = (c.sb(own, n + x, [P, self.HEADS, S], F32R) for x in ("_qr_hi", "_qr_lo"))
        self.ctx_raw = c.sb(own, n + "_ctx_raw", [P, KD, CP])
        self.ctx_hi, self.ctx_lo = (c.sb(own, n + x, [P, KD, CP], F32R) for x in ("_ctx_hi", "_ctx_lo"))
        self.latent = c.sb(own, n + "_latent", [P, CP])
        self.l_hi, self.l_lo, self.kr_hi, self.kr_lo = (
            c.sb(own, n + x, [P, 2, CP], F32R) for x in ("_l_hi", "_l_lo", "_kr_hi", "_kr_lo"))
        self.l_turned = c.sb(own, n + "_l_turned", [P, 2, 3, P])
        spare = c.ln_squares[:, :, :].rearrange("p k t -> p (k t)")[:, 2 * T:]
        self.k_rot = spare[:, 0:2 * CP].rearrange("p (x t) -> p x t", x=2)
        self.early_enough = spare[0:S, 2 * CP:2 * CP + C]
        self.cos_k, self.sin_k = (c.sb(own, n + x, [P, CP]) for x in ("_cos_k", "_sin_k"))
        self.probs = c.sb(own, n + "_probs", [S, 4, C])
        self.ids = c.sb(own, n + "_ids", [S, B], I32)
        self.ids_f = c.sb(own, n + "_ids_f", [S, B])
        self.positions = c.sb(own, n + "_positions", [S, C])
        self.distance = c.sb(own, n + "_distance", [S, C])
        self.outside = c.sb(own, n + "_outside", [S, 2, C])
        self.highest, self.shift, self.total, self.inverse = (
            c.sb(own, n + x, [S, 4]) for x in ("_highest", "_shift", "_total", "_inverse"))

    def turned(self, c):
        return c.ln_squares[:, :, :].rearrange("p k t -> p (k t)")[:, 0:1200].rearrange("p (t n) -> p t n", t=3)

    def rotated(self, c, x):
        return c.ln_squares[:, x, :]

    def q_latent_of(self, c, head):
        if isinstance(head, int):
            return c.xn[:, head, :] if head < 4 else self.q_latent[:, head - 4, :]
        return self.q_latent[:, bass.DynSlice(head - 4, 1), :].rearrange("p a t -> p (a t)")

    def steps(self, engine, body):
        body(0, 0, True)
        body(1, 1, True)
        with engine.Fori(1, self.PAIRS // 2 - 1) as i:
            body(i * 2, 0, True)
            body(i * 2 + 1, 1, True)
        body(self.PAIRS - 2, 0, True)
        body(self.PAIRS - 1, 1, False)

    def slab_landed(self, engine, n, j=0):
        engine.wait_ge(self.s(f"w_landed{n % 3}"), (j + n // 3 + 1) * 16)

    def prefetch(self, c, sp):
        pass

    def nearly_over(self, c, sp):
        sp.wait_ge(c.sem("residual_ready"), self.index + 2)

    def sync(self, c, sp):

        def slab(n, j=0):
            if not isinstance(j, int) or n + 3 * j >= 3:
                sp.wait_ge(self.s("w_split"), j * 3 + n - 2)
            src = (c.slabs[self.slabs_at + n + 3 * j, :, :] if isinstance(j, int) else
                   c.slabs[bass.DynSlice(j * 3 + (self.slabs_at + n), 1), :, :].rearrange("a p n -> p (a n)"))
            sp.dma_start(self.w_raw[:, n % 3, :], src).then_inc(self.s(f"w_landed{n % 3}"), 16)
        sp.dma_start(self.ctx_raw[:, :, :], c.a["ctx"][0, :, :, :]).then_inc(self.s("ctx_landed"), 16)
        for n in range(self.FIRST):
            slab(n)
        for name, buffer in (("cos_q", self.cos_q), ("sin_q", self.sin_q), ("cos_k", self.cos_k), ("sin_k", self.sin_k),
                             ("ids", self.ids), ("positions", self.positions)):
            sp.dma_start(buffer[:, :], c.a[name]).then_inc(self.s(name + "_landed"), 16)

        def step(first):
            def body(j, q, more):
                for x in range(3):
                    slab(first + x, j)
            return body
        self.steps(sp, step(self.FIRST))
        sp.wait_ge(self.s("ctx_split"), 1)
        sp.dma_start(self.ctx_raw[:, :, :], c.a["ctx"][1, :, :, :]).then_inc(self.s("ctx_landed"), 16)

        def batch(b, q, more, two_more):
            if two_more:
                sp.wait_ge(self.s("ctx_split"), b + 2)
                sp.dma_start(self.ctx_raw[:, :, :], c.a["ctx"][bass.DynSlice(b + 2, 1), :, :, :].rearrange(
                    "a p k t -> p (a k) t") if not isinstance(b, int) else c.a["ctx"][b + 2, :, :, :]).then_inc(
                        self.s("ctx_landed"), 16)
        batches(sp, batch)
        self.steps(sp, step(self.LAST))

    def pool(self, c, pool):
        pool.wait_ge(c.sem("residual_ready"), self.index + 1)

        def low(place, n, j=0):
            pool.wait_ge(self.s("w_hi"), j * 3 + n + 1)
            pool.tensor_tensor(self.w_lo[:, place, :], self.w_raw[:, n % 3, :], self.w_hi[:, place, :],
                               ALU.subtract).then_inc(self.s("w_split"), 1)
        pool.wait_ge(self.s("ctx_landed"), 16)
        pool.tensor_copy(self.ctx_hi[:, :, :], self.ctx_raw[:, :, :]).then_inc(self.s("ctx_hi"), 1)
        self.context_low(pool, 0)
        for n, place in ((0, self.KVC), (1, self.KR)):
            self.slab_landed(pool, n)
            pool.tensor_copy(self.w_hi[:, place, :], self.w_raw[:, n % 3, :]).then_inc(self.s("w_hi"), 1)
            low(place, n)
        low(0, 2)
        low(1, 3)

        def step(first):
            def body(j, q, more):
                for x in range(3):
                    low(x, first + x, j)
            return body
        self.steps(pool, step(self.FIRST))
        pool.wait_ge(self.s("ql_units"), self.HEADS)
        for buffer in (self.qr_hi, self.qr_lo):
            pool.memset(buffer[:, :, :].bitcast(F32), 0.0).then_inc(self.s("qr_zero"), 1)
        pool.wait_ge(self.s("ids_landed"), 16)
        pool.wait_ge(self.s("positions_landed"), 16)
        pool.tensor_copy(self.ids_f[:, :], self.ids[:, :]).then_inc(self.s("ids_f"), 1)
        pool.wait_ge(self.s("ids_f"), 1)
        pool.tensor_scalar(self.ids_f[:, :], self.ids_f[:, :], -1.0, None, ALU.mult).then_inc(self.s("ids_f"), 1)
        self.make_mask(c, pool, 0, 0)
        self.make_mask(c, pool, 1, 1)
        self.context_low(pool, 1)

        def batch(b, q, more, two_more):
            for m in range(4):
                if m == 3 and two_more:
                    self.make_mask(c, pool, b + 2, q)
                if more:
                    self.low_latent_queries(c, pool, b + 1, m)
                if m == 0 and two_more:
                    self.context_low(pool, b + 2)
        batches(pool, batch)
        self.steps(pool, step(self.LAST))

    def context_low(self, pool, b):
        pool.wait_ge(self.s("ctx_hi"), b + 1)
        pool.tensor_tensor(self.ctx_lo[:, :, :], self.ctx_raw[:, :, :], self.ctx_hi[:, :, :], ALU.subtract).then_inc(
            self.s("ctx_split"), 1)

    def act_distance(self, c, act, b):
        act.wait_ge(self.s("ids_f"), 2)
        wait(act, self.s("masks"), b)
        mine = self.ids_f[:, b:b + 1] if isinstance(b, int) else self.ids_f[:, bass.DynSlice(b, 1)]
        act.activation(self.distance[:, :], self.positions[:, :], ACT.Identity, bias=mine).then_inc(
            self.s("distances"), 1)

    def make_mask(self, c, pool, b, q):
        out, early, step = self.outside[:, q, :], self.early_enough, self.s("mask_steps")
        pool.wait_ge(self.s("distances"), b + 1)
        wait(pool, self.s("masked"), (b - 1) * 16)
        c.apart(pool)
        pool.tensor_scalar(early, self.distance[:, :], 0.0, None, ALU.is_le).then_inc(step, 1)
        pool.tensor_scalar(out, self.distance[:, :], -float(self.LOOKBACK), None, ALU.is_ge).then_inc(step, 1)
        pool.wait_ge(step, b * 3 + 2)
        pool.tensor_tensor(out, out, early, ALU.mult).then_inc(step, 1)
        pool.wait_ge(step, b * 3 + 3)
        c.apart(pool)
        pool.tensor_scalar(out, out, self.NEG, -self.NEG, ALU.mult, ALU.add).then_inc(self.s("masks"), 1)

    def pe(self, c, pe):
        ln_pe(c, pe, self)
        wait_for_input(c, pe, self)
        pe.wait_ge(self.s("w_split"), self.FIRST)
        for m in range(2):
            for k in range(KD):
                w = slice(k * P, (k + 1) * P)
                mm = product(pe, [c.psum[:, 2 * m + h, 0:HALF] for h in range(2)], self.w_hi[:, m, w], self.w_lo[:, m, w],
                             [tuple(x[:, k, h * HALF:(h + 1) * HALF] for x in (c.xn_hi, c.xn_lo)) for h in range(2)],
                             k == 0, k == KD - 1)
            mm.then_inc(self.s("qc_units"), 1)
        pe.wait_ge(self.s("qc_lo"), 2)
        qc = [[tuple(x[:, k, h * HALF:(h + 1) * HALF] for x in (self.qc_hi, self.qc_lo)) for h in range(2)]
              for k in range(2)]

        def step(j, q, more):
            pe.wait_ge(self.s("w_split"), j * 3 + self.FIRST + 2)
            wait(pe, self.s("ql_copied"), j * 2 - 1)
            for x in range(2):
                uk = slice(2 * P, 3 * P)
                for k in range(2):
                    at = (x * 2 + k) * P
                    uq = slice(k * P, (k + 1) * P)
                    mm = product(pe, [c.psum[:, 4, at:at + P]], self.w_hi[:, x, uq], self.w_lo[:, x, uq],
                                 [(self.w_hi[:, x, uk], self.w_lo[:, x, uk])], True, True)
            mm.then_inc(self.s("fused_units"), 1)
            pe.wait_ge(self.s("w_split"), j * 3 + self.FIRST + 3)
            wait(pe, self.s("rot_read"), j * 2)
            for x in range(2):
                for k in range(2):
                    w = slice((x * 2 + k) * P, (x * 2 + k + 1) * P)
                    mm = product(pe, [c.psum[:, 2 * x + h, 0:HALF] for h in range(2)], self.w_hi[:, 2, w],
                                 self.w_lo[:, 2, w], qc[k], k == 0, k == 1)
                mm.then_inc(self.s("rot_units"), 1)
            pe.wait_ge(self.s("fused_lo"), j + 1)
            for x in range(2):
                if x:
                    wait(pe, self.s("ql_copied"), j * 2)
                for k in range(2):
                    w = slice(k * P, (k + 1) * P)
                    mm = product(pe, [c.psum[:, 4 + 2 * x + h, 0:HALF] for h in range(2)], self.fused_hi[:, x, w],
                                 self.fused_lo[:, x, w], qc[k], k == 0, k == 1)
                mm.then_inc(self.s("ql_units"), 1)
        self.steps(pe, step)
        pe.wait_ge(self.s("ql_copied"), self.HEADS)
        pe.wait_ge(self.s("rot_read"), self.HEADS)
        for m in range(4):
            self.pe_piece(c, pe, 0, 0, m)
        self.pe_scores(c, pe, 0, 0, 0)
        batches(pe, lambda b, q, more, two_more: self.pe_batch(c, pe, b, q, more))

        def fuse_output(j, q):
            pe.wait_ge(self.s("w_split"), j * 3 + self.LAST + 3)
            wait(pe, self.s("out_w_lo"), j)
            for x in range(2):
                uv = slice(x * P, (x + 1) * P)
                mm = product(pe, [c.psum[:, 4 + x, :]], self.w_hi[:, 0, uv], self.w_lo[:, 0, uv],
                             [(self.w_hi[:, 1 + x, :], self.w_lo[:, 1 + x, :])], True, True)
            mm.then_inc(self.s("out_w_units"), 1)

        def out(j, q, more):
            if more:
                fuse_output(j + 1, 1 - q)
            pe.wait_ge(self.s("out_w_lo"), j + 1)
            pe.wait_ge(self.s("o_lo"), j + 1)
            for m in range(KD):
                wait(pe, self.s("added"), j * 4 + m - 1)
                for x in range(2):
                    w = slice(m * P, (m + 1) * P)
                    mm = product(pe, [c.psum[:, 2 * (m % 2) + h, 0:HALF] for h in range(2)], self.out_w_hi[:, q, x, w],
                                 self.out_w_lo[:, q, x, w],
                                 [tuple(o[:, q, x, h * HALF:(h + 1) * HALF] for o in (self.o_hi, self.o_lo))
                                  for h in range(2)], x == 0, x == 1)
                mm.then_inc(self.s("out_units"), 1)
        fuse_output(0, 0)
        pe.wait_ge(self.s("o_copied"), B * 4)
        self.steps(pe, out)
        ln_mean_pe(c, pe, self.index + 1, lambda k: pe.wait_ge(self.s("added"), (self.PAIRS - 1) * 4 + k + 1))

    def pe_piece(self, c, pe, b, q, m):
        bank = c.psum[:, 7, 0:CP]
        if m == 0:
            pe.wait_ge(self.s("ctx_split"), b + 1)
            for k in range(KD):
                w = slice(k * P, (k + 1) * P)
                mm = product(pe, [bank], self.w_hi[:, self.KVC, w], self.w_lo[:, self.KVC, w],
                             [(self.ctx_hi[:, k, :], self.ctx_lo[:, k, :])], k == 0, k == KD - 1)
        elif m < 3:
            pe.wait_ge(self.s("l_lo"), b + 1)
            if m == 2:
                pe.wait_ge(self.s("k_rotated"), b * 2 + 1)
            w = slice((m - 1) * P, m * P)
            mm = product(pe, [bank], self.w_hi[:, self.KR, w], self.w_lo[:, self.KR, w],
                         [(self.l_hi[:, q, :], self.l_lo[:, q, :])], True, True)
        else:
            pe.wait_ge(self.s("k_rotated"), b * 2 + 2)
            for t, (a, z) in enumerate(KEY_TILES):
                mm = pe.transpose(c.psum[0:z - a, 7, t * P:(t + 1) * P], self.latent[:, a:z], c.identity[:, :])
        mm.then_inc(self.s(f"piece{m}"), 1)

    def pe_scores(self, c, pe, b, q, m):
        i = b * 4 + m
        pe.wait_ge(self.s("q_split"), i + 1)
        pe.wait_ge(self.s("q_rot_split"), i * 2 + 2)
        if m == 0:
            pe.wait_ge(self.s("kr_lo"), b + 1)
            pe.wait_ge(self.s("l_lo"), b + 1)
        wait(pe, self.s("masked"), i * 4)
        for g in range(4):
            head = m * 4 + g
            bank = [c.psum[0:S, g, 0:CP]]
            product(pe, bank, self.ql_hi[:, head, :], self.ql_lo[:, head, :],
                    [(self.l_hi[:, q, :], self.l_lo[:, q, :])], True, False)
            mm = product(pe, bank, self.qr_hi[:, head, :], self.qr_lo[:, head, :],
                         [(self.kr_hi[:, q, :], self.kr_lo[:, q, :])], False, True)
        mm.then_inc(self.s("s_units"), 1)

    def pe_batch(self, c, pe, b, q, more):
        turned = self.turned(c)
        for m in range(4):
            i = b * 4 + m
            wait(pe, self.s("o_copied"), i)
            if more:
                self.pe_piece(c, pe, b + 1, 1 - q, m)
            if m < 3:
                self.pe_scores(c, pe, b, q, m + 1)
            elif more:
                self.pe_scores(c, pe, b + 1, 1 - q, 0)
            pe.wait_ge(self.s("normalised"), i * 4 + 4)
            wait(pe, self.s("turned_01"), i)
            wait(pe, self.s("turned_2"), i)
            for g in range(4):
                for t, (a, z) in enumerate(KEY_TILES):
                    mm = pe.transpose(c.psum[0:z - a, 4 + t, g * S:(g + 1) * S], self.probs[:, g, a:z],
                                      c.identity[0:S, 0:S])
            mm.then_inc(self.s("t_units"), 1)
            pe.wait_ge(self.s("turned_01"), i + 1)
            pe.wait_ge(self.s("turned_2"), i + 1)
            if m == 0:
                pe.wait_ge(self.s("l_turned"), b * 2 + 2)
            if more:
                if m == 0:
                    pe.wait_ge(self.s("l_lo"), b + 2)
                elif m < 3:
                    pe.wait_ge(self.s("k_rotated"), (b + 1) * 2 + m)
                else:
                    pe.wait_ge(self.s("l_turned"), (b + 1) * 2 + 2)
            for t, (a, z) in enumerate(KEY_TILES):
                mm = pe.matmul(c.psum[:, 7, 0:4 * S], self.l_turned[0:z - a, q, t, :], turned[0:z - a, t, :],
                               start=t == 0, stop=t == 2)
            mm.then_inc(self.s("pv_units"), 1)

    def act(self, c, act):
        ln_act(c, act, self)

        def high(place, n, j=0):
            self.slab_landed(act, n, j)
            act.activation(self.w_hi[:, place, :], self.w_raw[:, n % 3, :], ACT.Copy).then_inc(self.s("w_hi"), 1)
        act.wait_ge(self.s("w_hi"), 2)
        high(0, 2)
        high(1, 3)
        for m in range(2):
            act.wait_ge(self.s("qc_units"), m + 1)
            act.activation(self.qc_hi[:, m, :].rearrange("p (h t) -> p h t", h=2), c.psum[:, 2 * m:2 * m + 2, 0:HALF],
                           ACT.Copy).then_inc(self.s("qc_hi"), 1)
        for x in range(3):
            high(x, self.FIRST + x)

        def step(j, q, more):
            act.wait_ge(self.s("fused_units"), j + 1)
            act.activation(self.fused_hi[:, :, :].rearrange("p x n -> p (x n)"), c.psum[:, 4, :], ACT.Copy).then_inc(
                self.s("fused_hi"), 1)
            if more:
                for x in range(3):
                    if x == 2:
                        act.wait_ge(self.s("rot_units"), j * 2 + 2)
                    high(x, self.FIRST + 3 + x, j)
            for x in range(2):
                act.wait_ge(self.s("ql_units"), j * 2 + x + 1)
                act.activation(self.q_latent_of(c, j * 2 + x).rearrange("p (h t) -> p h t", h=2),
                               c.psum[:, 4 + 2 * x:6 + 2 * x, 0:HALF], ACT.Copy).then_inc(self.s("ql_copied"), 1)
        self.steps(act, step)
        self.act_distance(c, act, 0)
        for m in range(4):
            self.act_piece(c, act, 0, 0, m)
        self.act_context(act, 1)
        self.act_distance(c, act, 1)
        act.wait_ge(self.s("qr_zero"), 2)
        act.wait_ge(self.s("q_rotated"), self.PAIRS)
        act.wait_ge(self.s("ql_copied"), self.HEADS)
        for m in range(4):
            self.act_queries(c, act, 0, m)
        self.act_exps(c, act, 0)
        batches(act, lambda b, q, more, two_more: self.act_batch(c, act, b, q, more, two_more))
        act.wait_ge(self.s("pv_units"), B * 4)
        act.wait_ge(self.s("o_copied"), B * 4)

        def split_output(j, q):
            act.wait_ge(self.s("out_w_units"), j + 1)
            act.activation(self.out_w_hi[:, q, :, :], c.psum[:, 4:6, :], ACT.Copy).then_inc(self.s("out_w_hi"), 1)
            for x in range(2):
                act.activation(self.o_hi[:, q, x, :], self.q_latent_of(c, j * 2 + x), ACT.Copy).then_inc(self.s("o_hi"), 1)

        def out(j, q, more):
            if not isinstance(j, int) or j:
                act.wait_ge(self.s("out_units"), j * 4)
            if more:
                split_output(j + 1, 1 - q)
                if isinstance(j, int) and j + 2 >= self.PAIRS:
                    return
                for x in range(3):
                    high(x, self.LAST + 6 + x, j)
        split_output(0, 0)
        for x in range(3):
            high(x, self.LAST + 3 + x)
        self.steps(act, out)

    def act_context(self, act, b):
        act.wait_ge(self.s("ctx_landed"), (b + 1) * 16)
        act.wait_ge(self.s("piece0"), b)
        act.activation(self.ctx_hi[:, :, :], self.ctx_raw[:, :, :], ACT.Copy).then_inc(self.s("ctx_hi"), 1)

    def act_piece(self, c, act, b, q, m):
        bank = c.psum[:, 7, 0:CP]
        if m == 0:
            act.wait_ge(self.s("piece0"), b + 1)
            wait(act, self.s("piece3"), b)
            act.activation(self.latent[:, :], bank, ACT.Copy).then_inc(self.s("latent"), 1)
            act.activation(self.l_hi[:, q, :], bank, ACT.Copy).then_inc(self.s("l_hi"), 1)
        if m == 2:
            act.wait_ge(self.s("k_whole"), b + 1)
            act.activation(self.kr_hi[:, q, :], self.k_rot[:, 0, :], ACT.Copy).then_inc(self.s("kr_hi"), 1)
        if m == 3:
            act.wait_ge(self.s("piece3"), b + 1)
            act.activation(self.l_turned[:, q, 0:2, :], c.psum[:, 7, 0:2 * P].rearrange("p (t l) -> p t l", t=2),
                           ACT.Copy).then_inc(self.s("l_turned"), 1)

    def queries_of(self, c, b, m):
        t, heads, pairs = tokens_of(b), slice(4 * m, 4 * m + 4), slice(2 * m, 2 * m + 2)
        even, odd = slice(4 * m, 4 * m + 4, 2), slice(4 * m + 1, 4 * m + 4, 2)
        return [(c.xn[:, :, t] if m == 0 else self.q_latent[:, 4 * m - 4:4 * m, t],
                 self.ql_hi[:, heads, :], self.ql_lo[:, heads, :]),
                (self.q_rot[0:64, pairs, t], self.qr_hi[0:64, even, :], self.qr_lo[0:64, even, :]),
                (self.q_rot[64:128, pairs, t], self.qr_hi[64:128, odd, :], self.qr_lo[64:128, odd, :])]

    def act_queries(self, c, act, b, m):
        for whole, high, _ in self.queries_of(c, b, m):
            act.activation(high, whole, ACT.Copy).then_inc(self.s("q_hi"), 1)

    def high_output(self, act, b, m):
        if isinstance(b, int) and b == B - 1 and m < 3:
            n = self.LAST + m
            self.slab_landed(act, n)
            act.activation(self.w_hi[:, m, :], self.w_raw[:, n % 3, :], ACT.Copy).then_inc(self.s("w_hi"), 1)

    def act_exps(self, c, act, i):
        act.wait_ge(self.s("shifts"), i + 1)
        for g in range(4):
            act.activation(self.probs[:, g, :], self.probs[:, g, :], ACT.Exp, bias=self.shift[:, g:g + 1],
                           scale=self.SCALE, accum_out=self.total[:, g:g + 1]).then_inc(self.s("exps"), 1)

    def act_batch(self, c, act, b, q, more, two_more):
        turned = self.turned(c)
        for m in range(4):
            i = b * 4 + m
            if more:
                self.act_piece(c, act, b + 1, 1 - q, m)
            if two_more and m == 1:
                self.act_context(act, b + 2)
                self.act_distance(c, act, b + 2)
            act.wait_ge(self.s("t_units"), i + 1)
            wait(act, self.s("pv_units"), i)
            act.activation(turned[:, 0:2, :], c.psum[:, 4:6, 0:4 * S], ACT.Copy).then_inc(self.s("turned_01"), 1)
            if more:
                act.wait_ge(self.s("s_units"), i + 1)
                self.act_queries(c, act, b + 1, m)
            act.wait_ge(self.s("pv_units"), i + 1)
            into = (c.xn if m == 0 else self.q_latent)[:, (0 if m == 0 else m * 4 - 4):(4 if m == 0 else m * 4), tokens_of(b)]
            act.wait_ge(self.s("q_split"), i + 1)
            c.apart(act)
            act.activation(into, c.psum[:, 7, 0:4 * S].rearrange("p (g s) -> p g s", g=4), ACT.Copy).then_inc(
                self.s("o_copied"), 1)
            if m < 3 or more:
                self.act_exps(c, act, i + 1)
            self.high_output(act, b, m)

    def dve(self, c, dve):
        ln_dve(c, dve, self)
        for m in range(2):
            dve.wait_ge(self.s("qc_hi"), m + 1)
            dve.tensor_tensor(self.qc_lo[:, m, :].rearrange("p (h t) -> p h t", h=2), c.psum[:, 2 * m:2 * m + 2, 0:HALF],
                              self.qc_hi[:, m, :].rearrange("p (h t) -> p h t", h=2), ALU.subtract).then_inc(
                                  self.s("qc_lo"), 1)
        for x in ("cos_q", "sin_q", "cos_k", "sin_k"):
            dve.wait_ge(self.s(x + "_landed"), 16)

        def step(j, q, more):
            dve.wait_ge(self.s("fused_hi"), j + 1)
            dve.tensor_tensor(self.fused_lo[:, :, :].rearrange("p x n -> p (x n)"), c.psum[:, 4, :],
                              self.fused_hi[:, :, :].rearrange("p x n -> p (x n)"), ALU.subtract).then_inc(
                                  self.s("fused_lo"), 1)
            for x, table in enumerate((self.cos_q, self.sin_q)):
                dve.wait_ge(self.s("rot_units"), j * 2 + x + 1)
                wait(dve, self.s("q_rotated"), j)
                for h in range(2):
                    dst = self.rotated(c, x)[:, h * HALF:(h + 1) * HALF].rearrange("p (b s) -> p b s", s=S)
                    ins = dve.tensor_tensor(dst, c.psum[:, 2 * x + h, 0:HALF].rearrange("p (b s) -> p b s", s=S),
                                            table[:, :].unsqueeze(1).broadcast_to([P, HALF // S, S]), ALU.mult)
                    if h == 0:
                        ins.then_inc(self.s("rot_first_half"), 1)
                ins.then_inc(self.s("rot_read"), 1)
            dve.wait_ge(self.s("rot_read"), j * 2 + 2)
            dve.wait_ge(self.s("rot_first_half"), j * 2 + 2)
            out = self.q_rot[:, j, :] if isinstance(j, int) else self.q_rot[:, bass.DynSlice(j, 1), :].rearrange(
                "p a t -> p (a t)")
            dve.tensor_tensor(out, self.rotated(c, 0), self.rotated(c, 1), ALU.add).then_inc(self.s("q_rotated"), 1)
        self.steps(dve, step)
        for m in range(4):
            self.dve_piece(c, dve, 0, 0, m)
            if m == 2:
                self.low_rotary_keys(dve, 0, 0)
        for m in range(4):
            self.low_latent_queries(c, dve, 0, m)
            self.low_rotary_queries(c, dve, 0, m)
        self.dve_mask(c, dve, 0, 0, 0)
        batches(dve, lambda b, q, more, two_more: self.dve_batch(c, dve, b, q, more))

        def split_output(j, q):
            dve.wait_ge(self.s("out_w_hi"), j + 1)
            dve.tensor_tensor(self.out_w_lo[:, q, :, :], c.psum[:, 4:6, :], self.out_w_hi[:, q, :, :],
                              ALU.subtract).then_inc(self.s("out_w_lo"), 1)
            for x in range(2):
                dve.wait_ge(self.s("o_hi"), j * 2 + x + 1)
                ins = dve.tensor_tensor(self.o_lo[:, q, x, :], self.q_latent_of(c, j * 2 + x), self.o_hi[:, q, x, :],
                                        ALU.subtract)
                if x == 0:
                    ins.then_inc(self.s("o_lo_first"), 1)
            ins.then_inc(self.s("o_lo"), 1)

        def out(j, q, more):
            if more:
                split_output(j + 1, 1 - q)
            for m in range(KD):
                dve.wait_ge(self.s("out_units"), j * 4 + m + 1)
                if not isinstance(j, int) or j:
                    dve.wait_ge(self.s("added"), j * 4 + m - 3)
                into = c.residual[:, m, :].rearrange("p (h t) -> p h t", h=2)
                dve.tensor_tensor(into, into, c.psum[:, 2 * (m % 2):2 * (m % 2) + 2, 0:HALF], ALU.add).then_inc(
                    self.s("added"), 1)
        split_output(0, 0)
        self.steps(dve, out)
        dve.wait_ge(self.s("added"), self.PAIRS * 4)
        dve.nop().then_inc(c.sem("residual_ready"), 1)

    def dve_piece(self, c, dve, b, q, m):
        bank = c.psum[:, 7, 0:CP]
        if m == 0:
            dve.wait_ge(self.s("l_hi"), b + 1)
            dve.wait_ge(self.s("latent"), b + 1)
            dve.tensor_tensor(self.l_lo[:, q, :], bank, self.l_hi[:, q, :], ALU.subtract).then_inc(self.s("l_lo"), 1)
        elif m < 3:
            dve.wait_ge(self.s(f"piece{m}"), b + 1)
            if m == 1:
                wait(dve, self.s("kr_lo"), b)
                wait(dve, self.s("kr_hi"), b)
            dve.tensor_tensor(self.k_rot[:, m - 1, :], bank, (self.cos_k if m == 1 else self.sin_k)[:, :],
                              ALU.mult).then_inc(self.s("k_rotated"), 1)
            if m == 2:
                dve.wait_ge(self.s("k_rotated"), b * 2 + 2)
                dve.tensor_tensor(self.k_rot[:, 0, :], self.k_rot[:, 0, :], self.k_rot[:, 1, :], ALU.add).then_inc(
                    self.s("k_whole"), 1)
        else:
            n = KEY_TILES[2][1] - KEY_TILES[2][0]
            dve.wait_ge(self.s("l_turned"), b * 2 + 1)
            dve.tensor_copy(self.l_turned[0:n, q, 2, :], c.psum[0:n, 7, 2 * P:3 * P]).then_inc(self.s("l_turned"), 1)

    def low_rotary_keys(self, dve, b, q):
        dve.wait_ge(self.s("kr_hi"), b + 1)
        dve.tensor_tensor(self.kr_lo[:, q, :], self.k_rot[:, 0, :], self.kr_hi[:, q, :], ALU.subtract).then_inc(
            self.s("kr_lo"), 1)

    def low_latent_queries(self, c, engine, b, m):
        i = b * 4 + m
        whole, high, low = self.queries_of(c, b, m)[0]
        engine.wait_ge(self.s("q_hi"), i * 3 + 1)
        c.apart(engine)
        engine.tensor_tensor(low, whole, high, ALU.subtract).then_inc(self.s("q_split"), 1)

    def low_rotary_queries(self, c, dve, b, m):
        i = b * 4 + m
        for n, (whole, high, low) in enumerate(self.queries_of(c, b, m)[1:]):
            dve.wait_ge(self.s("q_hi"), i * 3 + n + 2)
            dve.tensor_tensor(low, whole, high, ALU.subtract).then_inc(self.s("q_rot_split"), 1)

    def dve_mask(self, c, dve, b, q, m):
        i = b * 4 + m
        dve.wait_ge(self.s("s_units"), i + 1)
        if m == 0:
            dve.wait_ge(self.s("masks"), b + 1)
        wait(dve, self.s("t_units"), i)
        c.apart(dve)
        for g in range(4):
            dve.tensor_tensor_reduce(self.probs[:, g, :], c.psum[0:S, g, 0:C], self.outside[:, q, :], 1.0, -3.0e38,
                                     ALU.add, ALU.max, self.highest[:, g:g + 1]).then_inc(self.s("masked"), 1)
        dve.wait_ge(self.s("masked"), i * 4 + 4)
        dve.tensor_scalar(self.shift[:, :], self.highest[:, :], -self.SCALE, None, ALU.mult).then_inc(self.s("shifts"), 1)

    def dve_batch(self, c, dve, b, q, more):
        turned = self.turned(c)
        for m in range(4):
            i = b * 4 + m
            dve.wait_ge(self.s("exps"), i * 4 + 4)
            dve.reciprocal(self.inverse[:, :], self.total[:, :]).then_inc(self.s("inverses"), 1)
            dve.wait_ge(self.s("inverses"), i + 1)
            for g in range(4):
                dve.tensor_scalar(self.probs[:, g, :], self.probs[:, g, :], self.inverse[:, g:g + 1], None,
                                  ALU.mult).then_inc(self.s("normalised"), 1)
            if more:
                self.dve_piece(c, dve, b + 1, 1 - q, m)
            n = KEY_TILES[2][1] - KEY_TILES[2][0]
            dve.wait_ge(self.s("t_units"), i + 1)
            wait(dve, self.s("pv_units"), i)
            dve.tensor_copy(turned[0:n, 2, :], c.psum[0:n, 6, 0:4 * S]).then_inc(self.s("turned_2"), 1)
            if m < 3:
                self.dve_mask(c, dve, b, q, m + 1)
            elif more:
                self.dve_mask(c, dve, b + 1, 1 - q, 0)
            if more and m == 2:
                self.low_rotary_keys(dve, b + 1, 1 - q)
            if more:
                self.low_rotary_queries(c, dve, b + 1, m)


def program(nc, a, out, stages):
    with ExitStack() as ctx:
        c = Core(nc, ctx, stages)
        c.a = a
        c.slabs = a["slabs"]
        c.psum = ctx.enter_context(nc.psum_tensor("psum", [P, 8, 512], F32))
        c.residual = c.sb(ctx, "residual", [P, KD, T])
        c.xn = c.sb(ctx, "xn", [P, KD, T])
        c.ln_rstd = c.sb(ctx, "ln_rstd", [P, T])
        c.ln_std = c.sb(ctx, "ln_std", [P, T])
        c.eps = c.sb(ctx, "eps", [P, 1])
        c.mean_matrix = c.sb(ctx, "mean_matrix", [P, P])
        c.ones = c.sb(ctx, "ones", [P, P])
        c.identity = c.sb(ctx, "identity", [P, P])
        c.ln_squares = c.sb(ctx, "ln_squares", [P, KD, T])
        early = [st for st in stages if isinstance(st, ChosenFfn)]
        for st in early:
            st.early_buffers(c, ctx)
        with ExitStack() as shared:
            c.xn_hi = c.sb(shared, "xn_hi", [P, KD, T], F32R)
            c.xn_lo = c.sb(shared, "xn_lo", [P, KD, T], F32R)
            for st in stages:
                if not isinstance(st, (LatentAttention, BitFfn)):
                    with ExitStack() as own:
                        st.buffers(c, own)
        for st in stages:
            if isinstance(st, (LatentAttention, BitFfn)):
                with ExitStack() as own:
                    st.buffers(c, own)

        block = ctx.enter_context(nc.Block())

        @block.sync
        def _(sp):
            for k in range(KD):
                sp.dma_start(c.residual[:, k, :], a["x"][:, k, :]).then_inc(c.sem(f"x_landed{k}"), 16)
            sp.dma_start(c.identity[:, :], a["identity"]).then_inc(c.sem("identity_landed"), 16)
            for st in early:
                st.early_sync(c, sp)
            for st in stages:
                c.enter(sp, st)
                if st.index:
                    stages[st.index - 1].nearly_over(c, sp)
                st.prefetch(c, sp)
                st.sync(c, sp)
                c.clear_set(sp, st)
            sp.wait_ge(c.sem("residual_ready"), len(stages) + 1)
            sp.dma_start(out, c.residual[:, :, :]).then_inc(c.sem("out_written"), 16)
            sp.wait_ge(c.sem("out_written"), 16)

        @block.gpsimd
        def _(pool):
            for st in stages:
                c.enter(pool, st)
                st.pool(c, pool)
                c.leave(pool, "pool")

        @block.tensor
        def _(pe):
            pe.wait_ge(c.sem("constants"), 3)
            ln_mean_pe(c, pe, 0, lambda k: pe.wait_ge(c.sem(f"x_landed{k}"), 16))
            for st in stages:
                c.enter(pe, st)
                st.pe(c, pe)
                c.leave(pe, "tensor")

        @block.scalar
        def _(act):
            for st in stages:
                c.enter(act, st)
                st.act(c, act)
                c.leave(act, "scalar")

        @block.vector
        def _(dve):
            dve.memset(c.mean_matrix[:, :], 1.0 / D).then_inc(c.sem("constants"), 1)
            dve.memset(c.ones[:, :], 1.0).then_inc(c.sem("constants"), 1)
            dve.memset(c.eps[:, :], EPS_LN).then_inc(c.sem("constants"), 1)
            dve.wait_ge(c.sem("constants"), 3)
            for k in range(KD):
                dve.wait_ge(c.sem(f"x_landed{k}"), 16)
            dve.wait_ge(c.sem("identity_landed"), 16)
            dve.nop().then_inc(c.sem("residual_ready"), 1)
            for st in early:
                st.early_dve(c, dve)
            for st in stages:
                c.enter(dve, st)
                st.dve(c, dve)
                c.leave(dve, "vector")



def tiles(w, rows, cols):
    full = np.zeros((rows * P, cols * P), w.dtype)
    full[:w.shape[0], :w.shape[1]] = w
    return full.reshape(rows, P, cols, P).transpose(0, 2, 1, 3)


def slabs(blocks):
    blocks = np.stack(blocks)
    pad = -len(blocks) % 4
    if pad:
        blocks = np.concatenate([blocks, np.zeros((pad, P, P), blocks.dtype)])
    return blocks.reshape(-1, 4, P, P).transpose(0, 2, 1, 3).reshape(-1, P, 512)


def ffn_slabs(chunks):
    out = []
    for gate, up, down in chunks:
        nb = -(-gate.shape[1] // P)
        g, u, d = tiles(gate, KD, nb), tiles(up, KD, nb), tiles(down, nb, KD)
        for j in range(nb):
            out.append(slabs([g[k, j] for k in range(KD)]))
            out.append(slabs([u[k, j] for k in range(KD)]))
        out.append(slabs([d[k, m] for m in range(KD) for k in range(nb)]))
    return np.concatenate(out)


def l2f_slabs(i):
    gate_up, down = i["L2_ffn_w_gate_up"].T, i["L2_ffn_w_down"].T
    inner, w = down.shape[0], 2 * P
    return ffn_slabs([(gate_up[:, j:j + w], gate_up[:, inner + j:inner + j + w], down[j:j + w])
                      for j in range(0, inner, w)])


def feature_major(x):
    return np.ascontiguousarray(x.reshape(-1, KD, P).transpose(2, 1, 0))


def l0f_slabs(i):
    experts = [(w[:, :w.shape[1] // 2], w[:, w.shape[1] // 2:], d)
               for w, d in zip(i["L0_ffn_gate_up_w"], i["L0_ffn_down_w"])]
    return ffn_slabs(experts + [(i["L0_ffn_shared_gate_w"], i["L0_ffn_shared_up_w"], i["L0_ffn_shared_down_w"])])


def l3f_slabs(i):
    return ffn_slabs([(g.T, u.T, d.T) for g, u, d in zip(i["L3_ffn_gate_weight"], i["L3_ffn_up_weight"],
                                                         i["L3_ffn_down_weight"])])


def l0f_arrays(i):
    e = i["L0_ffn_router_w"].shape[1]
    return {"router": np.ascontiguousarray(i["L0_ffn_router_w"].reshape(KD, P, e).transpose(1, 0, 2)),
            "earlier": np.ascontiguousarray(np.broadcast_to(np.tril(np.ones((e, e), np.float32), -1), (S, e, e)))}


def l3f_arrays(i):
    def grouped(x):
        return np.ascontiguousarray(x.reshape(-1, P, x.shape[-1]).transpose(1, 0, 2))
    e = i["L3_ffn_gate_weight"].shape[0]
    return {"names": grouped(i["L3_ffn_topk_idx"]), "name_weights": grouped(i["L3_ffn_topk_weight"]),
            "expert_ids": np.ascontiguousarray(np.broadcast_to(np.arange(e, dtype=np.float32), (P, e)))}


def attention_slabs(i, layer):
    q, k, v, o = (tiles(i[f"{layer}_xattn_W{x}"].T, KD, KD) for x in "qkvo")
    columns = lambda w: [slabs([w[k, m] for k in range(KD)]) for m in range(KD)]
    return np.concatenate(columns(k) + [slabs([v[k, m] for m in range(KD)]) for k in range(KD)] + columns(q) + columns(o))


def attention_arrays(i, layer, name, more=()):
    vectors = [i[f"{layer}_xattn_{x}"].reshape(KD, P).T for x in ("bq", "bk", "bo", *more)]
    return {name + "_vectors": np.ascontiguousarray(np.stack(vectors, 1)),
            name + "_bv": np.ascontiguousarray(np.broadcast_to(i[f"{layer}_xattn_bv"], (P, D)))}


def context(i):
    x = i["ctx_2048"].reshape(B, C, KD, P).transpose(0, 3, 2, 1)
    out = np.zeros((B, P, KD, CP), x.dtype)
    out[..., :C] = x
    return out


def by_key(x):
    out = np.zeros((3 * P, B), x.dtype)
    out[:C] = x.T
    return np.ascontiguousarray(out.reshape(3, P, B).transpose(1, 0, 2))


def l1x_arrays(i):
    return {**attention_arrays(i, "L1", "l1x", ("ln_gamma", "ln_beta")), "context_mask": by_key(i["mask_BxS2_ik0"]),
            "out_scale": np.ascontiguousarray(np.broadcast_to(i["L1_xattn_residual_scale"], (P, 1)))}


def l3x_arrays(i):
    wq, wk = i["L3_xattn_Wqf"], i["L3_xattn_Wkf"]
    maps = np.zeros((P, 4 * P), wq.dtype)
    for h in range(GROUP):
        rows = slice(h * HD, (h + 1) * HD)
        maps[rows, h * 64:(h + 1) * 64] = wq.T
        maps[rows, 2 * P + h * 64:2 * P + (h + 1) * 64] = wk.T
    return {**attention_arrays(i, "L3", "l3x"), "key_mask": by_key(i["mask_BxS2_ff1"]),
            "feature_maps": maps.reshape(P, 4, P)}


def bit_arrays(i):
    return {f"bit_w{x}": np.ascontiguousarray(w.T.reshape(-1, P, w.shape[0]).transpose(1, 0, 2)).reshape(P, -1)
            for x, w in ((1, i["L1_ffn_w1"]), (2, i["L1_ffn_w2"]))}


def l0x_slabs(i):
    kvc, dq = i["L0_xattn_W_kvc"], i["L0_xattn_W_dq"]
    uq, qr, uk, kr, uv, o = (i[f"L0_xattn_W_{x}"] for x in ("uq", "qr", "uk", "kr", "uv", "o"))
    heads, rot = LatentAttention.HEADS, LatentAttention.ROT
    exchanged = np.concatenate([np.arange(rot // 2, rot), np.arange(rot // 2)])
    out = [slabs([t for t in tiles(kvc, KD, 1)[:, 0]]),
           slabs([np.concatenate([w, w], 1) for w in (kr, kr[:, exchanged])])]
    q_latent = tiles(dq, KD, 2)
    out += [slabs([q_latent[k, m] for k in range(KD)]) for m in range(2)]
    head = lambda w, h: w[:, h * P:(h + 1) * P]
    for j in range(heads // 2):
        for h in (2 * j, 2 * j + 1):
            up = tiles(head(uq, h).T, 1, 2)[0]
            out.append(slabs([up[0], up[1], head(uk, h).T]))
        pair = qr[:, 2 * j * rot:2 * (j + 1) * rot].reshape(-1, 2, rot)
        as_is, swapped = (tiles(x.reshape(-1, P), 2, 1)[:, 0] for x in (pair, pair[:, :, exchanged]))
        out.append(slabs([as_is[0], as_is[1], swapped[0], swapped[1]]))
    for j in range(heads // 2):
        out.append(slabs([head(uv, 2 * j).T, head(uv, 2 * j + 1).T]))
        out += [slabs(list(tiles(o[h * P:(h + 1) * P], 1, KD)[0])) for h in (2 * j, 2 * j + 1)]
    return np.concatenate(out)


def l0x_arrays(i):
    half = LatentAttention.ROT // 2
    inv_freq = np.float32(1.0) / np.float32(10000.0) ** (np.arange(half, dtype=np.float32) / np.float32(half))
    angle = np.arange(CP, dtype=np.float32)[None, :] * inv_freq[:, None]
    cos, sin = np.cos(angle).astype(np.float32), np.sin(angle).astype(np.float32)
    cos, sin = np.concatenate([cos] * 4), np.concatenate([-sin, sin] * 2)
    return {"cos_q": np.ascontiguousarray(cos[:, :S]), "sin_q": np.ascontiguousarray(sin[:, :S]), "cos_k": cos, "sin_k": sin,
            "ids": np.ascontiguousarray(i["itok_BxS_0_1023"].T),
            "positions": np.ascontiguousarray(np.broadcast_to(np.arange(C, dtype=np.float32), (S, C)))}



def all_stages():
    at, stages = 0, []
    for make, n in ((lambda i, at: LatentAttention("l0x", i, at), 52),
                    (lambda i, at: RoutedFfn("l0f", i, 9, 2, T, "before", at, experts=9), 54),
                    (lambda i, at: BoundedAttention("l1x", i, at), 16),
                    (lambda i, at: BitFfn("l1f", i), 0),
                    (lambda i, at: Attention("l2x", i, at), 16),
                    (lambda i, at: Ffn("l2f", i, 8, 2, T, "none", at), 48),
                    (lambda i, at: LinearAttention("l3x", i, at), 16),
                    (lambda i, at: ChosenFfn("l3f", i, 16, 3, 512, "after", at, experts=16), 144)):
        stages.append(make(len(stages), at))
        at += n
    return stages


def laid_out(i):
    weights = (l0x_slabs(i), l0f_slabs(i), attention_slabs(i, "L1"), attention_slabs(i, "L2"), l2f_slabs(i),
               attention_slabs(i, "L3"), l3f_slabs(i))
    return {"x": feature_major(i["x"]), "ctx": context(i), "identity": np.eye(P, dtype=np.float32),
            "slabs": np.concatenate(weights), **l0x_arrays(i), **l0f_arrays(i), **l1x_arrays(i), **bit_arrays(i),
            **attention_arrays(i, "L2", "l2x"), **l3x_arrays(i), **l3f_arrays(i)}


def kernel(**inputs):
    import concourse.bacc as _bacc
    from concourse.bass_utils import run_bass_kernel_spmd as _run

    inputs = {name: np.asarray(a) for name, a in inputs.items()}
    nc = _bacc.Bacc("TRN2", target_bir_lowering=False, num_devices=1)
    arrays, aps = {}, {}
    for name, a in laid_out(inputs).items():
        a = arrays[f"in_{name}_dram"] = np.ascontiguousarray(a)
        aps[name] = nc.dram_tensor(f"in_{name}_dram", a.shape, mybir.dt.from_np(a.dtype), kind="ExternalInput").ap()
    out = nc.dram_tensor("out_dram", (P, KD, T), F32, kind="ExternalOutput").ap()
    program(nc, aps, out, all_stages())
    r = _run(nc, [arrays], core_ids=[0])
    return np.ascontiguousarray(r.results[0]["out_dram"].transpose(2, 1, 0).reshape(B, S, D))
```
